# Optimizing a Trainium2 kernel written in Bass

```python
import numpy as np
import jax
import jax.numpy as jnp

def _softmax(x, axis=-1):
    return jax.nn.softmax(x, axis=axis)

def _gelu(x):
    return jax.nn.gelu(x, approximate=True)

def _silu(x):
    return jax.nn.silu(x)

def _sigmoid(x):
    return jax.nn.sigmoid(x)

def _layernorm(x, axis=-1, eps=1e-05):
    m = jnp.mean(x, axis=axis, keepdims=True)
    v = jnp.var(x, axis=axis, keepdims=True)
    return (x - m) / jnp.sqrt(v + eps)

def _scatter_add(tgt, idx, src, axis=0):
    return tgt.at[idx].add(src)

def _segment_sum(src, seg, n):
    return jax.ops.segment_sum(src, seg, n)
kernel_name = 'mk_prb_d4_jaxref_r8_5cea1b'

def setup_inputs(seed: int=0):
    np.random.seed(seed)
    _w = jnp.asarray

    def _L0_attn_setup():
        import jax, jax.numpy as jnp
        import numpy as np
        B, S, D = (8, 256, 128)
        key = jax.random.key(seed)
        k1, k2, k3, k4 = jax.random.split(key, 4)
        x = jax.random.normal(k1, (B, S, D), dtype=jnp.float32)
        W0 = jax.random.normal(k2, (D, D), dtype=jnp.float32) / jnp.sqrt(jnp.float32(D))
        Wkv = jax.random.normal(k3, (2 * D, D), dtype=jnp.float32) / jnp.sqrt(jnp.float32(D))
        bkv = jax.random.normal(k4, (2 * D,), dtype=jnp.float32) * 0.01
        eta = jnp.float32(0.1)
        return {'x': x, 'W0': W0, 'Wkv': Wkv, 'bkv': bkv, 'eta': eta}
    _L0_attn_in = _L0_attn_setup()

    def _L0_ffn_setup():
        import jax, jax.numpy as jnp
        import numpy as np
        B, S, D, O, E, R = (8, 256, 128, 128, 8, 4)
        TOP_K = 2
        SCALING = 4.0 / 4.0
        key = jax.random.key(seed)
        k0, k1, k2, k3, k4 = jax.random.split(key, 5)
        hidden_states = jax.random.normal(k0, (B, S, D), dtype=jnp.float32)
        W_lin = jax.random.normal(k1, (O, D), dtype=jnp.float32) * 0.02
        b_lin = jnp.zeros((O,), dtype=jnp.float32)
        gate_w = jax.random.normal(k2, (E, D), dtype=jnp.float32) * 0.02
        left = jax.random.normal(k3, (E, D, R), dtype=jnp.float32) * 0.02
        right = jax.random.normal(k4, (E, R, O), dtype=jnp.float32) * 0.02
        return {'hidden_states': hidden_states, 'W_lin': W_lin, 'b_lin': b_lin, 'gate_w': gate_w, 'left': left, 'right': right}
    _L0_ffn_in = _L0_ffn_setup()

    def _L1_attn_setup():
        import math
        import jax, jax.numpy as jnp
        import numpy as np
        H = 16

        def get_alibi_slopes(n):

            def pow2_slopes(n):
                start = 2 ** (-2 ** (-(math.log2(n) - 3)))
                return [start * start ** i for i in range(n)]
            if math.log2(n).is_integer():
                return pow2_slopes(n)
            c = 2 ** math.floor(math.log2(n))
            return pow2_slopes(c) + get_alibi_slopes(2 * c)[0::2][:n - c]

        def alibi_bias(num_heads, L, dtype=jnp.float32):
            slopes = jnp.asarray(get_alibi_slopes(num_heads), dtype=dtype)
            pos = jnp.arange(L)
            rel = (pos[None, :] - pos[:, None]).astype(dtype)
            bias = slopes[:, None, None] * rel[None, :, :]
            causal = pos[None, :] <= pos[:, None]
            return jnp.where(causal[None, :, :], bias, -jnp.inf)
        key = jax.random.key(seed)
        ks = jax.random.split(key, 4)
        D = 128
        B, L = (2, 256)
        s_in = 1.0 / math.sqrt(D)
        return {'x': jax.random.normal(ks[0], (B, L, D), dtype=jnp.float32), 'w_in': jax.random.normal(ks[1], (D, 3 * D), dtype=jnp.float32) * s_in, 'b_in': jnp.zeros((3 * D,), dtype=jnp.float32), 'w_out': jax.random.normal(ks[2], (D, D), dtype=jnp.float32) * s_in, 'b_out': jnp.zeros((D,), dtype=jnp.float32)}
    _L1_attn_in = _L1_attn_setup()

    def _L1_ffn_setup():
        import jax, jax.numpy as jnp
        import numpy as np
        D_MODEL = 128
        NUM_EXPERTS = 8
        HIDDEN = 512
        TOP_K = 2
        key = jax.random.key(seed)
        ks = jax.random.split(key, 6)
        x = jax.random.normal(ks[0], (2, 128, D_MODEL), dtype=jnp.float32)
        gate_w = jax.random.normal(ks[1], (NUM_EXPERTS, D_MODEL), dtype=jnp.float32) * (1.0 / np.sqrt(D_MODEL))
        w1 = jax.random.normal(ks[2], (NUM_EXPERTS, HIDDEN, D_MODEL), dtype=jnp.float32) * (1.0 / np.sqrt(D_MODEL))
        b1 = jax.random.normal(ks[3], (NUM_EXPERTS, HIDDEN), dtype=jnp.float32) * 0.01
        w2 = jax.random.normal(ks[4], (NUM_EXPERTS, D_MODEL, HIDDEN), dtype=jnp.float32) * (1.0 / np.sqrt(HIDDEN))
        b2 = jax.random.normal(ks[5], (NUM_EXPERTS, D_MODEL), dtype=jnp.float32) * 0.01
        return {'x': x, 'gate_w': gate_w, 'w1': w1, 'b1': b1, 'w2': w2, 'b2': b2}
    _L1_ffn_in = _L1_ffn_setup()

    def _L2_attn_setup():
        import jax, jax.numpy as jnp
        import numpy as np

        def _forgetting_attn(q, k, v, g):
            scale = q.shape[-1] ** (-0.5)
            scores = jnp.einsum('bqhd,bkhd->bhqk', q, k) * scale
            gc = jnp.cumsum(g, axis=1).transpose(0, 2, 1)
            scores = scores + gc[:, :, :, None] - gc[:, :, None, :]
            T = q.shape[1]
            causal = jnp.tril(jnp.ones((T, T), dtype=bool))
            scores = jnp.where(causal, scores, -jnp.inf)
            probs = jax.nn.softmax(scores.astype(jnp.float32), axis=-1).astype(q.dtype)
            return jnp.einsum('bhqk,bkhd->bqhd', probs, v)
        key = jax.random.key(seed)
        ks = jax.random.split(key, 7)
        B, T, H = (1, 256, 128)
        nh = 16
        s = 0.02
        return {'hidden_states': jax.random.normal(ks[0], (B, T, H), jnp.float32), 'Wq': jax.random.normal(ks[1], (H, H), jnp.float32) * s, 'Wk': jax.random.normal(ks[2], (H, H), jnp.float32) * s, 'Wv': jax.random.normal(ks[3], (H, H), jnp.float32) * s, 'Wf': jax.random.normal(ks[4], (nh, H), jnp.float32) * s, 'bf': jnp.zeros((nh,), jnp.float32), 'Wo': jax.random.normal(ks[5], (H, 2 * H), jnp.float32) * s}
    _L2_attn_in = _L2_attn_setup()

    def _L2_ffn_setup():
        import jax, jax.numpy as jnp
        import numpy as np
        DIM = 128
        DEPTH = 2
        HEADS = 8
        DIM_HEAD = 64
        WINDOW = 64
        INNER = HEADS * DIM_HEAD
        HID = int(DIM * 4 * 2 / 3)
        B, N = (2, 1024)
        QK_SCALE = 8.0

        def shift_token(t):
            t1, t2 = jnp.split(t, 2, axis=-1)
            t2 = jnp.pad(t2, ((0, 0), (1, 0), (0, 0)))[:, :-1]
            return jnp.concatenate([t1, t2], axis=-1)

        def l2norm(t):
            return t / jnp.clip(jnp.linalg.norm(t, axis=-1, keepdims=True), 1e-12)

        def rotate_half(x):
            x1, x2 = jnp.split(x, 2, axis=-1)
            return jnp.concatenate([-x2, x1], axis=-1)

        def rotary_xpos(q, k):
            n = q.shape[-2]
            half_idx = jnp.arange(0, DIM_HEAD, 2, dtype=jnp.float32)
            inv_freq = 1.0 / 10000.0 ** (half_idx / DIM_HEAD)
            t = jnp.arange(n, dtype=jnp.float32)
            freqs = t[:, None] * inv_freq[None, :]
            freqs = jnp.concatenate([freqs, freqs], axis=-1)
            base = (half_idx + 0.4 * DIM_HEAD) / (1.4 * DIM_HEAD)
            power = (t - n // 2) / float(WINDOW // 2)
            scale = base[None, :] ** power[:, None]
            scale = jnp.concatenate([scale, scale], axis=-1)
            cos, sin = (jnp.cos(freqs), jnp.sin(freqs))
            q = q * cos * scale + rotate_half(q) * sin * scale
            k = k * cos / scale + rotate_half(k) * sin / scale
            return (q, k)

        def local_attention(q, k, v):
            b, h, n, d = q.shape
            w = n // WINDOW
            bq = q.reshape(b, h, w, WINDOW, d) * QK_SCALE
            bk = k.reshape(b, h, w, WINDOW, d)
            bv = v.reshape(b, h, w, WINDOW, d)

            def look_around(t):
                p = jnp.pad(t, ((0, 0), (0, 0), (1, 0), (0, 0), (0, 0)))
                return jnp.concatenate([p[:, :, :w], p[:, :, 1:]], axis=3)
            bk, bv = (look_around(bk), look_around(bv))
            bt = jnp.arange(n).reshape(w, WINDOW)
            btp = jnp.pad(bt, ((1, 0), (0, 0)), constant_values=-1)
            btk = jnp.concatenate([btp[:w], btp[1:]], axis=1)
            sim = jnp.einsum('bhwid,bhwjd->bhwij', bq, bk)
            i = bt[:, :, None]
            j = btk[:, None, :]
            mask = (i < j) | (i > j + WINDOW) | (j == -1)
            sim = jnp.where(mask, -jnp.finfo(sim.dtype).max, sim)
            attn = jax.nn.softmax(sim, axis=-1)
            out = jnp.einsum('bhwij,bhwjd->bhwid', attn, bv)
            return out.reshape(b, h, n, d)

        def _layer(x, wqkv, qs, ksc, wo, lg, lb, w1, b1, w2, b2):
            b, n, _ = x.shape
            h = shift_token(x)
            qkv = h @ wqkv
            q, k, v = jnp.split(qkv, 3, axis=-1)
            to_heads = lambda t: t.reshape(b, n, HEADS, DIM_HEAD).transpose(0, 2, 1, 3)
            q, k, v = (to_heads(q), to_heads(k), to_heads(v))
            q = l2norm(q) * qs
            k = l2norm(k) * ksc
            q, k = rotary_xpos(q, k)
            o = local_attention(q, k, v)
            o = o.transpose(0, 2, 1, 3).reshape(b, n, INNER)
            x = x + o @ wo
            h = shift_token(x)
            mu = h.mean(-1, keepdims=True)
            var = h.var(-1, keepdims=True)
            h = (h - mu) / jnp.sqrt(var + 1e-05) * lg + lb
            h = h @ w1 + b1
            a, g = jnp.split(h, 2, axis=-1)
            h = a * jax.nn.gelu(g, approximate=False)
            x = x + h @ w2 + b2
            return x
        key = jax.random.key(seed)
        ks = jax.random.split(key, 6)
        return {'x': jax.random.normal(ks[0], (B, N, DIM), jnp.float32), 'wqkv': jax.random.normal(ks[1], (DEPTH, DIM, 3 * INNER), jnp.float32) * 0.02, 'q_scale': jnp.ones((DEPTH, DIM_HEAD), jnp.float32), 'k_scale': jnp.ones((DEPTH, DIM_HEAD), jnp.float32), 'wo': jax.random.normal(ks[2], (DEPTH, INNER, DIM), jnp.float32) * 0.02, 'ln_g': jnp.ones((DEPTH, DIM), jnp.float32), 'ln_b': jnp.zeros((DEPTH, DIM), jnp.float32), 'w1': jax.random.normal(ks[3], (DEPTH, DIM, 2 * HID), jnp.float32) * 0.02, 'b1': jnp.zeros((DEPTH, 2 * HID), jnp.float32), 'w2': jax.random.normal(ks[4], (DEPTH, HID, DIM), jnp.float32) * 0.02, 'b2': jnp.zeros((DEPTH, DIM), jnp.float32)}
    _L2_ffn_in = _L2_ffn_setup()

    def _L3_attn_setup():
        import jax, jax.numpy as jnp
        import numpy as np
        B, S, IN_DIM = (8, 512, 128)
        H, D = (16, 64)
        OUT_DIM = 128
        EPS = 1e-06
        HI = jax.lax.Precision.HIGHEST

        def _feature_map(t):
            return jax.nn.elu(t) + 1.0
        key = jax.random.key(seed)
        ks = jax.random.split(key, 9)
        sx = 1.0 / np.sqrt(IN_DIM)
        so = 1.0 / np.sqrt(H * D)
        return {'x': jax.random.normal(ks[0], (B, S, IN_DIM), jnp.float32), 'wq': jax.random.normal(ks[1], (IN_DIM, H, D), jnp.float32) * sx, 'bq': jnp.zeros((H, D), jnp.float32), 'wk': jax.random.normal(ks[2], (IN_DIM, H, D), jnp.float32) * sx, 'bk': jnp.zeros((H, D), jnp.float32), 'wv': jax.random.normal(ks[3], (IN_DIM, H, D), jnp.float32) * sx, 'bv': jnp.zeros((H, D), jnp.float32), 'wo': jax.random.normal(ks[4], (H, D, OUT_DIM), jnp.float32) * so, 'bo': jnp.zeros((OUT_DIM,), jnp.float32)}
    _L3_attn_in = _L3_attn_setup()

    def _L3_ffn_setup():
        import jax, jax.numpy as jnp
        import numpy as np
        B, S, H, F, E, TOPK = (4, 256, 128, 512, 8, 2)
        key = jax.random.key(seed)
        k0, k1, k2, k3, k4 = jax.random.split(key, 5)
        scale = 0.02
        return {'hidden_states': jax.random.normal(k0, (B, S, H), dtype=jnp.float32), 'router_w': jax.random.normal(k1, (E, H), dtype=jnp.float32) * scale, 'gate_w': jax.random.normal(k2, (E, F, H), dtype=jnp.float32) * scale, 'up_w': jax.random.normal(k3, (E, F, H), dtype=jnp.float32) * scale, 'down_w': jax.random.normal(k4, (E, H, F), dtype=jnp.float32) * scale}
    _L3_ffn_in = _L3_ffn_setup()
    _d = {'L0_attn_x': _L0_attn_in['x'], 'L0_attn_W0': _L0_attn_in['W0'], 'L0_attn_Wkv': _L0_attn_in['Wkv'], 'L0_attn_bkv': _L0_attn_in['bkv'], 'L0_attn_eta': _L0_attn_in['eta'], 'L0_ffn_W_lin': _L0_ffn_in['W_lin'], 'L0_ffn_b_lin': _L0_ffn_in['b_lin'], 'L0_ffn_gate_w': _L0_ffn_in['gate_w'], 'L0_ffn_left': _L0_ffn_in['left'], 'L0_ffn_right': _L0_ffn_in['right'], 'L1_attn_w_in': _L1_attn_in['w_in'], 'L1_attn_b_in': _L1_attn_in['b_in'], 'L1_attn_w_out': _L1_attn_in['w_out'], 'L1_attn_b_out': _L1_attn_in['b_out'], 'L1_ffn_gate_w': _L1_ffn_in['gate_w'], 'L1_ffn_w1': _L1_ffn_in['w1'], 'L1_ffn_b1': _L1_ffn_in['b1'], 'L1_ffn_w2': _L1_ffn_in['w2'], 'L1_ffn_b2': _L1_ffn_in['b2'], 'L2_attn_Wq': _L2_attn_in['Wq'], 'L2_attn_Wk': _L2_attn_in['Wk'], 'L2_attn_Wv': _L2_attn_in['Wv'], 'L2_attn_Wf': _L2_attn_in['Wf'], 'L2_attn_bf': _L2_attn_in['bf'], 'L2_attn_Wo': _L2_attn_in['Wo'], 'L2_ffn_wqkv': _L2_ffn_in['wqkv'], 'L2_ffn_q_scale': _L2_ffn_in['q_scale'], 'L2_ffn_k_scale': _L2_ffn_in['k_scale'], 'L2_ffn_wo': _L2_ffn_in['wo'], 'L2_ffn_ln_g': _L2_ffn_in['ln_g'], 'L2_ffn_ln_b': _L2_ffn_in['ln_b'], 'L2_ffn_w1': _L2_ffn_in['w1'], 'L2_ffn_b1': _L2_ffn_in['b1'], 'L2_ffn_w2': _L2_ffn_in['w2'], 'L2_ffn_b2': _L2_ffn_in['b2'], 'L3_attn_wq': _L3_attn_in['wq'], 'L3_attn_bq': _L3_attn_in['bq'], 'L3_attn_wk': _L3_attn_in['wk'], 'L3_attn_bk': _L3_attn_in['bk'], 'L3_attn_wv': _L3_attn_in['wv'], 'L3_attn_bv': _L3_attn_in['bv'], 'L3_attn_wo': _L3_attn_in['wo'], 'L3_attn_bo': _L3_attn_in['bo'], 'L3_ffn_router_w': _L3_ffn_in['router_w'], 'L3_ffn_gate_w': _L3_ffn_in['gate_w'], 'L3_ffn_up_w': _L3_ffn_in['up_w'], 'L3_ffn_down_w': _L3_ffn_in['down_w']}
    _x0 = _d['L0_attn_x']
    _d['L0_attn_x'] = jax.random.normal(jax.random.fold_in(jax.random.key(seed), 1), (16, 256, 128), dtype=_x0.dtype)
    del _x0
    return _d

def reference(L0_attn_x, L0_attn_W0, L0_attn_Wkv, L0_attn_bkv, L0_attn_eta, L0_ffn_W_lin, L0_ffn_b_lin, L0_ffn_gate_w, L0_ffn_left, L0_ffn_right, L1_attn_w_in, L1_attn_b_in, L1_attn_w_out, L1_attn_b_out, L1_ffn_gate_w, L1_ffn_w1, L1_ffn_b1, L1_ffn_w2, L1_ffn_b2, L2_attn_Wq, L2_attn_Wk, L2_attn_Wv, L2_attn_Wf, L2_attn_bf, L2_attn_Wo, L2_ffn_wqkv, L2_ffn_q_scale, L2_ffn_k_scale, L2_ffn_wo, L2_ffn_ln_g, L2_ffn_ln_b, L2_ffn_w1, L2_ffn_b1, L2_ffn_w2, L2_ffn_b2, L3_attn_wq, L3_attn_bq, L3_attn_wk, L3_attn_bk, L3_attn_wv, L3_attn_bv, L3_attn_wo, L3_attn_bo, L3_ffn_router_w, L3_ffn_gate_w, L3_ffn_up_w, L3_ffn_down_w):

    def _L0_attn_ref(x, W0, Wkv, bkv, eta):
        import jax, jax.numpy as jnp
        import numpy as np
        B, S, D = (8, 256, 128)
        b, s, d = x.shape
        v = jnp.einsum('bsd,ed->bse', x, Wkv[d:, :]) + bkv[d:]
        scale = 2.0 / (b * d)

        def step(W, inp):
            xt, vt = inp
            y = xt @ W.T
            err = y - vt
            gW = scale * (err.T @ xt)
            return (W - eta * gW, y)
        xs = jnp.swapaxes(x, 0, 1)
        vs = jnp.swapaxes(v, 0, 1)
        _, ys = jax.lax.scan(step, W0, (xs, vs))
        return jnp.swapaxes(ys, 0, 1)

    def _L0_ffn_ref(hidden_states, W_lin, b_lin, gate_w, left, right):
        import jax, jax.numpy as jnp
        import numpy as np
        B, S, D, O, E, R = (8, 256, 128, 128, 8, 4)
        TOP_K = 2
        SCALING = 4.0 / 4.0
        bsz, seq, d_in = hidden_states.shape
        x = hidden_states.reshape(-1, d_in)
        logits = x @ gate_w.T
        scores = jax.nn.softmax(logits, axis=-1)
        weights, idx = jax.lax.top_k(scores, TOP_K)
        base = x @ W_lin.T + b_lin
        left_sel = left[idx]
        right_sel = right[idx]
        t = jnp.einsum('nd,nkdr->nkr', x, left_sel)
        out_k = jnp.einsum('nkr,nkro->nko', t, right_sel)
        lora = jnp.sum(weights[..., None] * out_k, axis=1) * SCALING
        return (base + lora).reshape(bsz, seq, -1)

    def _L1_attn_ref(x, w_in, b_in, w_out, b_out):
        import math
        import jax, jax.numpy as jnp
        import numpy as np
        H = 16

        def get_alibi_slopes(n):

            def pow2_slopes(n):
                start = 2 ** (-2 ** (-(math.log2(n) - 3)))
                return [start * start ** i for i in range(n)]
            if math.log2(n).is_integer():
                return pow2_slopes(n)
            c = 2 ** math.floor(math.log2(n))
            return pow2_slopes(c) + get_alibi_slopes(2 * c)[0::2][:n - c]

        def alibi_bias(num_heads, L, dtype=jnp.float32):
            slopes = jnp.asarray(get_alibi_slopes(num_heads), dtype=dtype)
            pos = jnp.arange(L)
            rel = (pos[None, :] - pos[:, None]).astype(dtype)
            bias = slopes[:, None, None] * rel[None, :, :]
            causal = pos[None, :] <= pos[:, None]
            return jnp.where(causal[None, :, :], bias, -jnp.inf)
        B, L, D = x.shape
        dh = D // H
        qkv = x @ w_in + b_in
        q, k, v = jnp.split(qkv, 3, axis=-1)

        def heads(t):
            return t.reshape(B, L, H, dh).transpose(0, 2, 1, 3)
        q, k, v = (heads(q), heads(k), heads(v))
        scores = jnp.einsum('bhqd,bhkd->bhqk', q, k) / math.sqrt(dh)
        scores = scores + alibi_bias(H, L, scores.dtype)[None]
        attn = jax.nn.softmax(scores, axis=-1)
        out = jnp.einsum('bhqk,bhkd->bhqd', attn, v)
        out = out.transpose(0, 2, 1, 3).reshape(B, L, D)
        return out @ w_out + b_out

    def _L1_ffn_ref(x, gate_w, w1, b1, w2, b2):
        import jax, jax.numpy as jnp
        import numpy as np
        D_MODEL = 128
        NUM_EXPERTS = 8
        HIDDEN = 512
        TOP_K = 2
        B, S, D = x.shape
        xf = x.reshape(-1, D)
        T = xf.shape[0]
        gate_logits = xf @ gate_w.T
        gate_probs = jax.nn.softmax(gate_logits, axis=-1)
        topk_scores, topk_idx = jax.lax.top_k(gate_probs, TOP_K)
        topk_scores = topk_scores / jnp.sum(topk_scores, axis=-1, keepdims=True)
        combine = jnp.zeros((T, NUM_EXPERTS), dtype=x.dtype)
        combine = combine.at[jnp.arange(T)[:, None], topk_idx].set(topk_scores)
        h = jax.nn.relu(jnp.einsum('td,ehd->teh', xf, w1) + b1)
        expert_out = jnp.einsum('teh,edh->ted', h, w2) + b2
        out = jnp.einsum('ted,te->td', expert_out, combine)
        return out.reshape(B, S, D)

    def _L2_attn_ref(hidden_states, Wq, Wk, Wv, Wf, bf, Wo):
        import jax, jax.numpy as jnp
        import numpy as np

        def _forgetting_attn(q, k, v, g):
            scale = q.shape[-1] ** (-0.5)
            scores = jnp.einsum('bqhd,bkhd->bhqk', q, k) * scale
            gc = jnp.cumsum(g, axis=1).transpose(0, 2, 1)
            scores = scores + gc[:, :, :, None] - gc[:, :, None, :]
            T = q.shape[1]
            causal = jnp.tril(jnp.ones((T, T), dtype=bool))
            scores = jnp.where(causal, scores, -jnp.inf)
            probs = jax.nn.softmax(scores.astype(jnp.float32), axis=-1).astype(q.dtype)
            return jnp.einsum('bhqk,bkhd->bqhd', probs, v)
        B, T, H = hidden_states.shape
        nh = Wf.shape[0]
        d = H // nh
        q = (hidden_states @ Wq.T).reshape(B, T, nh, d)
        k = (hidden_states @ Wk.T).reshape(B, T, nh, d)
        v = (hidden_states @ Wv.T).reshape(B, T, nh, d)
        f = jax.nn.log_sigmoid((hidden_states @ Wf.T + bf).astype(jnp.float32))
        o_fwd = _forgetting_attn(q, k, v, f)
        flip = lambda x: jnp.flip(x, axis=1)
        o_bwd = flip(_forgetting_attn(flip(q), flip(k), flip(v), flip(f)))
        o = jnp.concatenate([o_fwd.reshape(B, T, H), o_bwd.reshape(B, T, H)], axis=-1)
        return o @ Wo.T

    def _L2_ffn_ref(x, wqkv, q_scale, k_scale, wo, ln_g, ln_b, w1, b1, w2, b2):
        import jax, jax.numpy as jnp
        import numpy as np
        DIM = 128
        DEPTH = 2
        HEADS = 8
        DIM_HEAD = 64
        WINDOW = 64
        INNER = HEADS * DIM_HEAD
        HID = int(DIM * 4 * 2 / 3)
        B, N = (2, 1024)
        QK_SCALE = 8.0

        def shift_token(t):
            t1, t2 = jnp.split(t, 2, axis=-1)
            t2 = jnp.pad(t2, ((0, 0), (1, 0), (0, 0)))[:, :-1]
            return jnp.concatenate([t1, t2], axis=-1)

        def l2norm(t):
            return t / jnp.clip(jnp.linalg.norm(t, axis=-1, keepdims=True), 1e-12)

        def rotate_half(x):
            x1, x2 = jnp.split(x, 2, axis=-1)
            return jnp.concatenate([-x2, x1], axis=-1)

        def rotary_xpos(q, k):
            n = q.shape[-2]
            half_idx = jnp.arange(0, DIM_HEAD, 2, dtype=jnp.float32)
            inv_freq = 1.0 / 10000.0 ** (half_idx / DIM_HEAD)
            t = jnp.arange(n, dtype=jnp.float32)
            freqs = t[:, None] * inv_freq[None, :]
            freqs = jnp.concatenate([freqs, freqs], axis=-1)
            base = (half_idx + 0.4 * DIM_HEAD) / (1.4 * DIM_HEAD)
            power = (t - n // 2) / float(WINDOW // 2)
            scale = base[None, :] ** power[:, None]
            scale = jnp.concatenate([scale, scale], axis=-1)
            cos, sin = (jnp.cos(freqs), jnp.sin(freqs))
            q = q * cos * scale + rotate_half(q) * sin * scale
            k = k * cos / scale + rotate_half(k) * sin / scale
            return (q, k)

        def local_attention(q, k, v):
            b, h, n, d = q.shape
            w = n // WINDOW
            bq = q.reshape(b, h, w, WINDOW, d) * QK_SCALE
            bk = k.reshape(b, h, w, WINDOW, d)
            bv = v.reshape(b, h, w, WINDOW, d)

            def look_around(t):
                p = jnp.pad(t, ((0, 0), (0, 0), (1, 0), (0, 0), (0, 0)))
                return jnp.concatenate([p[:, :, :w], p[:, :, 1:]], axis=3)
            bk, bv = (look_around(bk), look_around(bv))
            bt = jnp.arange(n).reshape(w, WINDOW)
            btp = jnp.pad(bt, ((1, 0), (0, 0)), constant_values=-1)
            btk = jnp.concatenate([btp[:w], btp[1:]], axis=1)
            sim = jnp.einsum('bhwid,bhwjd->bhwij', bq, bk)
            i = bt[:, :, None]
            j = btk[:, None, :]
            mask = (i < j) | (i > j + WINDOW) | (j == -1)
            sim = jnp.where(mask, -jnp.finfo(sim.dtype).max, sim)
            attn = jax.nn.softmax(sim, axis=-1)
            out = jnp.einsum('bhwij,bhwjd->bhwid', attn, bv)
            return out.reshape(b, h, n, d)

        def _layer(x, wqkv, qs, ksc, wo, lg, lb, w1, b1, w2, b2):
            b, n, _ = x.shape
            h = shift_token(x)
            qkv = h @ wqkv
            q, k, v = jnp.split(qkv, 3, axis=-1)
            to_heads = lambda t: t.reshape(b, n, HEADS, DIM_HEAD).transpose(0, 2, 1, 3)
            q, k, v = (to_heads(q), to_heads(k), to_heads(v))
            q = l2norm(q) * qs
            k = l2norm(k) * ksc
            q, k = rotary_xpos(q, k)
            o = local_attention(q, k, v)
            o = o.transpose(0, 2, 1, 3).reshape(b, n, INNER)
            x = x + o @ wo
            h = shift_token(x)
            mu = h.mean(-1, keepdims=True)
            var = h.var(-1, keepdims=True)
            h = (h - mu) / jnp.sqrt(var + 1e-05) * lg + lb
            h = h @ w1 + b1
            a, g = jnp.split(h, 2, axis=-1)
            h = a * jax.nn.gelu(g, approximate=False)
            x = x + h @ w2 + b2
            return x
        for l in range(DEPTH):
            x = _layer(x, wqkv[l], q_scale[l], k_scale[l], wo[l], ln_g[l], ln_b[l], w1[l], b1[l], w2[l], b2[l])
        return x

    def _L3_attn_ref(x, wq, bq, wk, bk, wv, bv, wo, bo):
        import jax, jax.numpy as jnp
        import numpy as np
        B, S, IN_DIM = (8, 512, 128)
        H, D = (16, 64)
        OUT_DIM = 128
        EPS = 1e-06
        HI = jax.lax.Precision.HIGHEST

        def _feature_map(t):
            return jax.nn.elu(t) + 1.0
        q = jnp.einsum('bsi,ihd->bshd', x, wq) + bq
        k = jnp.einsum('bsi,ihd->bshd', x, wk) + bk
        v = jnp.einsum('bsi,ihd->bshd', x, wv) + bv
        Q = _feature_map(q)
        K = _feature_map(k)
        KV = jnp.einsum('bshd,bshd->bhd', K, v, precision=HI)
        Ksum = jnp.sum(K, axis=1)
        Z = 1.0 / (Q * Ksum[:, None, :, :] + EPS)
        attn = Q * KV[:, None, :, :] * Z
        out = jnp.einsum('bshd,hdo->bso', attn, wo) + bo
        return jax.nn.gelu(out)

    def _L3_ffn_ref(hidden_states, router_w, gate_w, up_w, down_w):
        import jax, jax.numpy as jnp
        import numpy as np
        B, S, H, F, E, TOPK = (4, 256, 128, 512, 8, 2)
        b, s, h = hidden_states.shape
        x = hidden_states.reshape(-1, h)
        router_logits = x @ router_w.T
        top_vals, top_idx = jax.lax.top_k(router_logits, TOPK)
        routing_weights = jax.nn.softmax(top_vals, axis=-1)
        combine = jnp.sum(jax.nn.one_hot(top_idx, E, dtype=x.dtype) * routing_weights[..., None], axis=1)
        out = jnp.zeros_like(x)
        for e in range(E):
            g = x @ gate_w[e].T
            u = x @ up_w[e].T
            y = jax.nn.silu(g) * u @ down_w[e].T
            out = out + combine[:, e:e + 1] * y
        return out.reshape(b, s, h)
    x = L0_attn_x
    xn = _layernorm(x, axis=-1)
    x = x + _L0_attn_ref(xn, L0_attn_W0, L0_attn_Wkv, L0_attn_bkv, L0_attn_eta) + _L0_ffn_ref(xn, L0_ffn_W_lin, L0_ffn_b_lin, L0_ffn_gate_w, L0_ffn_left, L0_ffn_right)
    xn = _layernorm(x, axis=-1)
    x = x + _L1_attn_ref(xn, L1_attn_w_in, L1_attn_b_in, L1_attn_w_out, L1_attn_b_out) + _L1_ffn_ref(xn, L1_ffn_gate_w, L1_ffn_w1, L1_ffn_b1, L1_ffn_w2, L1_ffn_b2)
    xn = _layernorm(x, axis=-1)
    x = x + _L2_attn_ref(xn, L2_attn_Wq, L2_attn_Wk, L2_attn_Wv, L2_attn_Wf, L2_attn_bf, L2_attn_Wo) + _L2_ffn_ref(xn, L2_ffn_wqkv, L2_ffn_q_scale, L2_ffn_k_scale, L2_ffn_wo, L2_ffn_ln_g, L2_ffn_ln_b, L2_ffn_w1, L2_ffn_b1, L2_ffn_w2, L2_ffn_b2)
    xn = _layernorm(x, axis=-1)
    x = x + _L3_attn_ref(xn, L3_attn_wq, L3_attn_bq, L3_attn_wk, L3_attn_bk, L3_attn_wv, L3_attn_bv, L3_attn_wo, L3_attn_bo) + _L3_ffn_ref(xn, L3_ffn_router_w, L3_ffn_gate_w, L3_ffn_up_w, L3_ffn_down_w)
    return x

_drawn_inputs = setup_inputs


def setup_inputs(seed=0):
    import zlib

    import numpy as np

    out = dict(_drawn_inputs(seed))
    spreads = {'L0_ffn_b_lin': (0.0, 0.1),
     'L1_attn_b_in': (0.0, 0.1),
     'L1_attn_b_out': (0.0, 0.1),
     'L2_attn_bf': (0.0, 2.0),
     'L2_ffn_q_scale': (1.0, 0.6),
     'L2_ffn_k_scale': (1.0, 0.6),
     'L2_ffn_ln_g': (1.0, 0.6),
     'L2_ffn_ln_b': (0.0, 0.8),
     'L2_ffn_b1': (0.0, 0.8),
     'L2_ffn_b2': (0.0, 0.713),
     'L3_attn_bq': (0.0, 2.0),
     'L3_attn_bk': (0.0, 2.0),
     'L3_attn_bv': (0.0, 2.0),
     'L3_attn_bo': (0.0, 2.0)}
    factors = {'L0_attn_bkv': 29.215,
     'L0_ffn_gate_w': 5.937,
     'L0_ffn_left': 6.737,
     'L0_ffn_right': 6.382,
     'L1_ffn_b1': 8.0,
     'L1_ffn_b2': 8.0,
     'L2_attn_Wq': 8.0,
     'L2_attn_Wk': 8.0,
     'L2_attn_Wv': 3.437,
     'L2_attn_Wf': 40.967,
     'L2_attn_Wo': 3.384,
     'L2_ffn_wqkv': 3.513,
     'L2_ffn_wo': 3.504,
     'L2_ffn_w1': 8.0,
     'L2_ffn_w2': 8.0,
     'L3_attn_wq': 64.0,
     'L3_attn_wk': 25.448,
     'L3_ffn_router_w': 8.0,
     'L3_ffn_gate_w': 8.0,
     'L3_ffn_up_w': 8.0,
     'L3_ffn_down_w': 8.0,
     'L3_attn_wv': 5.905,
     'L3_attn_wo': 5.75}
    for name, (base, spread) in spreads.items():
        noise = np.random.default_rng([zlib.crc32(name.encode()), seed]).standard_normal(out[name].shape)
        drawn = base * np.exp(spread * noise) if base else spread * noise
        out[name] = jnp.asarray(drawn.astype(out[name].dtype))
    for name, factor in factors.items():
        out[name] = (out[name] * factor).astype(out[name].dtype)
    return out
```

```python
import math
from contextlib import ExitStack

import numpy as np
import concourse.bass as bass
from concourse import mybir

FP32 = mybir.dt.float32
BF16 = mybir.dt.bfloat16
U32 = mybir.dt.uint32
ALU = mybir.AluOpType
ACT = mybir.ActivationFunctionType
AX = mybir.AxisListType

PHASES = (0, 1, 2, 3)

P = 128
D = 128
S = 256
NC = S // P
NH = 16
DH = D // NH
SLOT = 32
GH = P // SLOT
NG = NH // GH
E = 8
HID = 512
HC = HID // P
LN_EPS = 1e-5
AW = 3 * P
NEG = -1e30


class Chain:

    def __init__(self, eng, sem, rnd, n_per):
        self.eng, self.sem, self.rnd, self.n_per, self.n = eng, sem, rnd, n_per, 0

    def mark(self, ins):
        ins.then_inc(self.sem, 1)
        self.n += 1
        return self.n

    def wait(self, n):
        self.eng.wait_ge(self.sem, self.rnd * self.n_per + n)

    def hold(self, n, pad):
        self.wait(n)
        self.eng.memset(pad, 0.0)

    def __call__(self, ins):
        self.wait(self.mark(ins))

    def done(self):
        assert self.n == self.n_per, f"chain: {self.n} steps, declared {self.n_per}"


def pool_hold(pool, g, pad):
    pool.tensor_tensor(pad, g.neg_half[0:1, 0:1], g.neg_half[0:1, 0:1], ALU.mult)


class Banks:

    def __init__(self, banks, full, taken, uses):
        self.b, self.full, self.taken = banks, full, taken
        self.n, self.per = len(banks), uses // len(banks)
        assert uses % len(banks) == 0

    def open(self, pe):
        for t in self.taken:
            pe.sem_inc(t, 1)

    def fill(self, pe, rnd, k):
        pe.wait_ge(self.taken[k % self.n], rnd * self.per + k // self.n + 1)
        return self.b[k % self.n]

    def filled(self, ins, k):
        ins.then_inc(self.full[k % self.n], 1)

    def read(self, eng, rnd, k):
        eng.wait_ge(self.full[k % self.n], rnd * self.per + k // self.n + 1)
        return self.b[k % self.n]

    def took(self, ins, k):
        ins.then_inc(self.taken[k % self.n], 1)

    def wait_taken(self, eng, rnd, k):
        eng.wait_ge(self.taken[k % self.n], rnd * self.per + k // self.n + 2)


class Names:
    pass


def chunks(ap, n=NC):
    return ap.rearrange("p (c d) -> p c d", c=n)


def over_chunks(row, n=NC):
    return row.unsqueeze(1).to_broadcast([P, n, row.shape[-1]])


def stat_buffers(sb, n):
    t = Names()
    t.stats = sb("stats", [P, n, 6])
    t.mv = sb("mean_var", [P, n, 2])
    t.pad = sb("norm_pad", [1, 1])
    t.var = sb("var", [P, n])
    t.rstd = sb("rstd", [P, n])
    return t


def norm_stats(dve, chain, x, t, n):
    for c in range(n):
        m = chain.mark(dve.bn_stats(t.stats[:, c, :], x[:, c, :]))
    chain.hold(m, t.pad[:, :])
    for c in range(n):
        m = chain.mark(dve.bn_aggr(t.mv[:, c, :], t.stats[:, c, :]))
    chain.wait(m)
    return dve.tensor_scalar(t.var[:, :], t.mv[:, :, 1], LN_EPS, None, ALU.add)


def norm_rstd(pool, g, t, n):
    return pool.tensor_tensor(t.rstd[:, :], t.var[:, :], g.neg_half[:, 0:n], ALU.pow)


def norm_apply(dve, x, xn, t, n):
    for c in range(n):
        last = dve.tensor_scalar(xn[:, c, :], x[:, c, :], t.mv[:, c, 0:1], t.rstd[:, c:c + 1],
                                 ALU.subtract, ALU.mult)
    return last


def router_buffers(sb, n):
    r = Names()
    r.pad = sb("r_pad", [1, 1])
    r.lg = sb("r_logits", [P, n, E])
    r.mx = sb("r_best", [P, n, 8])
    r.ix = sb("r_index", [P, n, 8], U32)
    r.ixf = sb("r_indexf", [P, n, 2])
    r.ls = sb("r_shifted", [P, n, E])
    r.ex = sb("r_exp", [P, n, E])
    r.mk = sb("r_first", [P, n, E])
    r.mk2 = sb("r_chosen", [P, n, E])
    r.cu = sb("r_kept", [P, n, E])
    r.den = sb("r_sum", [P, n])
    r.rden = sb("r_rsum", [P, n])
    r.comb = sb("r_comb", [P, n, E])
    return r


def router_rank(dve, chain, r, logits, n):
    chain.hold(chain.mark(dve.tensor_copy(r.lg[:, :, :], logits)), r.pad[:, :])
    for c in range(n):
        m = chain.mark(dve.max(r.mx[:, c, :], r.lg[:, c, :]))
    chain.hold(m, r.pad[:, :])
    for c in range(n):
        m = chain.mark(dve.max_index(r.ix[:, c, :], r.mx[:, c, :], r.lg[:, c, :]))
    chain.wait(m)
    chain(dve.tensor_copy(r.ixf[:, :, :], r.ix[:, :, 0:2]))
    return dve.tensor_tensor(r.ls[:, :, :], r.lg[:, :, :], r.mx[:, :, 0:1].to_broadcast([P, n, E]), ALU.subtract)


def router_mix(dve, chain, r, iota, n, over_all, scale=1.0):
    for c in range(n):
        m = chain.mark(dve.tensor_scalar(r.mk[:, c, :], iota[:, 0:E], r.ixf[:, c, 0:1], None, ALU.is_equal))
    chain.wait(m)
    for c in range(n):
        m = chain.mark(dve.scalar_tensor_tensor(out=r.mk2[:, c, :], in0=iota[:, 0:E], scalar=r.ixf[:, c, 1:2],
                                                in1=r.mk[:, c, :], op0=ALU.is_equal, op1=ALU.add))
    chain.wait(m)
    chain(dve.tensor_tensor(r.cu[:, :, :], r.mk2[:, :, :], r.ex[:, :, :], ALU.mult))
    chain(dve.reduce_sum(r.den[:, :], (r.ex if over_all else r.cu)[:, :, :], AX.X))
    chain(dve.reciprocal(r.rden[:, :], r.den[:, :]))
    return dve.scalar_tensor_tensor(out=r.comb[:, :, :], in0=r.cu[:, :, :], scalar=scale,
                                    in1=r.rden[:, :].unsqueeze(2).to_broadcast([P, n, E]),
                                    op0=ALU.mult, op1=ALU.mult)


ROUTER_STEPS = lambda n: (1 + 2 * n + 1) + (2 * n + 3)
NORM_STEPS = lambda n: 2 * n

FORWARD = dict(split=P, parts=((0, 0, 1), (1, 0, 2)))
BACKWARD = dict(split=2 * P, parts=((0, 0, 2), (1, 1, 1)))


def pe_scores(pe, g, bank, q, k, mask, way):
    pe.matmul(bank[:, 0:AW], g.ident16[:, :], mask[:, :], start=True, stop=False, skip_group_check=True)
    at = 0
    for c, k0, n in way["parts"]:
        last = pe.matmul(bank[:, at:at + n * P], q[:, c * P:(c + 1) * P], k[:, k0 * P:(k0 + n) * P],
                         start=False, stop=(c == 1), skip_group_check=True)
        at += n * P
    return last


def pe_transpose3(pe, g, bank, probs):
    for j in range(3):
        last = pe.transpose(bank[:, j * P:(j + 1) * P], probs[:, j * P:(j + 1) * P], g.ident[:, :])
    return last


def pe_values(pe, outs, probsT, v, way):
    j = 0
    for c, k0, n in way["parts"]:
        for i in range(n):
            last = pe.matmul(outs[c], probsT[:, j * P:(j + 1) * P], v[:, k0 + i, :],
                             start=(i == 0), stop=(i == n - 1))
            j += 1
    return last


def dve_negmax(dve, bank, negmax, way):
    s = way["split"]
    dve.tensor_reduce(negmax[:, 0:1], bank[:, 0:s], AX.X, ALU.max, negate=True)
    return dve.tensor_reduce(negmax[:, 1:2], bank[:, s:AW], AX.X, ALU.max, negate=True)


def act_probs(act, bank, negmax, probs, sums, way):
    s = way["split"]
    act.activation(probs[:, 0:s], bank[:, 0:s], ACT.Exp, bias=negmax[:, 0:1], accum_out=sums[0])
    return act.activation(probs[:, s:AW], bank[:, s:AW], ACT.Exp, bias=negmax[:, 1:2], accum_out=sums[1])


TS = 8
RC = 4
LR = 4


def layer0(nc, g, B, x_in, scratch):
    assert B * TS == P
    w = g.w
    rounds = S // TS // RC
    with ExitStack() as ctx:
        def sb(name, shape, dt=FP32):
            return ctx.enter_context(nc.sbuf_tensor("l0_" + name, shape, dt))

        def sem(name):
            return ctx.enter_context(nc.semaphore("l0_" + name))

        x0 = g.x_all
        xs = sb("xs", [P, RC, D])
        xn = sb("xn", [P, RC, D])
        xnT = sb("xnT", [P, RC, P])
        st = stat_buffers(sb, RC)
        r = router_buffers(sb, RC)
        neg_c = sb("neg_c", [P, 1])
        before = sb("before", [P, P])
        after = sb("after", [P, P])
        N1, N1T, N2, N2T, N4 = (sb(n, [P, RC, P]) for n in ("n1", "n1t", "n2", "n2t", "n4"))
        S1, S2, AT = (sb(n, [P, RC, P]) for n in ("s1", "s2", "at"))
        w_sum = sb("w_sum", [P, D])
        b_sum = sb("b_sum", [P, D])
        U = sb("U", [P, D])
        low = sb("low", [P, RC, E * LR])
        lowT = sb("lowT", [E * LR, RC, P])
        rest = sb("rest", [P, RC, D])
        rs = sb("rs", [P, 2, D])
        err = sb("err", [P, 2, D])
        y = sb("y", [P, RC, D])

        A_XNT, A_GRAM, A_LOGIT, A_LOWT, A_REST, A_N2, A_N2T, A_N4, A_S2, A_AT = range(10)
        G = Banks(g.bank[0:5], [sem(f"g_full{i}") for i in range(5)], [sem(f"g_taken{i}") for i in range(5)], 10)
        bank_r, bank_e, bank_u = g.bank[5:8]

        x_loaded = sem("x_loaded")
        setup_done = sem("setup_done")
        var_ready = sem("var_ready")
        rstd_ready = sem("rstd_ready")
        xn_ready = sem("xn_ready")
        gate_exp = sem("gate_exp")
        low_ready = sem("low_ready")
        s1_ready = sem("s1_ready")
        r_full = sem("r_full")
        rs_ready = sem("rs_ready")
        e_full = sem("e_full")
        err_ready = sem("err_ready")
        u_full = sem("u_full")
        u_ready = sem("u_ready")
        y_ready = sem("y_ready")
        stored = sem("stored")
        dve_chain = sem("dve_chain")
        n_chain = 1 + NORM_STEPS(RC) + ROUTER_STEPS(RC) + 1 + 2 + RC

        block = ctx.enter_context(nc.Block())

        @block.sync
        def _(sp):
            for b in range(B):
                sp.dma_start(x0[b * TS:(b + 1) * TS, :, :],
                             x_in[b].rearrange("(c t) d -> t c d", t=TS)).then_inc(x_loaded, 16)
            g.issue_loads(sp)
            sp.sem_inc(stored, 16 * B)
            with sp.Fori(0, rounds) as rd:
                sp.wait_ge(y_ready, rd + 1)
                for b in range(B):
                    sp.dma_start(scratch[b, bass.ds(rd * (RC * TS), RC * TS), :].rearrange("(c t) d -> t c d", t=TS),
                                 y[b * TS:(b + 1) * TS, :, :]).then_inc(stored, 16)
            sp.wait_ge(stored, 16 * B * (rounds + 1))

        @block.tensor
        def _(pe):
            g.wait_consts(pe)
            pe.wait_ge(setup_done, 1)
            G.open(pe)
            with pe.Fori(0, rounds) as rd:
                def each(k, lhs, rhs, width=P):
                    b = G.fill(pe, rd, k)
                    for j in range(RC):
                        last = pe.matmul(b[:, j * width:(j + 1) * width], lhs(j), rhs(j), start=True, stop=True)
                    G.filled(last, k)

                pe.wait_ge(xn_ready, rd + 1)
                b = G.fill(pe, rd, A_XNT)
                for j in range(RC):
                    last = pe.transpose(b[:, j * P:(j + 1) * P], xn[:, j, :], g.ident[:, :])
                G.filled(last, A_XNT)
                G.wait_taken(pe, rd, A_XNT)
                each(A_GRAM, lambda j: xnT[:, j, :], lambda j: xnT[:, j, :])
                b = G.fill(pe, rd, A_LOGIT)
                for j in range(RC):
                    pe.matmul(b[:, j * E:(j + 1) * E], xnT[:, j, :], w["gate0"][:, :], start=True, stop=True)
                    last = pe.matmul(b[:, RC * E + j * E * LR:RC * E + (j + 1) * E * LR], xnT[:, j, :],
                                     w["left0"][:, :], start=True, stop=True)
                G.filled(last, A_LOGIT)
                pe.wait_ge(low_ready, rd + 1)
                b = G.fill(pe, rd, A_LOWT)
                for j in range(RC):
                    last = pe.transpose(b[0:E * LR, j * P:(j + 1) * P], low[:, j, :], g.ident[:, :])
                G.filled(last, A_LOWT)
                G.wait_taken(pe, rd, A_LOWT)
                b = G.fill(pe, rd, A_REST)
                for j in range(RC):
                    pe.matmul(b[:, j * P:(j + 1) * P], xnT[:, j, :], w_sum[:, :], start=True, stop=False)
                    last = pe.matmul(b[:, j * P:(j + 1) * P], lowT[:, j, :], w["right0"][:, :], start=False, stop=True)
                G.filled(last, A_REST)
                G.wait_taken(pe, rd, A_GRAM)
                each(A_N2, lambda j: N1T[:, j, :], lambda j: N1[:, j, :])
                each(A_N2T, lambda j: N1[:, j, :], lambda j: N1T[:, j, :])
                G.wait_taken(pe, rd, A_N2)
                G.wait_taken(pe, rd, A_N2T)
                each(A_N4, lambda j: N2T[:, j, :], lambda j: N2[:, j, :])
                pe.wait_ge(s1_ready, rd + 1)
                each(A_S2, lambda j: N2[:, j, :], lambda j: S1[:, j, :])
                G.wait_taken(pe, rd, A_N4)
                G.wait_taken(pe, rd, A_S2)
                each(A_AT, lambda j: N4[:, j, :], lambda j: S2[:, j, :])
                G.wait_taken(pe, rd, A_AT)
                for j in range(RC):
                    pe.wait_ge(u_ready, rd * RC + j + 1)
                    pe.matmul(bank_r[:, 0:D], xnT[:, j, :], U[:, :], start=True, stop=True).then_inc(r_full, 1)
                    pe.wait_ge(rs_ready, rd * RC + j + 1)
                    pe.matmul(bank_e[:, 0:D], AT[:, j, :], rs[:, j % 2, :], start=True, stop=True).then_inc(e_full, 1)
                    pe.wait_ge(err_ready, rd * RC + j + 1)
                    pe.matmul(bank_u[:, 0:D], xn[:, j, :], err[:, j % 2, :], start=True, stop=True).then_inc(u_full, 1)

        @block.gpsimd
        def _(pool):
            g.wait_layer(pool, 0)
            with pool.Fori(0, rounds) as rd:
                pool.wait_ge(var_ready, rd + 1)
                norm_rstd(pool, g, st, RC).then_inc(rstd_ready, 1)

        @block.scalar
        def _(act):
            with act.Fori(0, rounds) as rd:
                G.wait_taken(act, rd, A_LOGIT)
                act.activation(r.ex[:, :, :], r.ls[:, :, :], ACT.Exp).then_inc(gate_exp, 1)
                b = G.read(act, rd, A_N2T)
                G.took(act.activation(N2T[:, :, :], chunks(b[:, :], RC), ACT.Copy), A_N2T)
                b = G.read(act, rd, A_N4)
                G.took(act.activation(N4[:, :, :], chunks(b[:, :], RC), ACT.Copy), A_N4)

        @block.vector
        def _(dve):
            g.wait_consts(dve)
            dve.tensor_scalar(neg_c[:, :], w["eta0"][:, :], -2.0 / (B * D), None, ALU.mult).then_inc(setup_done, 1)
            dve.wait_ge(setup_done, 1)
            dve.tensor_scalar(before[:, :], w["before0"][:, :], neg_c[:, 0:1], None, ALU.mult)
            dve.tensor_scalar(after[:, :], w["after0"][:, :], neg_c[:, 0:1], None, ALU.mult)
            dve.tensor_tensor(w_sum[:, :], w["wv0"][:, :], w["lin0"][:, :], ALU.add)
            dve.tensor_tensor(b_sum[:, :], w["bv0"][:, :], w["blin0"][:, :], ALU.add)
            dve.tensor_tensor(U[:, :], w["start0"][:, :], w["wv0"][:, :], ALU.subtract).then_inc(u_ready, 1)
            dve.wait_ge(u_ready, 1)
            dve.wait_ge(x_loaded, 16 * B)
            with dve.Fori(0, rounds) as rd:
                ch = Chain(dve, dve_chain, rd, n_chain)
                ch(dve.tensor_copy(xs[:, :, :], x0[:, bass.ds(rd * RC, RC), :]))
                norm_stats(dve, ch, xs, st, RC).then_inc(var_ready, 1)
                dve.wait_ge(rstd_ready, rd + 1)
                norm_apply(dve, xs, xn, st, RC).then_inc(xn_ready, 1)
                b = G.read(dve, rd, A_XNT)
                G.took(dve.tensor_copy(xnT[:, :, :], chunks(b[:, :], RC)), A_XNT)
                b = G.read(dve, rd, A_GRAM)
                dve.tensor_tensor(N1T[:, :, :], chunks(b[:, :], RC), over_chunks(after[:, :], RC), ALU.mult)
                G.took(dve.tensor_tensor(N1[:, :, :], chunks(b[:, :], RC), over_chunks(before[:, :], RC), ALU.mult), A_GRAM)
                b = G.read(dve, rd, A_LOGIT)
                ch(router_rank(dve, ch, r, b[:, 0:RC * E].rearrange("p (c e) -> p c e", e=E), RC))
                G.took(dve.tensor_copy(low[:, :, :], b[:, RC * E:RC * E * (1 + LR)].rearrange("p (c k) -> p c k", c=RC)),
                       A_LOGIT)
                G.wait_taken(dve, rd, A_GRAM)
                dve.tensor_tensor(S1[:, :, :], N1T[:, :, :], over_chunks(g.ident[:, :], RC), ALU.add).then_inc(s1_ready, 1)
                dve.wait_ge(gate_exp, rd + 1)
                ch(router_mix(dve, ch, r, g.iota, RC, True))
                dve.tensor_tensor(low[:, :, :].rearrange("p c (e k) -> p (c e) k", k=LR),
                                  low[:, :, :].rearrange("p c (e k) -> p (c e) k", k=LR),
                                  r.comb[:, :, :].rearrange("p c e -> p (c e)").unsqueeze(2).to_broadcast([P, RC * E, LR]),
                                  ALU.mult).then_inc(low_ready, 1)
                b = G.read(dve, rd, A_LOWT)
                G.took(dve.tensor_copy(lowT[:, :, :], chunks(b[0:E * LR, :], RC)), A_LOWT)
                b = G.read(dve, rd, A_N2)
                G.took(dve.tensor_copy(N2[:, :, :], chunks(b[:, :], RC)), A_N2)
                b = G.read(dve, rd, A_REST)
                G.took(dve.tensor_tensor(rest[:, :, :], chunks(b[:, :], RC), over_chunks(b_sum[:, :], RC), ALU.add), A_REST)
                b = G.read(dve, rd, A_S2)
                G.took(dve.tensor_tensor(S2[:, :, :], chunks(b[:, :], RC), S1[:, :, :], ALU.add), A_S2)
                G.wait_taken(dve, rd, A_S2)
                ch(dve.tensor_tensor(rest[:, :, :], rest[:, :, :], xs[:, :, :], ALU.add))
                b = G.read(dve, rd, A_AT)
                G.took(dve.tensor_tensor(AT[:, :, :], chunks(b[:, :], RC), S2[:, :, :], ALU.add), A_AT)
                for j in range(RC):
                    dve.wait_ge(r_full, rd * RC + j + 1)
                    dve.tensor_tensor(rs[:, j % 2, :], bank_r[:, 0:D], w["bv0"][:, :], ALU.subtract).then_inc(rs_ready, 1)
                    dve.wait_ge(e_full, rd * RC + j + 1)
                    dve.tensor_copy(err[:, j % 2, :], bank_e[:, 0:D]).then_inc(err_ready, 1)
                    if j == 0:
                        dve.wait_ge(stored, (rd + 1) * (16 * B))
                    dve.wait_ge(err_ready, rd * RC + j + 1)
                    ch.mark(dve.tensor_tensor(y[:, j, :], rest[:, j, :], err[:, j % 2, :], ALU.add))
                    dve.wait_ge(u_full, rd * RC + j + 1)
                    dve.wait_ge(u_ready, rd * RC + j + 1)
                    dve.scalar_tensor_tensor(out=U[:, :], in0=bank_u[:, 0:D], scalar=neg_c[:, 0:1], in1=U[:, :],
                                             op0=ALU.mult, op1=ALU.add).then_inc(u_ready, 1)
                ch.wait(ch.n)
                dve.memset(st.pad[:, :], 0.0).then_inc(y_ready, 1)
                ch.done()


def layer1(nc, g, B):
    w = g.w
    with ExitStack() as ctx:
        def sb(name, shape, dt=FP32):
            return ctx.enter_context(nc.sbuf_tensor("l1_" + name, shape, dt))

        def sem(name):
            return ctx.enter_context(nc.semaphore("l1_" + name))

        xt = sb("xt", [P, NC, D])
        xn = sb("xn", [P, NC, D])
        xnT = sb("xnT", [P, S])
        st = stat_buffers(sb, NC)
        qT = sb("qT", [P, NG, S])
        kT = sb("kT", [P, NG, S])
        v = sb("v", [P, NC, D])
        negmax = sb("negmax", [P, 2, NC])
        probs = sb("probs", [P, 2, AW])
        probsT = sb("probsT", [P, 2, AW])
        rowsum = sb("rowsum", [P, NC, NH])
        rrow = sb("rrow", [P, NC, NH])
        on = sb("on", [P, NC, D])
        oT = sb("oT", [P, S])
        hT = sb("hT", [P, 2, HC, S])
        combT = sb("combT", [E, S])
        qbias = sb("qbias", [P, NG])
        kconst = sb("kconst", [P, NG, S])
        r = router_buffers(sb, NC)

        Sb, Tb, Ob, Db = g.bank[0:2], g.bank[2:4], g.bank[6], g.bank[7]
        G_XNT, G_LOGIT, G_Q, G_K, G_V, G_UP = 0, 1, 2, 4, 6, 7
        G_COMBT = G_UP + 2 * E
        G_OT, G_OUT = G_COMBT + 1, G_COMBT + 2
        G = Banks(g.bank[4:6], [sem("g_full0"), sem("g_full1")], [sem("g_taken0"), sem("g_taken1")], G_OUT + 1)

        setup_done = sem("setup_done")
        var_ready = sem("var_ready")
        rstd_ready = sem("rstd_ready")
        xn_ready = sem("xn_ready")
        gate_exp = sem("gate_exp")
        comb_ready = sem("comb_ready")
        scores_ready = sem("scores_ready")
        negmax_ready = sem("negmax_ready")
        probs_ready = sem("probs_ready")
        transposed = sem("transposed")
        probsT_ready = sem("probsT_ready")
        heads_summed = sem("heads_summed")
        on_ready = sem("on_ready")
        down_ready = sem("down_ready")
        down_used = sem("down_used")
        dve_chain = sem("dve_chain")
        n_chain = 1 + NORM_STEPS(NC) + ROUTER_STEPS(NC) + 2

        block = ctx.enter_context(nc.Block())

        @block.tensor
        def _(pe):
            g.wait_consts(pe)
            g.wait_layer(pe, 1)
            G.open(pe)
            pe.sem_inc(down_used, 1)
            with pe.Fori(0, B) as it:
                pe.wait_ge(xn_ready, it + 1)
                b = G.fill(pe, it, G_XNT)
                for c in range(NC):
                    last = pe.transpose(b[:, c * P:(c + 1) * P], xn[:, c, :], g.ident[:, :])
                G.filled(last, G_XNT)
                G.wait_taken(pe, it, G_XNT)
                b = G.fill(pe, it, G_LOGIT)
                for c in range(NC):
                    last = pe.matmul(b[:, c * E:(c + 1) * E], xnT[:, c * P:(c + 1) * P], w["gate1"][:, :],
                                     start=True, stop=True)
                G.filled(last, G_LOGIT)
                for k0, wt in ((G_Q, w["q1"]), (G_K, w["k1"])):
                    for u in range(2):
                        b = G.fill(pe, it, k0 + u)
                        for j in range(2):
                            gg = 2 * u + j
                            last = pe.matmul(b[:, j * S:(j + 1) * S], wt[:, gg * P:(gg + 1) * P], xnT[:, :],
                                             start=True, stop=True)
                        G.filled(last, k0 + u)
                b = G.fill(pe, it, G_V)
                for c in range(NC):
                    last = pe.matmul(b[:, c * P:(c + 1) * P], xnT[:, c * P:(c + 1) * P], w["v1"][:, :],
                                     start=True, stop=True)
                G.filled(last, G_V)
                G.wait_taken(pe, it, G_V - 1)
                G.wait_taken(pe, it, G_V)
                for s in range(NH + 2):
                    e = s // 2
                    if s < NH:
                        rows, gg = slice(SLOT * (s % GH), SLOT * (s % GH + 1)), s // GH
                        pe_scores(pe, g, Sb[s % 2], qT[rows, gg, :], kT[rows, gg, :], g.mask_causal,
                                  FORWARD).then_inc(scores_ready, 1)
                        if s % 2 == 0:
                            for u in range(2):
                                k = G_UP + 2 * e + u
                                b = G.fill(pe, it, k)
                                for j in range(2):
                                    h = (e * HC + 2 * u + j) * P
                                    last = pe.matmul(b[:, j * S:(j + 1) * S], w["up1"][:, h:h + P], xnT[:, :],
                                                     start=True, stop=True)
                                G.filled(last, k)
                        else:
                            G.wait_taken(pe, it, G_UP + 2 * e)
                            G.wait_taken(pe, it, G_UP + 2 * e + 1)
                            pe.wait_ge(down_used, it * E + e + 1)
                            for c in range(NC):
                                for j in range(HC):
                                    last = pe.matmul(Db[:, c * P:(c + 1) * P], hT[:, e % 2, j, c * P:(c + 1) * P],
                                                     w["down1"][:, e * HC + j, :], start=(j == 0), stop=(j == HC - 1))
                            last.then_inc(down_ready, 1)
                    if s >= 2:
                        h = s - 2
                        pe.wait_ge(probsT_ready, it * NH + h + 1)
                        last = pe_values(pe, [Ob[:, c * D + h * DH:c * D + (h + 1) * DH] for c in range(NC)],
                                         probsT[:, h % 2, :], v[:, :, h * DH:(h + 1) * DH], FORWARD)
                        if h == NH - 1:
                            last.then_inc(heads_summed, 1)
                    if 1 <= s <= NH:
                        h = s - 1
                        pe.wait_ge(probs_ready, it * NH + h + 1)
                        pe_transpose3(pe, g, Tb[h % 2], probs[:, h % 2, :]).then_inc(transposed, 1)
                pe.wait_ge(comb_ready, it + 1)
                b = G.fill(pe, it, G_COMBT)
                for c in range(NC):
                    last = pe.transpose(b[0:E, c * P:(c + 1) * P], r.comb[:, c, :], g.ident[:, :])
                G.filled(last, G_COMBT)
                pe.wait_ge(on_ready, it + 1)
                b = G.fill(pe, it, G_OT)
                for c in range(NC):
                    last = pe.transpose(b[:, c * P:(c + 1) * P], on[:, c, :], g.ident[:, :])
                G.filled(last, G_OT)
                G.wait_taken(pe, it, G_COMBT)
                G.wait_taken(pe, it, G_OT)
                b = G.fill(pe, it, G_OUT)
                for c in range(NC):
                    pe.matmul(b[:, c * P:(c + 1) * P], oT[:, c * P:(c + 1) * P], w["out1"][:, :], start=True, stop=False)
                    last = pe.matmul(b[:, c * P:(c + 1) * P], combT[:, c * P:(c + 1) * P], w["bdown1"][:, :],
                                     start=False, stop=True)
                G.filled(last, G_OUT)

        @block.gpsimd
        def _(pool):
            g.wait_layer(pool, 0)
            with pool.Fori(0, B) as it:
                pool.wait_ge(var_ready, it + 1)
                norm_rstd(pool, g, st, NC).then_inc(rstd_ready, 1)

        @block.scalar
        def _(act):
            g.wait_layer(act, 1)
            act.wait_ge(setup_done, 1)
            with act.Fori(0, B) as it:
                for u in range(2):
                    b = G.read(act, it, G_Q + u)
                    for j in range(2):
                        gg = 2 * u + j
                        last = act.activation(qT[:, gg, :], b[:, j * S:(j + 1) * S], ACT.Identity,
                                              bias=qbias[:, gg:gg + 1], scale=DH ** -0.5)
                    G.took(last, G_Q + u)
                G.wait_taken(act, it, G_LOGIT)
                act.activation(r.ex[:, :, :], r.ls[:, :, :], ACT.Exp).then_inc(gate_exp, 1)
                for s in range(NH):
                    act.wait_ge(negmax_ready, it * NH + s + 1)
                    act_probs(act, Sb[s % 2], negmax[:, s % 2, :], probs[:, s % 2, :],
                              [rowsum[:, c, s:s + 1] for c in range(NC)], FORWARD).then_inc(probs_ready, 1)
                    if s % 2 == 0:
                        e = s // 2
                        b = G.read(act, it, G_UP + 2 * e)
                        for j in range(2):
                            h = e * HC + j
                            last = act.activation(hT[:, e % 2, j, :], b[:, j * S:(j + 1) * S], ACT.Relu,
                                                  bias=w["bup1"][:, h:h + 1])
                        G.took(last, G_UP + 2 * e)

        @block.vector
        def _(dve):
            g.wait_consts(dve)
            g.wait_layer(dve, 1)
            for gg in range(NG):
                dve.tensor_scalar(qbias[:, gg:gg + 1], w["bq1"][:, gg:gg + 1], DH ** -0.5, g.one_row[:, 0:1],
                                  ALU.mult, ALU.add)
                last = dve.tensor_scalar(kconst[:, gg, :], g.alibi[:, gg, :], w["bk1"][:, gg:gg + 1], None, ALU.add)
            last.then_inc(setup_done, 1)
            dve.wait_ge(setup_done, 1)
            with dve.Fori(0, B) as it:
                ch = Chain(dve, dve_chain, it, n_chain)
                ch(dve.tensor_copy(xt[:, :, :], g.x_all[:, bass.ds(it * NC, NC), :]))
                norm_stats(dve, ch, xt, st, NC).then_inc(var_ready, 1)
                dve.wait_ge(rstd_ready, it + 1)
                norm_apply(dve, xt, xn, st, NC).then_inc(xn_ready, 1)
                b = G.read(dve, it, G_XNT)
                G.took(dve.tensor_copy(xnT[:, :], b[:, 0:S]), G_XNT)
                b = G.read(dve, it, G_LOGIT)
                G.took(router_rank(dve, ch, r, b[:, 0:NC * E].rearrange("p (c e) -> p c e", e=E), NC), G_LOGIT)
                for u in range(2):
                    b = G.read(dve, it, G_K + u)
                    G.took(dve.tensor_tensor(kT[:, 2 * u:2 * u + 2, :], chunks(b[:, :]),
                                             kconst[:, 2 * u:2 * u + 2, :], ALU.add), G_K + u)
                b = G.read(dve, it, G_V)
                G.took(dve.tensor_tensor(v[:, :, :], chunks(b[:, 0:S]), over_chunks(w["bv1"][:, :]), ALU.add), G_V)
                dve.wait_ge(gate_exp, it + 1)
                router_mix(dve, ch, r, g.iota, NC, False).then_inc(comb_ready, 1)
                dve.wait_ge(comb_ready, it + 1)
                for s in range(NH + 1):
                    e = s // 2
                    if s < NH:
                        dve.wait_ge(scores_ready, it * NH + s + 1)
                        dve_negmax(dve, Sb[s % 2], negmax[:, s % 2, :], FORWARD).then_inc(negmax_ready, 1)
                        if s % 2 == 0:
                            b = G.read(dve, it, G_UP + 2 * e + 1)
                            for j in range(2):
                                h = e * HC + 2 + j
                                last = dve.tensor_scalar(hT[:, e % 2, 2 + j, :], b[:, j * S:(j + 1) * S],
                                                         w["bup1"][:, h:h + 1], 0.0, ALU.add, ALU.max)
                            G.took(last, G_UP + 2 * e + 1)
                    if s >= 1:
                        dve.wait_ge(transposed, it * NH + s)
                        dve.tensor_copy(probsT[:, (s - 1) % 2, :], Tb[(s - 1) % 2][:, 0:AW]).then_inc(probsT_ready, 1)
                    if s < NH and s % 2 == 1:
                        dve.wait_ge(down_ready, it * E + e + 1)
                        if e:
                            dve.wait_ge(down_used, it * E + e + 1)
                        dve.scalar_tensor_tensor(out=xt[:, 0, :], in0=Db[:, 0:D], scalar=r.comb[:, 0, e:e + 1],
                                                 in1=xt[:, 0, :], op0=ALU.mult, op1=ALU.add)
                        dve.scalar_tensor_tensor(out=xt[:, 1, :], in0=Db[:, D:2 * D], scalar=r.comb[:, 1, e:e + 1],
                                                 in1=xt[:, 1, :], op0=ALU.mult, op1=ALU.add).then_inc(down_used, 1)
                b = G.read(dve, it, G_COMBT)
                G.took(dve.tensor_copy(combT[:, :], b[0:E, 0:S]), G_COMBT)
                dve.wait_ge(heads_summed, it + 1)
                ch(dve.reciprocal(rrow[:, :, :], rowsum[:, :, :]))
                for c in range(NC):
                    last = dve.tensor_tensor(on[:, c, :].rearrange("p (h d) -> p h d", h=NH),
                                             Ob[:, c * D:(c + 1) * D].rearrange("p (h d) -> p h d", h=NH),
                                             rrow[:, c, :].unsqueeze(2).to_broadcast([P, NH, DH]), ALU.mult)
                last.then_inc(on_ready, 1)
                b = G.read(dve, it, G_OT)
                G.took(dve.tensor_copy(oT[:, :], b[:, 0:S]), G_OT)
                b = G.read(dve, it, G_OUT)
                dve.wait_ge(down_used, it * E + E + 1)
                m = dve.tensor_tensor(xt[:, :, :], xt[:, :, :], chunks(b[:, 0:S]), ALU.add)
                G.took(m, G_OUT)
                G.wait_taken(dve, it, G_OUT)
                ch(dve.tensor_tensor(g.x_all[:, bass.ds(it * NC, NC), :], xt[:, :, :], over_chunks(w["bout1"][:, :]), ALU.add))
                ch.done()


LH = 8
LD = 64
LHALF = LD // 2
INNER = LH * LD
IB = INNER // P
FFN = int(D * 4 * 2 / 3)
FC = -(-FFN // P)
WINDOW = 64
DEPTH = 2
WAYS = 2
UNITS = WAYS * NH + DEPTH * LH


def layer2(nc, g, B):
    w = g.w
    with ExitStack() as ctx:
        def sb(name, shape, dt=FP32):
            return ctx.enter_context(nc.sbuf_tensor("l2_" + name, shape, dt))

        def sem(name):
            return ctx.enter_context(nc.semaphore("l2_" + name))

        xt = sb("xt", [P, NC, D])
        xl = sb("xl", [P, NC, D])
        xnT = sb("xnT", [P, S])
        st = stat_buffers(sb, NC)
        z = sb("z", [P, NC, NH])
        za = sb("za", [P, NC, NH])
        ze = sb("ze", [P, NC, NH])
        zl = sb("zl", [P, NC, NH])
        f = sb("f", [P, NC, NH])
        cums = sb("cums", [P, NC, NH, SLOT])
        qT = sb("qT", [P, WAYS, NG, S])
        kT = sb("kT", [P, NG, S])
        v = sb("v", [P, NC, D])
        negmax = sb("negmax", [P, 2, NC])
        probs = sb("probs", [P, 2, AW])
        probsT = sb("probsT", [P, 2, AW])
        rowsum = sb("rowsum", [P, WAYS, NC, NH])
        rrow = sb("rrow", [P, WAYS, NC, NH])
        on = sb("on", [P, WAYS, NC, D])
        oT = sb("oT", [P, WAYS, S])
        tables = sb("tables", [P, DEPTH, 4, NC * LD])
        hT = sb("hT", [P, S])
        sq = sb("sq", [P, 2, INNER])
        ss = sb("ss", [P, 4, LH])
        ssm = sb("ssm", [P, 4, LH])
        rinv = sb("rinv", [P, 4, LH])
        rot = sb("rot", [P, 2, INNER])
        qk_raw = sb("qk_raw", [P, 4, INNER])
        qkT = sb("qkT", [P, 2, IB, S])
        v2 = sb("v2", [P, NC, INNER])
        rowsum2 = sb("rowsum2", [P, NC, LH])
        rrow2 = sb("rrow2", [P, NC, LH])
        on2 = sb("on2", [P, NC, INNER])
        oT2 = sb("oT2", [P, IB, S])
        st2 = Names()
        st2.stats, st2.mv, st2.pad = sb("stats2", [P, NC, 6]), sb("mean_var2", [P, NC, 2]), sb("norm_pad2", [1, 1])
        st2.var, st2.rstd = sb("var2", [P, NC]), sb("rstd2", [P, NC])
        hs = sb("hs", [P, NC, D])
        hn = sb("hn", [P, NC, D])
        hnT = sb("hnT", [P, S])
        gg = sb("gg", [P, 2, S])
        hidT = sb("hidT", [P, FC, S])

        Sb, Tb, Ob = g.bank[0:2], g.bank[2:4], g.bank[6:8]
        G_XNT, G_F, G_CUM, G_Q, G_K, G_V, G_OT, G_OUT, G_LOCAL = 0, 1, 2, 3, 5, 7, 8, 9, 10
        L_XT, L_QK, L_V, L_QKT, L_OT, L_OUT, L_XT2, L_HS, L_HNT, L_UP = 0, 1, 5, 7, 11, 13, 14, 15, 16, 17
        L_DOWN = L_UP + FC
        PER_LAYER = L_DOWN + 1
        G = Banks(g.bank[4:6], [sem("g_full0"), sem("g_full1")], [sem("g_taken0"), sem("g_taken1")],
                  G_LOCAL + DEPTH * PER_LAYER)

        setup_done = sem("setup_done")
        var_ready = sem("var_ready")
        rstd_ready = sem("rstd_ready")
        xn_ready = sem("xn_ready")
        act_chain = sem("act_chain")
        zl_ready = sem("zl_ready")
        f_ready = sem("f_ready")
        scores_ready = sem("scores_ready")
        negmax_ready = sem("negmax_ready")
        probs_ready = sem("probs_ready")
        transposed = sem("transposed")
        probsT_ready = sem("probsT_ready")
        heads_summed = sem("heads_summed")
        on_ready = sem("on_ready")
        sq_ready = sem("sq_ready")
        ss_ready = sem("ss_ready")
        rinv_ready = sem("rinv_ready")
        qkn_ready = sem("qkn_ready")
        heads2_summed = sem("heads2_summed")
        on2_ready = sem("on2_ready")
        var2_ready = sem("var2_ready")
        rstd2_ready = sem("rstd2_ready")
        hn_ready = sem("hn_ready")
        gelu_ready = sem("gelu_ready")
        xl_ready = sem("xl_ready")
        x_done = sem("x_done")
        dve_chain = sem("dve_chain")
        n_chain = 1 + NORM_STEPS(NC) + 1 + DEPTH * (4 * 3 + 1 + NORM_STEPS(NC))

        block = ctx.enter_context(nc.Block())

        def unit_heads():
            return [(y * NH + h, y, h) for y in range(WAYS) for h in range(NH)]

        @block.tensor
        def _(pe):
            g.wait_consts(pe)
            g.wait_layer(pe, 2)
            G.open(pe)
            with pe.Fori(0, B) as it:
                def attention(units, u0, scores, values, summed):
                    for s in range(units + 2):
                        u = u0 + s
                        if s < units:
                            scores(s, Sb[u % 2]).then_inc(scores_ready, 1)
                        if s >= 2:
                            pe.wait_ge(probsT_ready, it * UNITS + u - 2 + 1)
                            last = values(s - 2, probsT[:, u % 2, :])
                            if s == units + 1:
                                last.then_inc(summed, 1)
                        if 1 <= s <= units:
                            pe.wait_ge(probs_ready, it * UNITS + u - 1 + 1)
                            pe_transpose3(pe, g, Tb[(u - 1) % 2], probs[:, (u - 1) % 2, :]).then_inc(transposed, 1)

                pe.wait_ge(xn_ready, it + 1)
                b = G.fill(pe, it, G_XNT)
                for c in range(NC):
                    last = pe.transpose(b[:, c * P:(c + 1) * P], xl[:, c, :], g.ident[:, :])
                G.filled(last, G_XNT)
                G.wait_taken(pe, it, G_XNT)
                b = G.fill(pe, it, G_F)
                for c in range(NC):
                    last = pe.matmul(b[:, c * NH:(c + 1) * NH], xnT[:, c * P:(c + 1) * P], w["f2"][:, :],
                                     start=True, stop=True)
                G.filled(last, G_F)
                pe.wait_ge(f_ready, it + 1)
                b = G.fill(pe, it, G_CUM)
                for y, c, parts in ((0, 0, ((0, w["tri2"]), )), (0, 1, ((0, w["ones2"]), (1, w["tri2"]))),
                                    (1, 0, ((0, w["tri_back2"]), (1, w["ones2"]))), (1, 1, ((1, w["tri_back2"]), ))):
                    at = (y * NC + c) * NH
                    for i, (src, m) in enumerate(parts):
                        last = pe.matmul(b[:, at:at + NH], m[:, :], f[:, src, :],
                                         start=(i == 0), stop=(i == len(parts) - 1))
                G.filled(last, G_CUM)
                for u in range(2):
                    b = G.fill(pe, it, G_Q + u)
                    for j in range(2):
                        gi = 2 * u + j
                        last = pe.matmul(b[:, j * S:(j + 1) * S], w["q2"][:, gi * P:(gi + 1) * P], xnT[:, :],
                                         start=True, stop=True)
                    G.filled(last, G_Q + u)
                for u in range(2):
                    b = G.fill(pe, it, G_K + u)
                    if u == 0:
                        G.wait_taken(pe, it, G_CUM)
                    for j in range(2):
                        gi = 2 * u + j
                        pe.matmul(b[:, j * S:(j + 1) * S], w["k2"][:, gi * P:(gi + 1) * P], xnT[:, :],
                                  start=True, stop=False, skip_group_check=True)
                        for c in range(NC):
                            last = pe.matmul(b[:, j * S + c * P:j * S + (c + 1) * P],
                                             cums[:, c, gi * GH:(gi + 1) * GH, :].rearrange("p h s -> p (h s)"),
                                             g.ident[:, :], start=False, stop=(c == NC - 1), skip_group_check=True)
                    G.filled(last, G_K + u)
                b = G.fill(pe, it, G_V)
                for c in range(NC):
                    last = pe.matmul(b[:, c * P:(c + 1) * P], xnT[:, c * P:(c + 1) * P], w["v2w"][:, :],
                                     start=True, stop=True)
                G.filled(last, G_V)
                G.wait_taken(pe, it, G_V - 1)
                G.wait_taken(pe, it, G_V)
                UH = unit_heads()

                def scores(s, bank):
                    _, y, h = UH[s]
                    rows = slice(SLOT * (h % GH), SLOT * (h % GH + 1))
                    return pe_scores(pe, g, bank, qT[rows, y, h // GH, :], kT[rows, h // GH, :],
                                     (g.mask_causal, g.mask_anti)[y], (FORWARD, BACKWARD)[y])

                def values(s, pt):
                    _, y, h = UH[s]
                    outs = [Ob[0][:, (y * NC + c) * D + h * DH:(y * NC + c) * D + (h + 1) * DH] for c in range(NC)]
                    return pe_values(pe, outs, pt, v[:, :, h * DH:(h + 1) * DH], (FORWARD, BACKWARD)[y])

                attention(WAYS * NH, 0, scores, values, heads_summed)
                pe.wait_ge(on_ready, it + 1)
                b = G.fill(pe, it, G_OT)
                for y in range(WAYS):
                    for c in range(NC):
                        last = pe.transpose(b[:, (y * NC + c) * P:(y * NC + c + 1) * P], on[:, y, c, :], g.ident[:, :])
                G.filled(last, G_OT)
                G.wait_taken(pe, it, G_OT)
                b = G.fill(pe, it, G_OUT)
                for c in range(NC):
                    for y in range(WAYS):
                        last = pe.matmul(b[:, c * P:(c + 1) * P], oT[:, y, c * P:(c + 1) * P], w["out2"][:, y, :],
                                         start=(y == 0), stop=(y == WAYS - 1))
                G.filled(last, G_OUT)

                for l in range(DEPTH):
                    k0 = G_LOCAL + l * PER_LAYER
                    if l:
                        pe.wait_ge(xl_ready, it * DEPTH + l)
                    b = G.fill(pe, it, k0 + L_XT)
                    for c in range(NC):
                        last = pe.transpose(b[:, c * P:(c + 1) * P], xl[:, c, :], g.ident[:, :])
                    G.filled(last, k0 + L_XT)
                    G.wait_taken(pe, it, k0 + L_XT)
                    for i in range(4):
                        c = i % 2
                        b = G.fill(pe, it, k0 + L_QK + i)
                        G.filled(pe.matmul(b[:, :], hT[:, c * P:(c + 1) * P],
                                           w["qkv2"][:, l, (i // 2) * INNER:(i // 2 + 1) * INNER], start=True, stop=True),
                                 k0 + L_QK + i)
                    for c in range(NC):
                        b = G.fill(pe, it, k0 + L_V + c)
                        G.filled(pe.matmul(b[:, :], hT[:, c * P:(c + 1) * P], w["qkv2"][:, l, 2 * INNER:3 * INNER],
                                           start=True, stop=True), k0 + L_V + c)
                    for i in range(4):
                        pe.wait_ge(qkn_ready, (it * DEPTH + l) * 4 + i + 1)
                        b = G.fill(pe, it, k0 + L_QKT + i)
                        for j in range(IB):
                            last = pe.transpose(b[:, j * P:(j + 1) * P], qk_raw[:, i, j * P:(j + 1) * P], g.ident[:, :])
                        G.filled(last, k0 + L_QKT + i)
                    G.wait_taken(pe, it, k0 + L_QKT + 2)
                    G.wait_taken(pe, it, k0 + L_QKT + 3)

                    def scores2(s, bank):
                        rows = slice(LD * (s % 2), LD * (s % 2 + 1))
                        return pe_scores(pe, g, bank, qkT[rows, 0, s // 2, :], qkT[rows, 1, s // 2, :],
                                         g.mask_band, FORWARD)

                    def values2(s, pt):
                        return pe_values(pe, [Ob[c][:, s * LD:(s + 1) * LD] for c in range(NC)], pt,
                                         v2[:, :, s * LD:(s + 1) * LD], FORWARD)

                    attention(LH, WAYS * NH + l * LH, scores2, values2, heads2_summed)
                    pe.wait_ge(on2_ready, it * DEPTH + l + 1)
                    for c in range(NC):
                        b = G.fill(pe, it, k0 + L_OT + c)
                        for j in range(IB):
                            last = pe.transpose(b[:, j * P:(j + 1) * P], on2[:, c, j * P:(j + 1) * P], g.ident[:, :])
                        G.filled(last, k0 + L_OT + c)
                    G.wait_taken(pe, it, k0 + L_OT)
                    G.wait_taken(pe, it, k0 + L_OT + 1)
                    b = G.fill(pe, it, k0 + L_OUT)
                    for c in range(NC):
                        for j in range(IB):
                            last = pe.matmul(b[:, c * P:(c + 1) * P], oT2[:, j, c * P:(c + 1) * P],
                                             w["wo2"][:, l, j, :], start=(j == 0), stop=(j == IB - 1))
                    G.filled(last, k0 + L_OUT)
                    G.wait_taken(pe, it, k0 + L_OUT)
                    b = G.fill(pe, it, k0 + L_XT2)
                    for c in range(NC):
                        last = pe.transpose(b[:, c * P:(c + 1) * P], xl[:, c, :], g.ident[:, :])
                    G.filled(last, k0 + L_XT2)
                    G.wait_taken(pe, it, k0 + L_XT2)
                    b = G.fill(pe, it, k0 + L_HS)
                    for c in range(NC):
                        last = pe.transpose(b[:, c * P:(c + 1) * P], hT[:, c * P:(c + 1) * P], g.ident[:, :])
                    G.filled(last, k0 + L_HS)
                    pe.wait_ge(hn_ready, it * DEPTH + l + 1)
                    b = G.fill(pe, it, k0 + L_HNT)
                    for c in range(NC):
                        last = pe.transpose(b[:, c * P:(c + 1) * P], hn[:, c, :], g.ident[:, :])
                    G.filled(last, k0 + L_HNT)
                    G.wait_taken(pe, it, k0 + L_HNT)
                    for m in range(FC):
                        b = G.fill(pe, it, k0 + L_UP + m)
                        pe.matmul(b[:, 0:S], w["up2"][:, l, 0, m * P:(m + 1) * P], hnT[:, :], start=True, stop=True)
                        G.filled(pe.matmul(b[:, S:2 * S], w["up2"][:, l, 1, m * P:(m + 1) * P], hnT[:, :],
                                           start=True, stop=True), k0 + L_UP + m)
                    G.wait_taken(pe, it, k0 + L_UP + FC - 2)
                    G.wait_taken(pe, it, k0 + L_UP + FC - 1)
                    b = G.fill(pe, it, k0 + L_DOWN)
                    for c in range(NC):
                        for m in range(FC):
                            last = pe.matmul(b[:, c * P:(c + 1) * P], hidT[:, m, c * P:(c + 1) * P],
                                             w["down2"][:, l, m, :], start=(m == 0), stop=(m == FC - 1))
                    G.filled(last, k0 + L_DOWN)

        @block.gpsimd
        def _(pool):
            g.wait_layer(pool, 0)
            with pool.Fori(0, B) as it:
                pool.wait_ge(var_ready, it + 1)
                norm_rstd(pool, g, st, NC).then_inc(rstd_ready, 1)
                for l in range(DEPTH):
                    pool.wait_ge(ss_ready, it * DEPTH + l + 1)
                    pool.tensor_tensor(rinv[:, :, :], ssm[:, :, :], g.neg_half[:, 0:4 * LH].rearrange(
                        "p (i h) -> p i h", i=4), ALU.pow).then_inc(rinv_ready, 1)
                    pool.wait_ge(rinv_ready, it * DEPTH + l + 1)
                    for i in range(4):
                        pool.tensor_tensor(qk_raw[:, i, :].rearrange("p (h d) -> p h d", h=LH),
                                           qk_raw[:, i, :].rearrange("p (h d) -> p h d", h=LH),
                                           rinv[:, i, :].unsqueeze(2).to_broadcast([P, LH, LD]),
                                           ALU.mult).then_inc(qkn_ready, 1)
                    pool.wait_ge(var2_ready, it * DEPTH + l + 1)
                    norm_rstd(pool, g, st2, NC).then_inc(rstd2_ready, 1)

        @block.scalar
        def _(act):
            g.wait_layer(act, 2)
            g.wait_consts(act)
            with act.Fori(0, B) as it:
                def exps(units, u0, sums, way):
                    for s in range(units):
                        u = u0 + s
                        act.wait_ge(negmax_ready, it * UNITS + u + 1)
                        act_probs(act, Sb[u % 2], negmax[:, u % 2, :], probs[:, u % 2, :], sums(s),
                                  way(s)).then_inc(probs_ready, 1)

                ch = Chain(act, act_chain, it, 2)
                G.wait_taken(act, it, G_F)
                ch(act.activation(za[:, :, :], z[:, :, :], ACT.Abs))
                ch(act.activation(ze[:, :, :], za[:, :, :], ACT.Exp, scale=-1.0))
                act.activation(zl[:, :, :], ze[:, :, :], ACT.Ln, bias=1.0).then_inc(zl_ready, 1)
                for u in range(2):
                    b = G.read(act, it, G_Q + u)
                    for y in range(WAYS):
                        last = act.activation(qT[:, y, 2 * u:2 * u + 2, :], chunks(b[:, :]), ACT.Identity,
                                              bias=w["one_rows2"][:, y:y + 1], scale=DH ** -0.5)
                    G.took(last, G_Q + u)
                exps(WAYS * NH, 0, lambda s: [rowsum[:, s // NH, c, s % NH:s % NH + 1] for c in range(NC)],
                     lambda s: (FORWARD, BACKWARD)[s // NH])
                for l in range(DEPTH):
                    k0 = G_LOCAL + l * PER_LAYER
                    for i in range(4):
                        b = G.read(act, it, k0 + L_QK + i)
                        act.activation(sq[:, i % 2, :], b[:, :], ACT.Square).then_inc(sq_ready, 1)
                    for c in range(NC):
                        b = G.read(act, it, k0 + L_V + c)
                        G.took(act.activation(v2[:, c, :], b[:, :], ACT.Copy), k0 + L_V + c)
                    for c in range(NC):
                        b = G.read(act, it, k0 + L_QKT + c)
                        G.took(act.activation(qkT[:, 0, :, c * P:(c + 1) * P], chunks(b[:, :], IB), ACT.Copy),
                               k0 + L_QKT + c)
                    exps(LH, WAYS * NH + l * LH, lambda s: [rowsum2[:, c, s:s + 1] for c in range(NC)],
                         lambda s: FORWARD)
                    for m in range(FC):
                        b = G.read(act, it, k0 + L_UP + m)
                        act.activation(gg[:, m % 2, :], b[:, S:2 * S], ACT.Gelu,
                                       bias=w["bup2"][:, l, 1, m:m + 1]).then_inc(gelu_ready, 1)

        @block.vector
        def _(dve):
            g.wait_consts(dve)
            g.wait_layer(dve, 2)
            for l in range(DEPTH):
                dve.tensor_tensor(tables[:, l, :, :].rearrange("p i (c d) -> p i c d", c=NC),
                                  w["rot2"][:, :, :].rearrange("p i (c d) -> p i c d", c=NC),
                                  w["scale_rows2"][:, l, :, :].unsqueeze(2).to_broadcast([P, 4, NC, LD]), ALU.mult)
            dve.memset(hT[:, 0:1], 0.0)
            dve.memset(cums[:, :, :, :], 0.0).then_inc(setup_done, 1)
            dve.wait_ge(setup_done, 1)
            with dve.Fori(0, B) as it:
                ch = Chain(dve, dve_chain, it, n_chain)

                def shifted(k):
                    b = G.read(dve, it, k)
                    dve.tensor_copy(hT[0:P // 2, :], b[0:P // 2, 0:S])
                    G.took(dve.tensor_copy(hT[P // 2:P, 1:S], b[P // 2:P, 0:S - 1]), k)

                def maxima(units, u0, way):
                    for s in range(units + 1):
                        u = u0 + s
                        if s < units:
                            dve.wait_ge(scores_ready, it * UNITS + u + 1)
                            dve_negmax(dve, Sb[u % 2], negmax[:, u % 2, :], way(s)).then_inc(negmax_ready, 1)
                        if s >= 1:
                            dve.wait_ge(transposed, it * UNITS + u)
                            dve.tensor_copy(probsT[:, (u - 1) % 2, :],
                                            Tb[(u - 1) % 2][:, 0:AW]).then_inc(probsT_ready, 1)

                ch(dve.tensor_copy(xt[:, :, :], g.x_all[:, bass.ds(it * NC, NC), :]))
                norm_stats(dve, ch, xt, st, NC).then_inc(var_ready, 1)
                dve.wait_ge(rstd_ready, it + 1)
                norm_apply(dve, xt, xl, st, NC).then_inc(xn_ready, 1)
                b = G.read(dve, it, G_XNT)
                G.took(dve.tensor_copy(xnT[:, :], b[:, 0:S]), G_XNT)
                b = G.read(dve, it, G_F)
                G.took(dve.tensor_tensor(z[:, :, :], chunks(b[:, 0:NC * NH]), over_chunks(w["bf2"][:, :]), ALU.add), G_F)
                dve.wait_ge(zl_ready, it + 1)
                dve.scalar_tensor_tensor(out=f[:, :, :], in0=z[:, :, :], scalar=0.0, in1=zl[:, :, :],
                                         op0=ALU.min, op1=ALU.subtract).then_inc(f_ready, 1)
                b = G.read(dve, it, G_CUM)
                for y in range(WAYS):
                    last = dve.tensor_scalar(cums[:, :, :, DH + y], chunks(b[:, y * NC * NH:(y + 1) * NC * NH]), -1.0,
                                             None, ALU.mult)
                G.took(last, G_CUM)
                for u in range(2):
                    b = G.read(dve, it, G_K + u)
                    G.took(dve.tensor_copy(kT[:, 2 * u:2 * u + 2, :], chunks(b[:, :])), G_K + u)
                b = G.read(dve, it, G_V)
                G.took(dve.tensor_copy(v[:, :, :], chunks(b[:, 0:S])), G_V)
                maxima(WAYS * NH, 0, lambda s: (FORWARD, BACKWARD)[s // NH])
                dve.wait_ge(heads_summed, it + 1)
                ch(dve.reciprocal(rrow[:, :, :, :], rowsum[:, :, :, :]))
                for y in range(WAYS):
                    for c in range(NC):
                        last = dve.tensor_tensor(
                            on[:, y, c, :].rearrange("p (h d) -> p h d", h=NH),
                            Ob[0][:, (y * NC + c) * D:(y * NC + c + 1) * D].rearrange("p (h d) -> p h d", h=NH),
                            rrow[:, y, c, :].unsqueeze(2).to_broadcast([P, NH, DH]), ALU.mult)
                last.then_inc(on_ready, 1)
                b = G.read(dve, it, G_OT)
                G.took(dve.tensor_copy(oT[:, :, :], chunks(b[:, :])), G_OT)
                b = G.read(dve, it, G_OUT)
                G.took(dve.tensor_tensor(xt[:, :, :], xt[:, :, :], chunks(b[:, 0:S]), ALU.add), G_OUT)

                for l in range(DEPTH):
                    k0 = G_LOCAL + l * PER_LAYER
                    shifted(k0 + L_XT)
                    for i in range(4):
                        c, cos, sin = i % 2, 2 * (i // 2), 2 * (i // 2) + 1
                        b = G.read(dve, it, k0 + L_QK + i)
                        dve.wait_ge(sq_ready, (it * DEPTH + l) * 4 + i + 1)
                        bh = b[:, :].rearrange("p (h d) -> p h d", h=LH)
                        rh = rot[:, i % 2, :].rearrange("p (h d) -> p h d", h=LH)

                        def table(n, lo, hi):
                            return tables[:, l, n, c * LD + lo:c * LD + hi].unsqueeze(1).to_broadcast([P, LH, hi - lo])

                        ch.mark(dve.reduce_sum(ss[:, i, :], sq[:, i % 2, :].rearrange("p (h d) -> p h d", h=LH), AX.X))
                        dve.tensor_tensor(rh[:, :, 0:LHALF], bh[:, :, LHALF:LD], table(sin, 0, LHALF), ALU.mult)
                        ch(dve.tensor_tensor(rh[:, :, LHALF:LD], bh[:, :, 0:LHALF], table(sin, LHALF, LD), ALU.mult))
                        ch(dve.tensor_tensor(bh, bh, table(cos, 0, LD), ALU.mult))
                        G.took(dve.tensor_tensor(qk_raw[:, i, :], b[:, :], rot[:, i % 2, :], ALU.add), k0 + L_QK + i)
                        if i == 3:
                            G.wait_taken(dve, it, k0 + L_QK + i)
                            dve.tensor_scalar(ssm[:, :, :], ss[:, :, :], 1e-24, None, ALU.max).then_inc(ss_ready, 1)
                    for c in range(NC):
                        b = G.read(dve, it, k0 + L_QKT + 2 + c)
                        G.took(dve.tensor_copy(qkT[:, 1, :, c * P:(c + 1) * P], chunks(b[:, :], IB)), k0 + L_QKT + 2 + c)
                    maxima(LH, WAYS * NH + l * LH, lambda s: FORWARD)
                    dve.wait_ge(heads2_summed, it * DEPTH + l + 1)
                    ch(dve.reciprocal(rrow2[:, :, :], rowsum2[:, :, :]))
                    for c in range(NC):
                        last = dve.tensor_tensor(on2[:, c, :].rearrange("p (h d) -> p h d", h=LH),
                                                 Ob[c][:, :].rearrange("p (h d) -> p h d", h=LH),
                                                 rrow2[:, c, :].unsqueeze(2).to_broadcast([P, LH, LD]), ALU.mult)
                    last.then_inc(on2_ready, 1)
                    for c in range(NC):
                        b = G.read(dve, it, k0 + L_OT + c)
                        G.took(dve.tensor_copy(oT2[:, :, c * P:(c + 1) * P], chunks(b[:, :], IB)), k0 + L_OT + c)
                    b = G.read(dve, it, k0 + L_OUT)
                    G.took(dve.tensor_tensor(xl[:, :, :], xl[:, :, :], chunks(b[:, 0:S]), ALU.add), k0 + L_OUT)
                    shifted(k0 + L_XT2)
                    b = G.read(dve, it, k0 + L_HS)
                    G.took(dve.tensor_copy(hs[:, :, :], chunks(b[:, 0:S])), k0 + L_HS)
                    G.wait_taken(dve, it, k0 + L_HS)
                    norm_stats(dve, ch, hs, st2, NC).then_inc(var2_ready, 1)
                    dve.wait_ge(rstd2_ready, it * DEPTH + l + 1)
                    norm_apply(dve, hs, hn, st2, NC).then_inc(hn_ready, 1)
                    b = G.read(dve, it, k0 + L_HNT)
                    G.took(dve.tensor_scalar(hnT[:, :], b[:, 0:S], w["ln2"][:, l, 0:1], w["ln2"][:, l, 1:2],
                                             ALU.mult, ALU.add), k0 + L_HNT)
                    for m in range(FC):
                        b = G.read(dve, it, k0 + L_UP + m)
                        dve.wait_ge(gelu_ready, (it * DEPTH + l) * FC + m + 1)
                        G.took(dve.scalar_tensor_tensor(out=hidT[:, m, :], in0=b[:, 0:S],
                                                        scalar=w["bup2"][:, l, 0, m:m + 1], in1=gg[:, m % 2, :],
                                                        op0=ALU.add, op1=ALU.mult), k0 + L_UP + m)
                    b = G.read(dve, it, k0 + L_DOWN)
                    G.took(dve.tensor_tensor(xl[:, :, :], xl[:, :, :], chunks(b[:, 0:S]), ALU.add), k0 + L_DOWN)
                    G.wait_taken(dve, it, k0 + L_DOWN)
                    dve.tensor_tensor(xl[:, :, :], xl[:, :, :], over_chunks(w["bdown2"][:, l, :]),
                                      ALU.add).then_inc(xl_ready, 1)
                dve.wait_ge(xl_ready, it * DEPTH + DEPTH)
                dve.tensor_tensor(g.x_all[:, bass.ds(it * NC, NC), :], xt[:, :, :], xl[:, :, :],
                                  ALU.add).then_inc(x_done, 1)
                dve.wait_ge(x_done, it + 1)
                dve.memset(st.pad[:, :], 0.0)
                ch.done()


FB = 8
GELU_IN = math.sqrt(2.0 / math.pi)


def layer3(nc, g, B, out):
    w = g.w
    with ExitStack() as ctx:
        def sb(name, shape, dt=FP32):
            return ctx.enter_context(nc.sbuf_tensor("l3_" + name, shape, dt))

        def sem(name):
            return ctx.enter_context(nc.semaphore("l3_" + name))

        xt = sb("xt", [P, NC, D])
        xn = sb("xn", [P, NC, D])
        xnT = sb("xnT", [P, S])
        st = stat_buffers(sb, NC)
        r = router_buffers(sb, NC)
        bq_one = sb("bq_one", [P, FB])
        bk_one = sb("bk_one", [P, FB])
        neg_bq = sb("neg_bq", [P, FB])
        neg_bk = sb("neg_bk", [P, FB])
        neg_part = sb("neg_part", [P, 2, 2, S])
        exp_raw = sb("exp_raw", [P, 2, 2, S])
        exp_part = sb("exp_part", [P, 2, 2, S])
        k_feat = sb("k_feat", [P, 2, S])
        q_feat = sb("q_feat", [P, 2, S])
        kv_junk = sb("kv_junk", [P, 2, S])
        k_sum = sb("k_sum", [P, FB])
        kv_sum = sb("kv_sum", [P, FB])
        den = sb("den", [P, 2, S])
        rden = sb("rden", [P, 2, S])
        pool_pad = sb("pool_pad", [1, 2 * FB])
        qkv = sb("qkv", [P, 2, S])
        attnT = sb("attnT", [P, FB, S])
        th = sb("th", [P, 2, 2 * S])
        gated = sb("gated", [P, 2, 2 * S])
        hT = sb("hT", [P, 2, HC, S])
        y = sb("y", [P, NC, D])
        y2 = sb("y2", [P, NC, D])
        ty = sb("ty", [P, NC, D])

        Db, Ob = g.bank[5:7], g.bank[7]
        G_XNT, G_LOGIT, G_STEP, PER_STEP = 0, 1, 2, 6
        G = Banks(g.bank[0:5], [sem(f"g_full{i}") for i in range(5)], [sem(f"g_taken{i}") for i in range(5)],
                  2 + PER_STEP * E)
        var_ready = sem("var_ready")
        rstd_ready = sem("rstd_ready")
        xn_ready = sem("xn_ready")
        setup_done = sem("setup_done")
        gate_exp = sem("gate_exp")
        neg_ready = sem("neg_ready")
        raw_ready = sem("raw_ready")
        pool_chain = sem("pool_chain")
        rden_ready = sem("rden_ready")
        exp_ready = sem("exp_ready")
        k_ready = sem("k_ready")
        attn_ready = sem("attn_ready")
        tanh_ready = sem("tanh_ready")
        down_ready = sem("down_ready")
        down_used = sem("down_used")
        out_ready = sem("out_ready")
        gelu_in = sem("gelu_in")
        gelu_tanh = sem("gelu_tanh")
        x_done = sem("x_done")
        stored = sem("stored")
        dve_chain = sem("dve_chain")
        n_chain = 1 + NORM_STEPS(NC) + ROUTER_STEPS(NC) + 1 + FB + 4

        block = ctx.enter_context(nc.Block())

        @block.tensor
        def _(pe):
            g.wait_consts(pe)
            g.wait_layer(pe, 3)
            G.open(pe)
            pe.sem_inc(down_used, 2)
            with pe.Fori(0, B) as it:
                pe.wait_ge(xn_ready, it + 1)
                b = G.fill(pe, it, G_XNT)
                for c in range(NC):
                    last = pe.transpose(b[:, c * P:(c + 1) * P], xn[:, c, :], g.ident[:, :])
                G.filled(last, G_XNT)
                G.wait_taken(pe, it, G_XNT)
                b = G.fill(pe, it, G_LOGIT)
                for c in range(NC):
                    last = pe.matmul(b[:, c * E:(c + 1) * E], xnT[:, c * P:(c + 1) * P], w["gate3"][:, :],
                                     start=True, stop=True)
                G.filled(last, G_LOGIT)
                for m in range(E + 1):
                    if m < E:
                        k = G_STEP + PER_STEP * m
                        cols = slice(m * P, (m + 1) * P)
                        b = G.fill(pe, it, k)
                        pe.matmul(b[:, 0:S], w["k3"][:, cols], xnT[:, :], start=True, stop=True)
                        G.filled(pe.matmul(b[:, S:2 * S], w["v3"][:, cols], xnT[:, :], start=True, stop=True), k)
                        b = G.fill(pe, it, k + 1)
                        G.filled(pe.matmul(b[:, 0:S], w["q3"][:, cols], xnT[:, :], start=True, stop=True), k + 1)
                        for u in range(2):
                            for i, wt in enumerate((w["egate3"], w["eup3"])):
                                kk = k + 2 + 2 * u + i
                                b = G.fill(pe, it, kk)
                                for j in range(2):
                                    h = (m * HC + 2 * u + j) * P
                                    last = pe.matmul(b[:, j * S:(j + 1) * S], wt[:, h:h + P], xnT[:, :],
                                                     start=True, stop=True)
                                G.filled(last, kk)
                    if m >= 1:
                        e = m - 1
                        G.wait_taken(pe, it, G_STEP + PER_STEP * e + 3)
                        G.wait_taken(pe, it, G_STEP + PER_STEP * e + 5)
                        pe.wait_ge(down_used, it * E + e + 1)
                        for c in range(NC):
                            for j in range(HC):
                                last = pe.matmul(Db[e % 2][:, c * P:(c + 1) * P], hT[:, e % 2, j, c * P:(c + 1) * P],
                                                 w["edown3"][:, e * HC + j, :], start=(j == 0), stop=(j == HC - 1))
                        last.then_inc(down_ready, 1)
                pe.wait_ge(attn_ready, it * FB + FB)
                for c in range(NC):
                    for m in range(FB):
                        last = pe.matmul(Ob[:, c * P:(c + 1) * P], attnT[:, m, c * P:(c + 1) * P], w["out3"][:, m, :],
                                         start=(m == 0), stop=(m == FB - 1))
                last.then_inc(out_ready, 1)

        @block.gpsimd
        def _(pool):
            g.wait_layer(pool, 0)
            with pool.Fori(0, B) as it:
                pool.wait_ge(var_ready, it + 1)
                norm_rstd(pool, g, st, NC).then_inc(rstd_ready, 1)
                ch = Chain(pool, pool_chain, it, FB)

                def attention_out(m):
                    s = m % 2
                    G.wait_taken(pool, it, G_STEP + PER_STEP * m)
                    pool_hold(pool, g, pool_pad[:, m:m + 1])
                    ch(pool.tensor_scalar(qkv[:, s, :], q_feat[:, s, :], kv_sum[:, m:m + 1], None, ALU.mult))
                    pool.wait_ge(rden_ready, it * FB + m + 1)
                    pool.tensor_tensor(attnT[:, m, :], qkv[:, s, :], rden[:, s, :], ALU.mult).then_inc(attn_ready, 1)

                for m in range(FB):
                    s = m % 2
                    pool.wait_ge(raw_ready, it * FB + m + 1)
                    pool_hold(pool, g, pool_pad[:, FB + m:FB + m + 1])
                    pool.tensor_scalar(exp_part[:, s, :, :], exp_raw[:, s, :, :], -1.0, 1.0,
                                       ALU.add, ALU.add).then_inc(exp_ready, 1)
                    if m >= 1:
                        attention_out(m - 1)
                attention_out(FB - 1)
                ch.done()

        @block.scalar
        def _(act):
            g.wait_layer(act, 3)
            act.wait_ge(setup_done, 1)
            with act.Fori(0, B) as it:
                G.wait_taken(act, it, G_LOGIT)
                act.activation(r.ex[:, :, :], r.ls[:, :, :], ACT.Exp).then_inc(gate_exp, 1)
                for m in range(E):
                    b = G.read(act, it, G_STEP + PER_STEP * m)
                    act.activation(neg_part[:, m % 2, 0, :], b[:, 0:S], ACT.Relu, bias=neg_bk[:, m:m + 1], scale=-1.0)
                    b = G.read(act, it, G_STEP + PER_STEP * m + 1)
                    act.activation(neg_part[:, m % 2, 1, :], b[:, 0:S], ACT.Relu, bias=neg_bq[:, m:m + 1],
                                   scale=-1.0).then_inc(neg_ready, 1)
                    act.wait_ge(neg_ready, it * FB + m + 1)
                    act.activation(exp_raw[:, m % 2, :, :], neg_part[:, m % 2, :, :], ACT.Exp,
                                   scale=-1.0).then_inc(raw_ready, 1)
                    for u in range(2):
                        b = G.read(act, it, G_STEP + PER_STEP * m + 2 + 2 * u)
                        act.activation(th[:, u, :], b[:, :], ACT.Tanh, scale=0.5).then_inc(tanh_ready, 1)
                act.wait_ge(gelu_in, it + 1)
                act.activation(ty[:, :, :], y2[:, :, :], ACT.Tanh, scale=GELU_IN).then_inc(gelu_tanh, 1)

        @block.sync
        def _(sp):
            with sp.Fori(0, B) as it:
                sp.wait_ge(x_done, it + 1)
                sp.dma_start(out[bass.ds(it, 1), :, :].rearrange("b (c p) d -> p (b c) d", p=P),
                             g.x_all[:, bass.ds(it * NC, NC), :]).then_inc(stored, 16)
            sp.wait_ge(stored, 16 * B)

        @block.vector
        def _(dve):
            g.wait_consts(dve)
            g.wait_layer(dve, 3)
            dve.tensor_scalar(bq_one[:, :], w["bq3"][:, :], 1.0, None, ALU.add)
            dve.tensor_scalar(neg_bk[:, :], w["bk3"][:, :], -1.0, None, ALU.mult)
            dve.tensor_scalar(neg_bq[:, :], w["bq3"][:, :], -1.0, None, ALU.mult)
            dve.tensor_scalar(bk_one[:, :], w["bk3"][:, :], 1.0, None, ALU.add).then_inc(setup_done, 1)
            dve.wait_ge(setup_done, 1)
            with dve.Fori(0, B) as it:
                ch = Chain(dve, dve_chain, it, n_chain)
                ch(dve.tensor_copy(xt[:, :, :], g.x_all[:, bass.ds(it * NC, NC), :]))
                norm_stats(dve, ch, xt, st, NC).then_inc(var_ready, 1)
                dve.wait_ge(rstd_ready, it + 1)
                norm_apply(dve, xt, xn, st, NC).then_inc(xn_ready, 1)
                b = G.read(dve, it, G_XNT)
                G.took(dve.tensor_copy(xnT[:, :], b[:, 0:S]), G_XNT)
                b = G.read(dve, it, G_LOGIT)
                G.took(router_rank(dve, ch, r, b[:, 0:NC * E].rearrange("p (c e) -> p c e", e=E), NC), G_LOGIT)
                dve.wait_ge(gate_exp, it + 1)
                ch(router_mix(dve, ch, r, g.iota, NC, False, scale=0.5))
                for m in range(E + 1):
                    if m < E:
                        k = G_STEP + PER_STEP * m
                        s = m % 2
                        bkv = G.read(dve, it, k)
                        bq = G.read(dve, it, k + 1)
                        dve.wait_ge(exp_ready, it * FB + m + 1)
                        dve.scalar_tensor_tensor(out=k_feat[:, s, :], in0=bkv[:, 0:S], scalar=bk_one[:, m:m + 1],
                                                 in1=exp_part[:, s, 0, :], op0=ALU.add, op1=ALU.max,
                                                 accum_out=k_sum[:, m:m + 1]).then_inc(k_ready, 1)
                        G.took(dve.scalar_tensor_tensor(out=q_feat[:, s, :], in0=bq[:, 0:S], scalar=bq_one[:, m:m + 1],
                                                        in1=exp_part[:, s, 1, :], op0=ALU.add, op1=ALU.max), k + 1)
                        dve.wait_ge(k_ready, it * E + m + 1)
                        G.took(dve.scalar_tensor_tensor(out=kv_junk[:, s, :], in0=bkv[:, S:2 * S],
                                                        scalar=w["bv3"][:, m:m + 1], in1=k_feat[:, s, :],
                                                        op0=ALU.add, op1=ALU.mult,
                                                        accum_out=kv_sum[:, m:m + 1]), k)
                        G.wait_taken(dve, it, k + 1)
                        ch(dve.tensor_scalar(den[:, s, :], q_feat[:, s, :], k_sum[:, m:m + 1], 1e-6,
                                             ALU.mult, ALU.add))
                        dve.reciprocal(rden[:, s, :], den[:, s, :]).then_inc(rden_ready, 1)
                        for u in range(2):
                            bg = G.read(dve, it, k + 2 + 2 * u)
                            dve.wait_ge(tanh_ready, it * 2 * E + 2 * m + u + 1)
                            G.took(dve.scalar_tensor_tensor(out=gated[:, u, :], in0=th[:, u, :], scalar=1.0,
                                                            in1=bg[:, :], op0=ALU.add, op1=ALU.mult), k + 2 + 2 * u)
                            bu = G.read(dve, it, k + 3 + 2 * u)
                            G.wait_taken(dve, it, k + 2 + 2 * u)
                            G.took(dve.tensor_tensor(hT[:, m % 2, 2 * u:2 * u + 2, :], chunks(gated[:, u, :]),
                                                     chunks(bu[:, :]), ALU.mult), k + 3 + 2 * u)
                    if m >= 1:
                        e = m - 1
                        dve.wait_ge(down_ready, it * E + e + 1)
                        dve.wait_ge(down_used, it * E + e + 2)
                        for c in range(NC):
                            last = dve.scalar_tensor_tensor(out=xt[:, c, :], in0=Db[e % 2][:, c * P:(c + 1) * P],
                                                            scalar=r.comb[:, c, e:e + 1], in1=xt[:, c, :],
                                                            op0=ALU.mult, op1=ALU.add)
                        last.then_inc(down_used, 1)
                dve.wait_ge(out_ready, it + 1)
                ch(dve.tensor_tensor(y[:, :, :], chunks(Ob[:, 0:S]), over_chunks(w["bout3"][:, :]), ALU.add))
                ch(dve.tensor_tensor(ty[:, :, :], y[:, :, :], y[:, :, :], ALU.mult))
                ch(dve.tensor_scalar(ty[:, :, :], ty[:, :, :], 0.044715, 1.0, ALU.mult, ALU.add))
                dve.tensor_tensor(y2[:, :, :], ty[:, :, :], y[:, :, :], ALU.mult).then_inc(gelu_in, 1)
                dve.wait_ge(gelu_tanh, it + 1)
                ch(dve.scalar_tensor_tensor(out=y2[:, :, :], in0=ty[:, :, :], scalar=1.0, in1=y[:, :, :],
                                            op0=ALU.add, op1=ALU.mult))
                dve.wait_ge(down_used, it * E + E + 2)
                dve.scalar_tensor_tensor(out=g.x_all[:, bass.ds(it * NC, NC), :], in0=y2[:, :, :], scalar=0.5,
                                         in1=xt[:, :, :], op0=ALU.mult, op1=ALU.add).then_inc(x_done, 1)
                dve.wait_ge(x_done, it + 1)
                dve.memset(st.pad[:, :], 0.0)
                ch.done()


def load_lists(B):
    t = {
        "ident": (0, [P, P]), "one_row": (0, [P, 1]), "iota": (0, [P, E]), "neg_half": (0, [P, 32]),
        "alibi": (1, [P, NG, S]), "masks": (0, [P, 3, AW]),
        "before0": (0, [P, P]), "after0": (0, [P, P]), "eta0": (0, [P, 1]), "wv0": (0, [P, D]), "start0": (0, [P, D]),
        "lin0": (0, [P, D]), "bv0": (0, [P, D]), "blin0": (0, [P, D]), "gate0": (0, [P, E]),
        "left0": (0, [P, E * LR]), "right0": (0, [E * LR, D]),
        "q1": (1, [P, NG * P]), "k1": (1, [P, NG * P]), "v1": (1, [P, D]), "out1": (1, [P, D]),
        "bq1": (1, [P, NG]), "bk1": (1, [P, NG]), "bv1": (1, [P, D]), "bout1": (1, [P, D]),
        "gate1": (1, [P, E]), "up1": (1, [P, E * HID]), "down1": (1, [P, E * HC, D]),
        "bup1": (1, [P, E * HC]), "bdown1": (1, [E, D]),
        "q2": (2, [P, NG * P]), "k2": (2, [P, NG * P]), "v2w": (2, [P, D]), "f2": (2, [P, NH]), "bf2": (2, [P, NH]),
        "out2": (2, [P, WAYS, D]), "one_rows2": (2, [P, WAYS]),
        "tri2": (2, [P, P]), "tri_back2": (2, [P, P]), "ones2": (2, [P, P]),
        "rot2": (2, [P, 4, NC * LD]), "scale_rows2": (2, [P, DEPTH, 4, LD]),
        "qkv2": (2, [P, DEPTH, 3 * INNER]), "wo2": (2, [P, DEPTH, IB, D]), "ln2": (2, [P, DEPTH, 2]),
        "up2": (2, [P, DEPTH, 2, FC * P]), "bup2": (2, [P, DEPTH, 2, FC]), "down2": (2, [P, DEPTH, FC, D]),
        "bdown2": (2, [P, DEPTH, D]),
        "gate3": (3, [P, E]), "q3": (3, [P, FB * P]), "k3": (3, [P, FB * P]), "v3": (3, [P, FB * P]),
        "bq3": (3, [P, FB]), "bk3": (3, [P, FB]), "bv3": (3, [P, FB]), "out3": (3, [P, FB, D]), "bout3": (3, [P, D]),
        "egate3": (3, [P, E * HID]), "eup3": (3, [P, E * HID]), "edown3": (3, [P, E * HC, D]),
    }
    return t


def program(nc, dram, x_in, out, scratch, B):
    g = Names()
    lists = load_lists(B)
    held = {}

    def hold(ctx, layer):
        for n, (of, shape) in lists.items():
            if of == layer and n != "masks":
                held[n] = ctx.enter_context(nc.sbuf_tensor("w_" + n, shape, FP32))

    with ExitStack() as ctx:
        hold(ctx, 0)
        hold(ctx, 3)
        only2 = ctx.enter_context(ExitStack())
        g.x_all = ctx.enter_context(nc.sbuf_tensor("x_all", [P, NC * B, D], FP32))
        g.ident16 = ctx.enter_context(nc.sbuf_tensor("ident16", [P, P], BF16))
        masks16 = ctx.enter_context(nc.sbuf_tensor("masks16", [P, 3, AW], BF16))
        hold(only2, 2)
        only1 = only2.enter_context(ExitStack())
        hold(only1, 1)
        g.w = held
        g.ident, g.one_row, g.iota, g.alibi = held["ident"], held["one_row"], held["iota"], held["alibi"]
        g.neg_half = held["neg_half"]
        g.mask_causal, g.mask_anti, g.mask_band = masks16[:, 0, :], masks16[:, 1, :], masks16[:, 2, :]
        g.bank = [ctx.enter_context(nc.psum_tensor(f"bank{i}", [P, 512], FP32)) for i in range(8)]
        loaded = [ctx.enter_context(nc.semaphore(f"loaded{i}")) for i in range(4)]
        x_loaded = ctx.enter_context(nc.semaphore("x_loaded"))
        consts_ready = ctx.enter_context(nc.semaphore("consts_ready"))
        n_loads = [0] * 4
        for n, (layer, _) in lists.items():
            n_loads[layer] += 16

        def wait_layer(eng, layer):
            eng.wait_ge(loaded[layer], n_loads[layer])

        def wait_consts(eng):
            eng.wait_ge(loaded[0], n_loads[0])
            eng.wait_ge(consts_ready, 1)

        g.wait_layer, g.wait_consts = wait_layer, wait_consts
        with ExitStack() as c0:
            masks32 = c0.enter_context(nc.sbuf_tensor("masks32", [P, 3, AW], FP32))
            block = c0.enter_context(nc.Block())

            def load(sp, layer):
                for n, (of, shape) in lists.items():
                    if of == layer:
                        dst = masks32 if n == "masks" else held[n]
                        sp.dma_start(dst.ap(), dram[n]).then_inc(loaded[layer], 16)

            def issue_loads(sp):
                for layer in (1, 2, 3):
                    if layer in PHASES:
                        load(sp, layer)

            g.issue_loads = issue_loads

            @block.sync
            def _(sp):
                load(sp, 0)
                if 0 in PHASES:
                    return
                issue_loads(sp)
                sp.dma_start(g.x_all[:, :, :], x_in.rearrange("b (c p) d -> p (b c) d", p=P)).then_inc(x_loaded, 16)

            @block.vector
            def _(dve):
                dve.wait_ge(loaded[0], n_loads[0])
                dve.tensor_copy(g.ident16[:, :], g.ident[:, :])
                dve.tensor_copy(masks16[:, :, :], masks32[:, :, :]).then_inc(consts_ready, 1)
                if 0 not in PHASES:
                    dve.wait_ge(x_loaded, 16)

        if 0 in PHASES:
            layer0(nc, g, B, x_in, scratch)
            with ExitStack() as c0:
                block = c0.enter_context(nc.Block())

                @block.sync
                def _(sp):
                    sp.dma_start(g.x_all[:, :, :], scratch.rearrange("b (c p) d -> p (b c) d", p=P)).then_inc(x_loaded, 16)
                    sp.wait_ge(x_loaded, 16)
        if 1 in PHASES:
            layer1(nc, g, B)
        only1.close()
        if 2 in PHASES:
            layer2(nc, g, B)
        only2.close()
        if 3 in PHASES:
            layer3(nc, g, B, out)
            return
        with ExitStack() as c0:
            stored = c0.enter_context(nc.semaphore("stored"))
            block = c0.enter_context(nc.Block())

            @block.sync
            def _(sp):
                sp.dma_start(out.rearrange("b (c p) d -> p (b c) d", p=P), g.x_all[:, :, :]).then_inc(stored, 16)
                sp.wait_ge(stored, 16)


def slot_columns(wt):
    out = np.zeros((wt.shape[0], NH, SLOT), wt.dtype)
    out[:, :, :DH] = wt.reshape(wt.shape[0], NH, DH)
    return out.reshape(wt.shape[0], NG * P)


def columns(v, n=P):
    return np.ascontiguousarray(v.reshape(-1, n).T)


def rows(v):
    return np.ascontiguousarray(np.broadcast_to(v, (P, v.shape[-1])))


def shape_constants():
    c = {}
    c["ident"] = np.eye(P, dtype=np.float32)
    p = np.arange(P)
    c["one_row"] = (p % SLOT == DH).astype(np.float32)[:, None]
    c["iota"] = np.broadcast_to(np.arange(E, dtype=np.float32), (P, E)).copy()
    c["neg_half"] = np.full((P, 32), -0.5, np.float32)
    early, late = (p % TS)[None, :] < (p % TS)[:, None], (p % TS)[None, :] > (p % TS)[:, None]
    c["before0"], c["after0"] = early.astype(np.float32), late.astype(np.float32)
    start = 2.0 ** (-2.0 ** (-(math.log2(NH) - 3)))
    slopes = np.array([start * start ** i for i in range(NH)], np.float32)
    al = np.zeros((NG, GH, SLOT, S), np.float32)
    al[:, :, DH, :] = slopes.reshape(NG, GH)[:, :, None] * np.arange(S, dtype=np.float32)
    c["alibi"] = al.reshape(NG, P, S).transpose(1, 0, 2).copy()
    q, k = np.arange(P)[:, None], np.arange(P)[None, :]
    c["one_rows2"] = np.stack([(p % SLOT == DH + y) for y in range(WAYS)], 1).astype(np.float32)
    c["tri2"] = (q <= k).astype(np.float32)
    c["tri_back2"] = (q >= k).astype(np.float32)
    c["ones2"] = np.ones((P, P), np.float32)
    half = np.arange(0, LD, 2, dtype=np.float64)
    t = np.arange(S, dtype=np.float64)
    inv = (1.0 / 10000.0 ** (half / LD)).astype(np.float32).astype(np.float64)
    angle = (t[:, None] * inv[None, :]).astype(np.float32).astype(np.float64)
    grow = ((half + 0.4 * LD) / (1.4 * LD))[None, :] ** ((t - S // 2) / float(WINDOW // 2))[:, None]
    cos, sin = (np.concatenate([y, y], 1) for y in (np.cos(angle), np.sin(angle)))
    grow = np.concatenate([grow, grow], 1)
    sign = np.where(np.arange(LD) < LHALF, -1.0, 1.0)[None, :]
    rot = np.stack([8 * cos * grow, 8 * sign * sin * grow, cos / grow, sign * sin / grow]).astype(np.float32)
    c["rot2"] = rot.reshape(4, NC, P, LD).transpose(2, 0, 1, 3).reshape(P, 4, NC * LD)
    no = np.float32(NEG)
    causal = np.where(k <= q, 0, no)
    anti = np.where(k >= q, 0, no)
    zero = np.zeros((P, P))
    full = np.full((P, P), no)
    far = np.where(q + P - k <= 64, 0, no)
    near = np.where((k <= q) & (q - k <= 64), 0, no)
    c["masks"] = np.stack([np.concatenate(x, 1) for x in
                           ((causal, zero, causal), (anti, zero, anti), (near, far, near))], 1).astype(np.float32)
    return c


def kernel(**a):
    import concourse.bacc as _bacc
    from concourse.bass_utils import run_bass_kernel_spmd as _run

    a = {n: np.asarray(v) for n, v in a.items()}
    x = np.ascontiguousarray(a["L0_attn_x"])
    B = x.shape[0]
    arrays = shape_constants()
    w_kv, b_kv = a["L0_attn_Wkv"], a["L0_attn_bkv"]
    arrays.update(
        eta0=rows(a["L0_attn_eta"].reshape(1)), wv0=w_kv[D:].T, start0=a["L0_attn_W0"].T, lin0=a["L0_ffn_W_lin"].T,
        bv0=rows(b_kv[D:]), blin0=rows(a["L0_ffn_b_lin"]), gate0=a["L0_ffn_gate_w"].T,
        left0=a["L0_ffn_left"].transpose(1, 0, 2).reshape(D, E * LR), right0=a["L0_ffn_right"].reshape(E * LR, D),
    )
    w_in, b_in = a["L1_attn_w_in"], a["L1_attn_b_in"]
    arrays.update(
        q1=slot_columns(w_in[:, :D]), k1=slot_columns(w_in[:, D:2 * D]), v1=w_in[:, 2 * D:], out1=a["L1_attn_w_out"],
        bq1=columns(slot_columns(b_in[None, :D])[0]), bk1=columns(slot_columns(b_in[None, D:2 * D])[0]),
        bv1=rows(b_in[2 * D:]), bout1=rows(a["L1_attn_b_out"]), gate1=a["L1_ffn_gate_w"].T,
        up1=a["L1_ffn_w1"].transpose(2, 0, 1).reshape(D, E * HID),
        down1=a["L1_ffn_w2"].transpose(0, 2, 1).reshape(E * HC, P, D).transpose(1, 0, 2),
        bup1=columns(a["L1_ffn_b1"].reshape(-1)), bdown1=a["L1_ffn_b2"],
    )
    qs, ks = a["L2_ffn_q_scale"], a["L2_ffn_k_scale"]

    def swapped(t):
        return np.concatenate([t[:, LHALF:], t[:, :LHALF]], 1)

    def ffn_blocks(t, axis):
        pad = [(0, 0)] * t.ndim
        pad[axis] = (0, FC * P - FFN)
        return np.pad(t, pad)

    w1, b1 = a["L2_ffn_w1"], a["L2_ffn_b1"]
    arrays.update(
        q2=slot_columns(a["L2_attn_Wq"].T), k2=slot_columns(a["L2_attn_Wk"].T), v2w=a["L2_attn_Wv"].T,
        f2=a["L2_attn_Wf"].T, bf2=rows(a["L2_attn_bf"]),
        out2=a["L2_attn_Wo"].T.reshape(WAYS, P, D).transpose(1, 0, 2),
        scale_rows2=rows(np.stack([qs, swapped(qs), ks, swapped(ks)], 1).reshape(-1)),
        qkv2=a["L2_ffn_wqkv"].transpose(1, 0, 2), wo2=a["L2_ffn_wo"].reshape(DEPTH, IB, P, D).transpose(2, 0, 1, 3),
        ln2=np.stack([a["L2_ffn_ln_g"], a["L2_ffn_ln_b"]], 1).transpose(2, 0, 1),
        up2=np.stack([ffn_blocks(w1[:, :, :FFN], 2), ffn_blocks(w1[:, :, FFN:], 2)], 1).transpose(2, 0, 1, 3),
        bup2=np.stack([ffn_blocks(b1[:, :FFN], 1), ffn_blocks(b1[:, FFN:], 1)], 1)
        .reshape(DEPTH, 2, FC, P).transpose(3, 0, 1, 2),
        down2=ffn_blocks(a["L2_ffn_w2"], 1).reshape(DEPTH, FC, P, D).transpose(2, 0, 1, 3),
        bdown2=rows(a["L2_ffn_b2"].reshape(-1)),
    )
    arrays.update(
        gate3=a["L3_ffn_router_w"].T,
        q3=a["L3_attn_wq"].reshape(D, FB * P), k3=a["L3_attn_wk"].reshape(D, FB * P),
        v3=a["L3_attn_wv"].reshape(D, FB * P),
        bq3=columns(a["L3_attn_bq"].reshape(-1)), bk3=columns(a["L3_attn_bk"].reshape(-1)),
        bv3=columns(a["L3_attn_bv"].reshape(-1)),
        out3=a["L3_attn_wo"].reshape(FB, P, D).transpose(1, 0, 2), bout3=rows(a["L3_attn_bo"]),
        egate3=a["L3_ffn_gate_w"].transpose(2, 0, 1).reshape(D, E * HID),
        eup3=a["L3_ffn_up_w"].transpose(2, 0, 1).reshape(D, E * HID),
        edown3=a["L3_ffn_down_w"].transpose(0, 2, 1).reshape(E * HC, P, D).transpose(1, 0, 2),
    )
    nc = _bacc.Bacc("TRN2", target_bir_lowering=False, num_devices=1)
    feed, dram = {}, {}

    def given(name, arr):
        arr = np.ascontiguousarray(arr)
        feed[f"in_{name}"] = arr
        return nc.dram_tensor(f"in_{name}", arr.shape, mybir.dt.from_np(arr.dtype), kind="ExternalInput").ap()

    for name, (_, shape) in load_lists(B).items():
        dram[name] = given(name, arrays[name].reshape(shape))
    x_in = given("x", x)
    scratch = nc.dram_tensor("scratch", x.shape, FP32, kind="Internal").ap()
    out = nc.dram_tensor("out_x", x.shape, FP32, kind="ExternalOutput").ap()
    program(nc, dram, x_in, out, scratch, B)
    res = _run(nc, [feed], core_ids=[0])
    return res.results[0]["out_x"]
```

```python
import math
from contextlib import ExitStack

import numpy as np
import concourse.bass as bass
from concourse import mybir

FP32 = mybir.dt.float32
BF16 = mybir.dt.bfloat16
U32 = mybir.dt.uint32
ALU = mybir.AluOpType
ACT = mybir.ActivationFunctionType
AX = mybir.AxisListType

PHASES = (0, 1, 2, 3)

P = 128
D = 128
S = 256
NC = S // P
NH = 16
DH = D // NH
SLOT = 32
GH = P // SLOT
NG = NH // GH
E = 8
HID = 512
HC = HID // P
LN_EPS = 1e-5
AW = 3 * P
NEG = -1e30


class Chain:

    def __init__(self, eng, sem, rnd, n_per):
        self.eng, self.sem, self.rnd, self.n_per, self.n = eng, sem, rnd, n_per, 0

    def mark(self, ins):
        ins.then_inc(self.sem, 1)
        self.n += 1
        return self.n

    def wait(self, n):
        self.eng.wait_ge(self.sem, self.rnd * self.n_per + n)

    def hold(self, n, pad):
        self.wait(n)
        self.eng.memset(pad, 0.0)

    def __call__(self, ins):
        self.wait(self.mark(ins))

    def done(self):
        assert self.n == self.n_per, f"chain: {self.n} steps, declared {self.n_per}"


def pool_hold(pool, g, pad):
    pool.tensor_tensor(pad, g.neg_half[0:1, 0:1], g.neg_half[0:1, 0:1], ALU.mult)


class Banks:

    def __init__(self, banks, full, taken, uses):
        self.b, self.full, self.taken = banks, full, taken
        self.n, self.per = len(banks), uses // len(banks)
        assert uses % len(banks) == 0

    def open(self, pe):
        for t in self.taken:
            pe.sem_inc(t, 1)

    def fill(self, pe, rnd, k, after=()):
        for bank in range(self.n):
            js = [j for j in after if j % self.n == bank]
            if js and not (bank == k % self.n and max(js) <= k - self.n):
                self.wait_taken(pe, rnd, max(js))
        pe.wait_ge(self.taken[k % self.n], rnd * self.per + k // self.n + 1)
        return self.b[k % self.n]

    def filled(self, ins, k):
        ins.then_inc(self.full[k % self.n], 1)

    def read(self, eng, rnd, k):
        eng.wait_ge(self.full[k % self.n], rnd * self.per + k // self.n + 1)
        return self.b[k % self.n]

    def took(self, ins, k):
        ins.then_inc(self.taken[k % self.n], 1)

    def wait_taken(self, eng, rnd, k):
        eng.wait_ge(self.taken[k % self.n], rnd * self.per + k // self.n + 2)


class Names:
    pass


def chunks(ap, n=NC):
    return ap.rearrange("p (c d) -> p c d", c=n)


def over_chunks(row, n=NC):
    return row.unsqueeze(1).to_broadcast([P, n, row.shape[-1]])


def stat_buffers(sb, n):
    t = Names()
    t.stats = sb("stats", [P, n, 6])
    t.mv = sb("mean_var", [P, n, 2])
    t.pad = sb("norm_pad", [1, 1])
    t.var = sb("var", [P, n])
    t.rstd = sb("rstd", [P, n])
    return t


def norm_stats(dve, chain, x, t, n):
    for c in range(n):
        m = chain.mark(dve.bn_stats(t.stats[:, c, :], x[:, c, :]))
    chain.hold(m, t.pad[:, :])
    for c in range(n):
        m = chain.mark(dve.bn_aggr(t.mv[:, c, :], t.stats[:, c, :]))
    chain.wait(m)
    return dve.tensor_scalar(t.var[:, :], t.mv[:, :, 1], LN_EPS, None, ALU.add)


def norm_rstd(pool, g, t, n):
    return pool.tensor_tensor(t.rstd[:, :], t.var[:, :], g.neg_half[:, 0:n], ALU.pow)


def norm_apply(dve, x, xn, t, n):
    for c in range(n):
        last = dve.tensor_scalar(xn[:, c, :], x[:, c, :], t.mv[:, c, 0:1], t.rstd[:, c:c + 1],
                                 ALU.subtract, ALU.mult)
    return last


def router_buffers(sb, n):
    r = Names()
    r.pad = sb("r_pad", [1, 1])
    r.lg = sb("r_logits", [P, n, E])
    r.mx = sb("r_best", [P, n, 8])
    r.ix = sb("r_index", [P, n, 8], U32)
    r.ixf = sb("r_indexf", [P, n, 2])
    r.ls = sb("r_shifted", [P, n, E])
    r.ex = sb("r_exp", [P, n, E])
    r.mk = sb("r_first", [P, n, E])
    r.mk2 = sb("r_chosen", [P, n, E])
    r.cu = sb("r_kept", [P, n, E])
    r.den = sb("r_sum", [P, n])
    r.rden = sb("r_rsum", [P, n])
    r.comb = sb("r_comb", [P, n, E])
    return r


def router_rank(dve, chain, r, logits, n):
    chain.hold(chain.mark(dve.tensor_copy(r.lg[:, :, :], logits)), r.pad[:, :])
    for c in range(n):
        m = chain.mark(dve.max(r.mx[:, c, :], r.lg[:, c, :]))
    chain.hold(m, r.pad[:, :])
    for c in range(n):
        m = chain.mark(dve.max_index(r.ix[:, c, :], r.mx[:, c, :], r.lg[:, c, :]))
    chain.wait(m)
    chain(dve.tensor_copy(r.ixf[:, :, :], r.ix[:, :, 0:2]))
    return dve.tensor_tensor(r.ls[:, :, :], r.lg[:, :, :], r.mx[:, :, 0:1].to_broadcast([P, n, E]), ALU.subtract)


def router_mix(dve, chain, r, iota, n, over_all, scale=1.0):
    for c in range(n):
        m = chain.mark(dve.tensor_scalar(r.mk[:, c, :], iota[:, 0:E], r.ixf[:, c, 0:1], None, ALU.is_equal))
    chain.wait(m)
    for c in range(n):
        m = chain.mark(dve.scalar_tensor_tensor(out=r.mk2[:, c, :], in0=iota[:, 0:E], scalar=r.ixf[:, c, 1:2],
                                                in1=r.mk[:, c, :], op0=ALU.is_equal, op1=ALU.add))
    chain.wait(m)
    chain(dve.tensor_tensor(r.cu[:, :, :], r.mk2[:, :, :], r.ex[:, :, :], ALU.mult))
    chain(dve.reduce_sum(r.den[:, :], (r.ex if over_all else r.cu)[:, :, :], AX.X))
    chain(dve.reciprocal(r.rden[:, :], r.den[:, :]))
    return dve.scalar_tensor_tensor(out=r.comb[:, :, :], in0=r.cu[:, :, :], scalar=scale,
                                    in1=r.rden[:, :].unsqueeze(2).to_broadcast([P, n, E]),
                                    op0=ALU.mult, op1=ALU.mult)


ROUTER_STEPS = lambda n: (1 + 2 * n + 1) + (2 * n + 3)
NORM_STEPS = lambda n: 2 * n

FORWARD = dict(split=P, parts=((0, 0, 1), (1, 0, 2)))
BACKWARD = dict(split=2 * P, parts=((0, 0, 2), (1, 1, 1)))


def pe_scores(pe, g, bank, q, k, mask, way):
    pe.matmul(bank[:, 0:AW], g.ident16[:, :], mask[:, :], start=True, stop=False, skip_group_check=True)
    at = 0
    for c, k0, n in way["parts"]:
        last = pe.matmul(bank[:, at:at + n * P], q[:, c * P:(c + 1) * P], k[:, k0 * P:(k0 + n) * P],
                         start=False, stop=(c == 1), skip_group_check=True)
        at += n * P
    return last


def pe_transpose3(pe, g, bank, probs):
    for j in range(3):
        last = pe.transpose(bank[:, j * P:(j + 1) * P], probs[:, j * P:(j + 1) * P], g.ident[:, :])
    return last


def pe_values(pe, outs, probsT, v, way):
    j = 0
    for c, k0, n in way["parts"]:
        for i in range(n):
            last = pe.matmul(outs[c], probsT[:, j * P:(j + 1) * P], v[:, k0 + i, :],
                             start=(i == 0), stop=(i == n - 1))
            j += 1
    return last


def dve_negmax(dve, bank, negmax, way):
    s = way["split"]
    dve.tensor_reduce(negmax[:, 0:1], bank[:, 0:s], AX.X, ALU.max, negate=True)
    return dve.tensor_reduce(negmax[:, 1:2], bank[:, s:AW], AX.X, ALU.max, negate=True)


def act_probs(act, bank, negmax, probs, sums, way):
    s = way["split"]
    act.activation(probs[:, 0:s], bank[:, 0:s], ACT.Exp, bias=negmax[:, 0:1], accum_out=sums[0])
    return act.activation(probs[:, s:AW], bank[:, s:AW], ACT.Exp, bias=negmax[:, 1:2], accum_out=sums[1])


TS = 8
RC = 4
LR = 4


def layer0(nc, g, B, x_in, scratch):
    assert B * TS == P
    w = g.w
    rounds = S // TS // RC
    with ExitStack() as ctx:
        def sb(name, shape, dt=FP32):
            return ctx.enter_context(nc.sbuf_tensor("l0_" + name, shape, dt))

        def sem(name):
            return ctx.enter_context(nc.semaphore("l0_" + name))

        x0 = g.x_all
        xs = sb("xs", [P, RC, D])
        xn = sb("xn", [P, RC, D])
        xnT = sb("xnT", [P, RC, P])
        st = stat_buffers(sb, RC)
        r = router_buffers(sb, RC)
        neg_c = sb("neg_c", [P, 1])
        before = sb("before", [P, P])
        after = sb("after", [P, P])
        N1, N1T, N2, N2T, N4 = (sb(n, [P, RC, P]) for n in ("n1", "n1t", "n2", "n2t", "n4"))
        S1, S2, AT = (sb(n, [P, RC, P]) for n in ("s1", "s2", "at"))
        w_sum = sb("w_sum", [P, D])
        b_sum = sb("b_sum", [P, D])
        U = sb("U", [P, D])
        low = sb("low", [P, RC, E * LR])
        lowT = sb("lowT", [E * LR, RC, P])
        rest = sb("rest", [P, RC, D])
        rs = sb("rs", [P, 2, D])
        err = sb("err", [P, 2, D])
        y = sb("y", [P, RC, D])

        A_XNT, A_GRAM, A_LOGIT, A_LOWT, A_REST, A_N2, A_N2T, A_N4, A_S2, A_AT = range(10)
        G = Banks(g.bank[0:5], [sem(f"g_full{i}") for i in range(5)], [sem(f"g_taken{i}") for i in range(5)], 10)
        bank_r, bank_e, bank_u = g.bank[5:8]

        x_loaded = sem("x_loaded")
        setup_done = sem("setup_done")
        var_ready = sem("var_ready")
        rstd_ready = sem("rstd_ready")
        xn_ready = sem("xn_ready")
        gate_exp = sem("gate_exp")
        low_ready = sem("low_ready")
        s1_ready = sem("s1_ready")
        r_full = sem("r_full")
        rs_ready = sem("rs_ready")
        e_full = sem("e_full")
        err_ready = sem("err_ready")
        u_full = sem("u_full")
        u_ready = sem("u_ready")
        y_ready = sem("y_ready")
        stored = sem("stored")
        dve_chain = sem("dve_chain")
        n_chain = 1 + NORM_STEPS(RC) + ROUTER_STEPS(RC) + 1 + 2 + RC

        block = ctx.enter_context(nc.Block())

        @block.sync
        def _(sp):
            for b in range(B):
                sp.dma_start(x0[b * TS:(b + 1) * TS, :, :],
                             x_in[b].rearrange("(c t) d -> t c d", t=TS)).then_inc(x_loaded, 16)
            g.issue_loads(sp)
            sp.sem_inc(stored, 16 * B)
            with sp.Fori(0, rounds) as rd:
                sp.wait_ge(y_ready, rd + 1)
                for b in range(B):
                    sp.dma_start(scratch[b, bass.ds(rd * (RC * TS), RC * TS), :].rearrange("(c t) d -> t c d", t=TS),
                                 y[b * TS:(b + 1) * TS, :, :]).then_inc(stored, 16)
            sp.wait_ge(stored, 16 * B * (rounds + 1))

        @block.tensor
        def _(pe):
            g.wait_consts(pe)
            pe.wait_ge(setup_done, 1)
            G.open(pe)
            with pe.Fori(0, rounds) as rd:
                def each(k, lhs, rhs, width=P):
                    b = G.fill(pe, rd, k)
                    for j in range(RC):
                        last = pe.matmul(b[:, j * width:(j + 1) * width], lhs(j), rhs(j), start=True, stop=True)
                    G.filled(last, k)

                pe.wait_ge(xn_ready, rd + 1)
                b = G.fill(pe, rd, A_XNT)
                for j in range(RC):
                    last = pe.transpose(b[:, j * P:(j + 1) * P], xn[:, j, :], g.ident[:, :])
                G.filled(last, A_XNT)
                G.wait_taken(pe, rd, A_XNT)
                each(A_GRAM, lambda j: xnT[:, j, :], lambda j: xnT[:, j, :])
                b = G.fill(pe, rd, A_LOGIT)
                for j in range(RC):
                    pe.matmul(b[:, j * E:(j + 1) * E], xnT[:, j, :], w["gate0"][:, :], start=True, stop=True)
                    last = pe.matmul(b[:, RC * E + j * E * LR:RC * E + (j + 1) * E * LR], xnT[:, j, :],
                                     w["left0"][:, :], start=True, stop=True)
                G.filled(last, A_LOGIT)
                pe.wait_ge(low_ready, rd + 1)
                b = G.fill(pe, rd, A_LOWT)
                for j in range(RC):
                    last = pe.transpose(b[0:E * LR, j * P:(j + 1) * P], low[:, j, :], g.ident[:, :])
                G.filled(last, A_LOWT)
                G.wait_taken(pe, rd, A_LOWT)
                b = G.fill(pe, rd, A_REST)
                for j in range(RC):
                    pe.matmul(b[:, j * P:(j + 1) * P], xnT[:, j, :], w_sum[:, :], start=True, stop=False)
                    last = pe.matmul(b[:, j * P:(j + 1) * P], lowT[:, j, :], w["right0"][:, :], start=False, stop=True)
                G.filled(last, A_REST)
                G.wait_taken(pe, rd, A_GRAM)
                each(A_N2, lambda j: N1T[:, j, :], lambda j: N1[:, j, :])
                each(A_N2T, lambda j: N1[:, j, :], lambda j: N1T[:, j, :])
                G.wait_taken(pe, rd, A_N2)
                G.wait_taken(pe, rd, A_N2T)
                each(A_N4, lambda j: N2T[:, j, :], lambda j: N2[:, j, :])
                pe.wait_ge(s1_ready, rd + 1)
                each(A_S2, lambda j: N2[:, j, :], lambda j: S1[:, j, :])
                G.wait_taken(pe, rd, A_N4)
                G.wait_taken(pe, rd, A_S2)
                each(A_AT, lambda j: N4[:, j, :], lambda j: S2[:, j, :])
                G.wait_taken(pe, rd, A_AT)
                for j in range(RC):
                    pe.wait_ge(u_ready, rd * RC + j + 1)
                    pe.matmul(bank_r[:, 0:D], xnT[:, j, :], U[:, :], start=True, stop=True).then_inc(r_full, 1)
                    pe.wait_ge(rs_ready, rd * RC + j + 1)
                    pe.matmul(bank_e[:, 0:D], AT[:, j, :], rs[:, j % 2, :], start=True, stop=True).then_inc(e_full, 1)
                    pe.wait_ge(err_ready, rd * RC + j + 1)
                    pe.matmul(bank_u[:, 0:D], xn[:, j, :], err[:, j % 2, :], start=True, stop=True).then_inc(u_full, 1)

        @block.gpsimd
        def _(pool):
            g.wait_layer(pool, 0)
            with pool.Fori(0, rounds) as rd:
                pool.wait_ge(var_ready, rd + 1)
                norm_rstd(pool, g, st, RC).then_inc(rstd_ready, 1)

        @block.scalar
        def _(act):
            with act.Fori(0, rounds) as rd:
                G.wait_taken(act, rd, A_LOGIT)
                act.activation(r.ex[:, :, :], r.ls[:, :, :], ACT.Exp).then_inc(gate_exp, 1)
                b = G.read(act, rd, A_N2T)
                G.took(act.activation(N2T[:, :, :], chunks(b[:, :], RC), ACT.Copy), A_N2T)
                b = G.read(act, rd, A_N4)
                G.took(act.activation(N4[:, :, :], chunks(b[:, :], RC), ACT.Copy), A_N4)

        @block.vector
        def _(dve):
            g.wait_consts(dve)
            dve.tensor_scalar(neg_c[:, :], w["eta0"][:, :], -2.0 / (B * D), None, ALU.mult).then_inc(setup_done, 1)
            dve.wait_ge(setup_done, 1)
            dve.tensor_scalar(before[:, :], w["before0"][:, :], neg_c[:, 0:1], None, ALU.mult)
            dve.tensor_scalar(after[:, :], w["after0"][:, :], neg_c[:, 0:1], None, ALU.mult)
            dve.tensor_tensor(w_sum[:, :], w["wv0"][:, :], w["lin0"][:, :], ALU.add)
            dve.tensor_tensor(b_sum[:, :], w["bv0"][:, :], w["blin0"][:, :], ALU.add)
            dve.tensor_tensor(U[:, :], w["start0"][:, :], w["wv0"][:, :], ALU.subtract).then_inc(u_ready, 1)
            dve.wait_ge(u_ready, 1)
            dve.wait_ge(x_loaded, 16 * B)
            with dve.Fori(0, rounds) as rd:
                ch = Chain(dve, dve_chain, rd, n_chain)
                ch(dve.tensor_copy(xs[:, :, :], x0[:, bass.ds(rd * RC, RC), :]))
                norm_stats(dve, ch, xs, st, RC).then_inc(var_ready, 1)
                dve.wait_ge(rstd_ready, rd + 1)
                norm_apply(dve, xs, xn, st, RC).then_inc(xn_ready, 1)
                b = G.read(dve, rd, A_XNT)
                G.took(dve.tensor_copy(xnT[:, :, :], chunks(b[:, :], RC)), A_XNT)
                b = G.read(dve, rd, A_GRAM)
                dve.tensor_tensor(N1T[:, :, :], chunks(b[:, :], RC), over_chunks(after[:, :], RC), ALU.mult)
                G.took(dve.tensor_tensor(N1[:, :, :], chunks(b[:, :], RC), over_chunks(before[:, :], RC), ALU.mult), A_GRAM)
                b = G.read(dve, rd, A_LOGIT)
                ch(router_rank(dve, ch, r, b[:, 0:RC * E].rearrange("p (c e) -> p c e", e=E), RC))
                G.took(dve.tensor_copy(low[:, :, :], b[:, RC * E:RC * E * (1 + LR)].rearrange("p (c k) -> p c k", c=RC)),
                       A_LOGIT)
                G.wait_taken(dve, rd, A_GRAM)
                dve.tensor_tensor(S1[:, :, :], N1T[:, :, :], over_chunks(g.ident[:, :], RC), ALU.add).then_inc(s1_ready, 1)
                dve.wait_ge(gate_exp, rd + 1)
                ch(router_mix(dve, ch, r, g.iota, RC, True))
                dve.tensor_tensor(low[:, :, :].rearrange("p c (e k) -> p (c e) k", k=LR),
                                  low[:, :, :].rearrange("p c (e k) -> p (c e) k", k=LR),
                                  r.comb[:, :, :].rearrange("p c e -> p (c e)").unsqueeze(2).to_broadcast([P, RC * E, LR]),
                                  ALU.mult).then_inc(low_ready, 1)
                b = G.read(dve, rd, A_LOWT)
                G.took(dve.tensor_copy(lowT[:, :, :], chunks(b[0:E * LR, :], RC)), A_LOWT)
                b = G.read(dve, rd, A_N2)
                G.took(dve.tensor_copy(N2[:, :, :], chunks(b[:, :], RC)), A_N2)
                b = G.read(dve, rd, A_REST)
                G.took(dve.tensor_tensor(rest[:, :, :], chunks(b[:, :], RC), over_chunks(b_sum[:, :], RC), ALU.add), A_REST)
                b = G.read(dve, rd, A_S2)
                G.took(dve.tensor_tensor(S2[:, :, :], chunks(b[:, :], RC), S1[:, :, :], ALU.add), A_S2)
                G.wait_taken(dve, rd, A_S2)
                ch(dve.tensor_tensor(rest[:, :, :], rest[:, :, :], xs[:, :, :], ALU.add))
                b = G.read(dve, rd, A_AT)
                G.took(dve.tensor_tensor(AT[:, :, :], chunks(b[:, :], RC), S2[:, :, :], ALU.add), A_AT)
                for j in range(RC):
                    dve.wait_ge(r_full, rd * RC + j + 1)
                    dve.tensor_tensor(rs[:, j % 2, :], bank_r[:, 0:D], w["bv0"][:, :], ALU.subtract).then_inc(rs_ready, 1)
                    dve.wait_ge(e_full, rd * RC + j + 1)
                    dve.tensor_copy(err[:, j % 2, :], bank_e[:, 0:D]).then_inc(err_ready, 1)
                    if j == 0:
                        dve.wait_ge(stored, (rd + 1) * (16 * B))
                    dve.wait_ge(err_ready, rd * RC + j + 1)
                    ch.mark(dve.tensor_tensor(y[:, j, :], rest[:, j, :], err[:, j % 2, :], ALU.add))
                    dve.wait_ge(u_full, rd * RC + j + 1)
                    dve.wait_ge(u_ready, rd * RC + j + 1)
                    dve.scalar_tensor_tensor(out=U[:, :], in0=bank_u[:, 0:D], scalar=neg_c[:, 0:1], in1=U[:, :],
                                             op0=ALU.mult, op1=ALU.add).then_inc(u_ready, 1)
                ch.wait(ch.n)
                dve.memset(st.pad[:, :], 0.0).then_inc(y_ready, 1)
                ch.done()


def layer1(nc, g, B):
    w = g.w
    with ExitStack() as ctx:
        def sb(name, shape, dt=FP32):
            return ctx.enter_context(nc.sbuf_tensor("l1_" + name, shape, dt))

        def sem(name):
            return ctx.enter_context(nc.semaphore("l1_" + name))

        xt = sb("xt", [P, NC, D])
        xn = sb("xn", [P, NC, D])
        xnT = sb("xnT", [P, S])
        st = stat_buffers(sb, NC)
        qT = sb("qT", [P, NG, S])
        kT = sb("kT", [P, NG, S])
        v = sb("v", [P, NC, D])
        negmax = sb("negmax", [P, 2, NC])
        probs = sb("probs", [P, 2, AW])
        probsT = sb("probsT", [P, 2, AW])
        rowsum = sb("rowsum", [P, NC, NH])
        rrow = sb("rrow", [P, NC, NH])
        on = sb("on", [P, NC, D])
        oT = sb("oT", [P, S])
        hT = sb("hT", [P, 2, HC, S])
        combT = sb("combT", [E, S])
        qbias = sb("qbias", [P, NG])
        kconst = sb("kconst", [P, NG, S])
        r = router_buffers(sb, NC)

        Sb, Tb, Ob, Db = g.bank[0:2], g.bank[2:4], g.bank[6], g.bank[7]
        G_XNT, G_LOGIT, G_Q, G_K, G_V, G_UP = 0, 1, 2, 4, 6, 7
        G_COMBT = G_UP + 2 * E
        G_OT, G_OUT = G_COMBT + 1, G_COMBT + 2
        G = Banks(g.bank[4:6], [sem("g_full0"), sem("g_full1")], [sem("g_taken0"), sem("g_taken1")], G_OUT + 1)

        setup_done = sem("setup_done")
        var_ready = sem("var_ready")
        rstd_ready = sem("rstd_ready")
        xn_ready = sem("xn_ready")
        gate_exp = sem("gate_exp")
        comb_ready = sem("comb_ready")
        scores_ready = sem("scores_ready")
        negmax_ready = sem("negmax_ready")
        probs_ready = sem("probs_ready")
        transposed = sem("transposed")
        probsT_ready = sem("probsT_ready")
        heads_summed = sem("heads_summed")
        on_ready = sem("on_ready")
        down_ready = sem("down_ready")
        down_used = sem("down_used")
        dve_chain = sem("dve_chain")
        n_chain = 1 + NORM_STEPS(NC) + ROUTER_STEPS(NC) + 2

        block = ctx.enter_context(nc.Block())

        @block.tensor
        def _(pe):
            g.wait_consts(pe)
            g.wait_layer(pe, 1)
            G.open(pe)
            pe.sem_inc(down_used, 1)
            with pe.Fori(0, B) as it:
                pe.wait_ge(xn_ready, it + 1)
                b = G.fill(pe, it, G_XNT)
                for c in range(NC):
                    last = pe.transpose(b[:, c * P:(c + 1) * P], xn[:, c, :], g.ident[:, :])
                G.filled(last, G_XNT)
                G.wait_taken(pe, it, G_XNT)
                b = G.fill(pe, it, G_LOGIT)
                for c in range(NC):
                    last = pe.matmul(b[:, c * E:(c + 1) * E], xnT[:, c * P:(c + 1) * P], w["gate1"][:, :],
                                     start=True, stop=True)
                G.filled(last, G_LOGIT)
                for k0, wt in ((G_Q, w["q1"]), (G_K, w["k1"])):
                    for u in range(2):
                        b = G.fill(pe, it, k0 + u)
                        for j in range(2):
                            gg = 2 * u + j
                            last = pe.matmul(b[:, j * S:(j + 1) * S], wt[:, gg * P:(gg + 1) * P], xnT[:, :],
                                             start=True, stop=True)
                        G.filled(last, k0 + u)
                b = G.fill(pe, it, G_V)
                for c in range(NC):
                    last = pe.matmul(b[:, c * P:(c + 1) * P], xnT[:, c * P:(c + 1) * P], w["v1"][:, :],
                                     start=True, stop=True)
                G.filled(last, G_V)
                G.wait_taken(pe, it, G_V - 1)
                G.wait_taken(pe, it, G_V)
                for s in range(NH + 2):
                    e = s // 2
                    if s < NH:
                        rows, gg = slice(SLOT * (s % GH), SLOT * (s % GH + 1)), s // GH
                        pe_scores(pe, g, Sb[s % 2], qT[rows, gg, :], kT[rows, gg, :], g.mask_causal,
                                  FORWARD).then_inc(scores_ready, 1)
                        if s % 2 == 0:
                            for u in range(2):
                                k = G_UP + 2 * e + u
                                b = G.fill(pe, it, k)
                                for j in range(2):
                                    h = (e * HC + 2 * u + j) * P
                                    last = pe.matmul(b[:, j * S:(j + 1) * S], w["up1"][:, h:h + P], xnT[:, :],
                                                     start=True, stop=True)
                                G.filled(last, k)
                        else:
                            G.wait_taken(pe, it, G_UP + 2 * e)
                            G.wait_taken(pe, it, G_UP + 2 * e + 1)
                            pe.wait_ge(down_used, it * E + e + 1)
                            for c in range(NC):
                                for j in range(HC):
                                    last = pe.matmul(Db[:, c * P:(c + 1) * P], hT[:, e % 2, j, c * P:(c + 1) * P],
                                                     w["down1"][:, e * HC + j, :], start=(j == 0), stop=(j == HC - 1))
                            last.then_inc(down_ready, 1)
                    if s >= 2:
                        h = s - 2
                        pe.wait_ge(probsT_ready, it * NH + h + 1)
                        last = pe_values(pe, [Ob[:, c * D + h * DH:c * D + (h + 1) * DH] for c in range(NC)],
                                         probsT[:, h % 2, :], v[:, :, h * DH:(h + 1) * DH], FORWARD)
                        if h == NH - 1:
                            last.then_inc(heads_summed, 1)
                    if 1 <= s <= NH:
                        h = s - 1
                        pe.wait_ge(probs_ready, it * NH + h + 1)
                        pe_transpose3(pe, g, Tb[h % 2], probs[:, h % 2, :]).then_inc(transposed, 1)
                pe.wait_ge(comb_ready, it + 1)
                b = G.fill(pe, it, G_COMBT)
                for c in range(NC):
                    last = pe.transpose(b[0:E, c * P:(c + 1) * P], r.comb[:, c, :], g.ident[:, :])
                G.filled(last, G_COMBT)
                pe.wait_ge(on_ready, it + 1)
                b = G.fill(pe, it, G_OT)
                for c in range(NC):
                    last = pe.transpose(b[:, c * P:(c + 1) * P], on[:, c, :], g.ident[:, :])
                G.filled(last, G_OT)
                G.wait_taken(pe, it, G_COMBT)
                G.wait_taken(pe, it, G_OT)
                b = G.fill(pe, it, G_OUT)
                for c in range(NC):
                    pe.matmul(b[:, c * P:(c + 1) * P], oT[:, c * P:(c + 1) * P], w["out1"][:, :], start=True, stop=False)
                    last = pe.matmul(b[:, c * P:(c + 1) * P], combT[:, c * P:(c + 1) * P], w["bdown1"][:, :],
                                     start=False, stop=True)
                G.filled(last, G_OUT)

        @block.gpsimd
        def _(pool):
            g.wait_layer(pool, 0)
            with pool.Fori(0, B) as it:
                pool.wait_ge(var_ready, it + 1)
                norm_rstd(pool, g, st, NC).then_inc(rstd_ready, 1)

        @block.scalar
        def _(act):
            g.wait_layer(act, 1)
            act.wait_ge(setup_done, 1)
            with act.Fori(0, B) as it:
                for u in range(2):
                    b = G.read(act, it, G_Q + u)
                    for j in range(2):
                        gg = 2 * u + j
                        last = act.activation(qT[:, gg, :], b[:, j * S:(j + 1) * S], ACT.Identity,
                                              bias=qbias[:, gg:gg + 1], scale=DH ** -0.5)
                    G.took(last, G_Q + u)
                G.wait_taken(act, it, G_LOGIT)
                act.activation(r.ex[:, :, :], r.ls[:, :, :], ACT.Exp).then_inc(gate_exp, 1)
                for s in range(NH):
                    act.wait_ge(negmax_ready, it * NH + s + 1)
                    act_probs(act, Sb[s % 2], negmax[:, s % 2, :], probs[:, s % 2, :],
                              [rowsum[:, c, s:s + 1] for c in range(NC)], FORWARD).then_inc(probs_ready, 1)
                    if s % 2 == 0:
                        e = s // 2
                        b = G.read(act, it, G_UP + 2 * e)
                        for j in range(2):
                            h = e * HC + j
                            last = act.activation(hT[:, e % 2, j, :], b[:, j * S:(j + 1) * S], ACT.Relu,
                                                  bias=w["bup1"][:, h:h + 1])
                        G.took(last, G_UP + 2 * e)

        @block.vector
        def _(dve):
            g.wait_consts(dve)
            g.wait_layer(dve, 1)
            for gg in range(NG):
                dve.tensor_scalar(qbias[:, gg:gg + 1], w["bq1"][:, gg:gg + 1], DH ** -0.5, g.one_row[:, 0:1],
                                  ALU.mult, ALU.add)
                last = dve.tensor_scalar(kconst[:, gg, :], g.alibi[:, gg, :], w["bk1"][:, gg:gg + 1], None, ALU.add)
            last.then_inc(setup_done, 1)
            dve.wait_ge(setup_done, 1)
            with dve.Fori(0, B) as it:
                ch = Chain(dve, dve_chain, it, n_chain)
                ch(dve.tensor_copy(xt[:, :, :], g.x_all[:, bass.ds(it * NC, NC), :]))
                norm_stats(dve, ch, xt, st, NC).then_inc(var_ready, 1)
                dve.wait_ge(rstd_ready, it + 1)
                norm_apply(dve, xt, xn, st, NC).then_inc(xn_ready, 1)
                b = G.read(dve, it, G_XNT)
                G.took(dve.tensor_copy(xnT[:, :], b[:, 0:S]), G_XNT)
                b = G.read(dve, it, G_LOGIT)
                G.took(router_rank(dve, ch, r, b[:, 0:NC * E].rearrange("p (c e) -> p c e", e=E), NC), G_LOGIT)
                for u in range(2):
                    b = G.read(dve, it, G_K + u)
                    G.took(dve.tensor_tensor(kT[:, 2 * u:2 * u + 2, :], chunks(b[:, :]),
                                             kconst[:, 2 * u:2 * u + 2, :], ALU.add), G_K + u)
                b = G.read(dve, it, G_V)
                G.took(dve.tensor_tensor(v[:, :, :], chunks(b[:, 0:S]), over_chunks(w["bv1"][:, :]), ALU.add), G_V)
                dve.wait_ge(gate_exp, it + 1)
                router_mix(dve, ch, r, g.iota, NC, False).then_inc(comb_ready, 1)
                dve.wait_ge(comb_ready, it + 1)
                for s in range(NH + 1):
                    e = s // 2
                    if s < NH:
                        dve.wait_ge(scores_ready, it * NH + s + 1)
                        dve_negmax(dve, Sb[s % 2], negmax[:, s % 2, :], FORWARD).then_inc(negmax_ready, 1)
                        if s % 2 == 0:
                            b = G.read(dve, it, G_UP + 2 * e + 1)
                            for j in range(2):
                                h = e * HC + 2 + j
                                last = dve.tensor_scalar(hT[:, e % 2, 2 + j, :], b[:, j * S:(j + 1) * S],
                                                         w["bup1"][:, h:h + 1], 0.0, ALU.add, ALU.max)
                            G.took(last, G_UP + 2 * e + 1)
                    if s >= 1:
                        dve.wait_ge(transposed, it * NH + s)
                        dve.tensor_copy(probsT[:, (s - 1) % 2, :], Tb[(s - 1) % 2][:, 0:AW]).then_inc(probsT_ready, 1)
                    if s < NH and s % 2 == 1:
                        dve.wait_ge(down_ready, it * E + e + 1)
                        if e:
                            dve.wait_ge(down_used, it * E + e + 1)
                        dve.scalar_tensor_tensor(out=xt[:, 0, :], in0=Db[:, 0:D], scalar=r.comb[:, 0, e:e + 1],
                                                 in1=xt[:, 0, :], op0=ALU.mult, op1=ALU.add)
                        dve.scalar_tensor_tensor(out=xt[:, 1, :], in0=Db[:, D:2 * D], scalar=r.comb[:, 1, e:e + 1],
                                                 in1=xt[:, 1, :], op0=ALU.mult, op1=ALU.add).then_inc(down_used, 1)
                b = G.read(dve, it, G_COMBT)
                G.took(dve.tensor_copy(combT[:, :], b[0:E, 0:S]), G_COMBT)
                dve.wait_ge(heads_summed, it + 1)
                ch(dve.reciprocal(rrow[:, :, :], rowsum[:, :, :]))
                for c in range(NC):
                    last = dve.tensor_tensor(on[:, c, :].rearrange("p (h d) -> p h d", h=NH),
                                             Ob[:, c * D:(c + 1) * D].rearrange("p (h d) -> p h d", h=NH),
                                             rrow[:, c, :].unsqueeze(2).to_broadcast([P, NH, DH]), ALU.mult)
                last.then_inc(on_ready, 1)
                b = G.read(dve, it, G_OT)
                G.took(dve.tensor_copy(oT[:, :], b[:, 0:S]), G_OT)
                b = G.read(dve, it, G_OUT)
                dve.wait_ge(down_used, it * E + E + 1)
                m = dve.tensor_tensor(xt[:, :, :], xt[:, :, :], chunks(b[:, 0:S]), ALU.add)
                G.took(m, G_OUT)
                G.wait_taken(dve, it, G_OUT)
                ch(dve.tensor_tensor(g.x_all[:, bass.ds(it * NC, NC), :], xt[:, :, :], over_chunks(w["bout1"][:, :]), ALU.add))
                ch.done()


LH = 8
LD = 64
LHALF = LD // 2
INNER = LH * LD
IB = INNER // P
FFN = int(D * 4 * 2 / 3)
FC = -(-FFN // P)
WINDOW = 64
DEPTH = 2
WAYS = 2
UNITS = WAYS * NH + DEPTH * LH


def attention_order():
    wide = [("wide", i) for i in range(WAYS * NH)]
    order = []
    for l, (before, between) in enumerate(((3, 1), (19, 1))):
        order += [wide.pop(0) for _ in range(before)] + [("local", l, h) for h in range(LH // 2)]
        order += [wide.pop(0) for _ in range(between)] + [("local", l, h) for h in range(LH // 2, LH)]
    return order + wide


UNIT_ORDER = attention_order()
LAG = 3
STEPS = UNITS + LAG

PROLOGUE = [("xnT", ), ("gates", ), ("qk", 0, 0), ("qk", 0, 1), ("cumulate", ), ("wide_q", 0), ("wide_q", 1),
            ("qk", 0, 2), ("qk", 0, 3), ("local_v", 0, 0), ("local_v", 0, 1), ("wide_k", 0), ("wide_k", 1), ("wide_v", )]


def local_tail(l, t):
    return {t: [("local_norm", l, 1)], t + 1: [("local_o", l, 1)], t + 2: [("local_out", l)],
            t + 3: [("shift", l, 1)], t + 4: [("back", l)], t + 5: [("norm", l)],
            t + 6: [("normed", l), ("up", l, 0)], t + 7: [("up", l, 1), ("up", l, 2)]}


BESIDE = {0: [("qk_t", 0, 0)], 1: [("qk_t", 0, 1)], 2: [("qk_t", 0, 2), ("qk_t", 0, 3)],
          10: [("local_norm", 0, 0)], 11: [("local_o", 0, 0)],
          **local_tail(0, 15), 24: [("down", 0)], 25: [("shift", 1, 0), ("qk", 1, 0)], 26: [("qk", 1, 1), ("qk", 1, 2)],
          27: [("qk", 1, 3), ("local_v", 1, 0)], 28: [("local_v", 1, 1)],
          29: [("qk_t", 1, 0), ("qk_t", 1, 1)], 30: [("qk_t", 1, 2), ("qk_t", 1, 3)],
          38: [("local_norm", 1, 0)], 39: [("local_o", 1, 0)], **local_tail(1, 43)}
EPILOGUE = [("down", 1), ("wide_o", 0), ("wide_o", 1), ("wide_out", )]
NO_BANK = ("local_norm", "norm")
USES = {name: k for k, name in enumerate(x for x in PROLOGUE + [y for s in range(STEPS) for y in BESIDE.get(s, ())]
                                         + EPILOGUE if x[0] not in NO_BANK)}


def layer2(nc, g, B):
    w = g.w
    with ExitStack() as ctx:
        def sb(name, shape, dt=FP32):
            return ctx.enter_context(nc.sbuf_tensor("l2_" + name, shape, dt))

        def sem(name):
            return ctx.enter_context(nc.semaphore("l2_" + name))

        xt = sb("xt", [P, NC, D])
        xl = sb("xl", [P, NC, D])
        xnT = sb("xnT", [P, S])
        st = stat_buffers(sb, NC)
        z = sb("z", [P, NC, NH])
        za = sb("za", [P, NC, NH])
        ze = sb("ze", [P, NC, NH])
        zl = sb("zl", [P, NC, NH])
        f = sb("f", [P, NC, NH])
        cums = sb("cums", [P, NC, NH, SLOT])
        qT = sb("qT", [P, WAYS, NG, S])
        kT = sb("kT", [P, NG, S])
        v = sb("v", [P, NC, 2 * D])
        negmax = sb("negmax", [P, 3, NC])
        probs = sb("probs", [P, 3, AW])
        probsT = sb("probsT", [P, 2, AW])
        rowsum = sb("rowsum", [P, WAYS, NC, NH])
        rrow = sb("rrow", [P, WAYS, NC, NH])
        on = sb("on", [P, WAYS, NC, D])
        oT = sb("oT", [P, WAYS, S])
        tables = sb("tables", [P, DEPTH, 4, NC * LD])
        hT = sb("hT", [P, S])
        sq = sb("sq", [P, 2, INNER])
        ss = sb("ss", [P, 4, LH])
        ssm = sb("ssm", [P, 4, LH])
        rinv = sb("rinv", [P, 4, LH])
        rot = sb("rot", [P, 2, INNER])
        qk_raw = sb("qk_raw", [P, 4, INNER])
        qkT = sb("qkT", [P, 2, IB, S])
        v2 = sb("v2", [P, NC, INNER])
        rowsum2 = sb("rowsum2", [P, 2, LH])
        rrow2 = sb("rrow2", [P, 2, LH])
        on2 = sb("on2", [P, 2, NC, INNER // 2])
        oT2 = sb("oT2", [P, IB, S])
        st2 = Names()
        st2.stats, st2.mv, st2.pad = sb("stats2", [P, NC, 6]), sb("mean_var2", [P, NC, 2]), sb("norm_pad2", [1, 1])
        st2.var, st2.rstd = sb("var2", [P, NC]), sb("rstd2", [P, NC])
        hs = sb("hs", [P, NC, D])
        hn = sb("hn", [P, NC, D])
        hnT = sb("hnT", [P, S])
        gg = sb("gg", [P, FC, S])
        hidT = sb("hidT", [P, FC, S])

        Sb, Tb, wide_sum, local_sum = g.bank[0:3], g.bank[3], g.bank[6], g.bank[7]
        G = Banks(g.bank[4:6], [sem("g_full0"), sem("g_full1")], [sem("g_taken0"), sem("g_taken1")], len(USES))

        setup_done = sem("setup_done")
        var_ready = sem("var_ready")
        rstd_ready = sem("rstd_ready")
        xn_ready = sem("xn_ready")
        act_chain = sem("act_chain")
        zl_ready = sem("zl_ready")
        f_ready = sem("f_ready")
        scores_ready = sem("scores_ready")
        negmax_ready = sem("negmax_ready")
        probs_ready = sem("probs_ready")
        transposed = sem("transposed")
        probsT_ready = sem("probsT_ready")
        heads_summed = sem("heads_summed")
        on_ready = sem("on_ready")
        sq_ready = sem("sq_ready")
        ss_ready = sem("ss_ready")
        rinv_ready = sem("rinv_ready")
        qkn_ready = sem("qkn_ready")
        heads2_summed = sem("heads2_summed")
        on2_ready = sem("on2_ready")
        var2_ready = sem("var2_ready")
        rstd2_ready = sem("rstd2_ready")
        hn_ready = sem("hn_ready")
        gelu_ready = sem("gelu_ready")
        xl_ready = sem("xl_ready")
        x_done = sem("x_done")
        dve_chain = sem("dve_chain")
        n_chain = 1 + NORM_STEPS(NC) + 1 + DEPTH * (4 * 3 + 2 + NORM_STEPS(NC))

        block = ctx.enter_context(nc.Block())

        @block.tensor
        def _(pe):
            g.wait_consts(pe)
            g.wait_layer(pe, 2)
            G.open(pe)
            with pe.Fori(0, B) as it:
                def open_bank(name, after=()):
                    return G.fill(pe, it, USES[name], [USES[n] for n in after])

                def transposes(name, blocks, after=()):
                    b = open_bank(name, after)
                    for j, t in enumerate(blocks):
                        last = pe.transpose(b[:, j * P:(j + 1) * P], t, g.ident[:, :])
                    G.filled(last, USES[name])

                def xnT_():
                    transposes(("xnT", ), [xl[:, c, :] for c in range(NC)])

                def gates():
                    b = open_bank(("gates", ), [("xnT", )])
                    for c in range(NC):
                        last = pe.matmul(b[:, c * NH:(c + 1) * NH], xnT[:, c * P:(c + 1) * P], w["f2"][:, :],
                                         start=True, stop=True)
                    G.filled(last, USES[("gates", )])

                def cumulate():
                    pe.wait_ge(f_ready, it + 1)
                    b = open_bank(("cumulate", ))
                    for y, c, parts in ((0, 0, ((0, w["tri2"]), )), (0, 1, ((0, w["ones2"]), (1, w["tri2"]))),
                                        (1, 0, ((0, w["tri_back2"]), (1, w["ones2"]))), (1, 1, ((1, w["tri_back2"]), ))):
                        at = (y * NC + c) * NH
                        for i, (src, m) in enumerate(parts):
                            last = pe.matmul(b[:, at:at + NH], m[:, :], f[:, src, :],
                                             start=(i == 0), stop=(i == len(parts) - 1))
                    G.filled(last, USES[("cumulate", )])

                def wide_q(u):
                    b = open_bank(("wide_q", u))
                    for j in range(2):
                        gi = 2 * u + j
                        last = pe.matmul(b[:, j * S:(j + 1) * S], w["q2"][:, gi * P:(gi + 1) * P], xnT[:, :],
                                         start=True, stop=True)
                    G.filled(last, USES[("wide_q", u)])

                def wide_k(u):
                    b = open_bank(("wide_k", u), [("cumulate", )])
                    for j in range(2):
                        gi = 2 * u + j
                        pe.matmul(b[:, j * S:(j + 1) * S], w["k2"][:, gi * P:(gi + 1) * P], xnT[:, :],
                                  start=True, stop=False, skip_group_check=True)
                        for c in range(NC):
                            last = pe.matmul(b[:, j * S + c * P:j * S + (c + 1) * P],
                                             cums[:, c, gi * GH:(gi + 1) * GH, :].rearrange("p h s -> p (h s)"),
                                             g.ident[:, :], start=False, stop=(c == NC - 1), skip_group_check=True)
                    G.filled(last, USES[("wide_k", u)])

                def wide_v():
                    b = open_bank(("wide_v", ))
                    for c in range(NC):
                        last = pe.matmul(b[:, c * P:(c + 1) * P], xnT[:, c * P:(c + 1) * P], w["v2w"][:, :],
                                         start=True, stop=True)
                    G.filled(last, USES[("wide_v", )])

                def shift(l, i):
                    if i == 0:
                        pe.wait_ge(xl_ready, it * DEPTH + l)
                    transposes(("shift", l, i), [xl[:, c, :] for c in range(NC)], [("local_out", l)] if i else [])

                def qk(l, i):
                    b = open_bank(("qk", l, i), [("shift", l, 0) if l else ("xnT", )])
                    c = i % 2
                    G.filled(pe.matmul(b[:, :], hT[:, c * P:(c + 1) * P],
                                       w["qkv2"][:, l, (i // 2) * INNER:(i // 2 + 1) * INNER], start=True, stop=True),
                             USES[("qk", l, i)])

                def local_v(l, c):
                    b = open_bank(("local_v", l, c))
                    G.filled(pe.matmul(b[:, :], hT[:, c * P:(c + 1) * P], w["qkv2"][:, l, 2 * INNER:3 * INNER],
                                       start=True, stop=True), USES[("local_v", l, c)])

                def qk_t(l, i):
                    pe.wait_ge(qkn_ready, (it * DEPTH + l) * 4 + i + 1)
                    transposes(("qk_t", l, i), [qk_raw[:, i, j * P:(j + 1) * P] for j in range(IB)])

                def local_o(l, half):
                    pe.wait_ge(on2_ready, (it * DEPTH + l) * 2 + half + 1)
                    transposes(("local_o", l, half),
                               [on2[:, half, c, j * P:(j + 1) * P] for j in range(IB // 2) for c in range(NC)])

                def local_out(l):
                    b = open_bank(("local_out", l), [("local_o", l, 0), ("local_o", l, 1)])
                    for c in range(NC):
                        for j in range(IB):
                            last = pe.matmul(b[:, c * P:(c + 1) * P], oT2[:, j, c * P:(c + 1) * P],
                                             w["wo2"][:, l, j, :], start=(j == 0), stop=(j == IB - 1))
                    G.filled(last, USES[("local_out", l)])

                def back(l):
                    transposes(("back", l), [hT[:, c * P:(c + 1) * P] for c in range(NC)], [("shift", l, 1)])

                def normed(l):
                    pe.wait_ge(hn_ready, it * DEPTH + l + 1)
                    transposes(("normed", l), [hn[:, c, :] for c in range(NC)])

                def up(l, m):
                    b = open_bank(("up", l, m), [("normed", l)])
                    pe.matmul(b[:, 0:S], w["up2"][:, l, 0, m * P:(m + 1) * P], hnT[:, :], start=True, stop=True)
                    G.filled(pe.matmul(b[:, S:2 * S], w["up2"][:, l, 1, m * P:(m + 1) * P], hnT[:, :],
                                       start=True, stop=True), USES[("up", l, m)])

                def down(l):
                    b = open_bank(("down", l), [("up", l, m) for m in range(FC)])
                    for c in range(NC):
                        for m in range(FC):
                            last = pe.matmul(b[:, c * P:(c + 1) * P], hidT[:, m, c * P:(c + 1) * P],
                                             w["down2"][:, l, m, :], start=(m == 0), stop=(m == FC - 1))
                    G.filled(last, USES[("down", l)])

                def wide_o(y):
                    if y == 0:
                        pe.wait_ge(on_ready, it + 1)
                    transposes(("wide_o", y), [on[:, y, c, :] for c in range(NC)])

                def wide_out():
                    b = open_bank(("wide_out", ), [("wide_o", y) for y in range(WAYS)])
                    for c in range(NC):
                        for y in range(WAYS):
                            last = pe.matmul(b[:, c * P:(c + 1) * P], oT[:, y, c * P:(c + 1) * P], w["out2"][:, y, :],
                                             start=(y == 0), stop=(y == WAYS - 1))
                    G.filled(last, USES[("wide_out", )])

                do = dict(xnT=xnT_, gates=gates, cumulate=cumulate, wide_q=wide_q, wide_k=wide_k, wide_v=wide_v,
                          shift=shift, qk=qk, local_v=local_v, qk_t=qk_t, local_o=local_o, local_out=local_out,
                          back=back, normed=normed, up=up, down=down, wide_o=wide_o, wide_out=wide_out)

                def scores(u):
                    kind, *of = UNIT_ORDER[u]
                    bank = Sb[u % 3]
                    if kind == "wide":
                        y, h = of[0] // NH, of[0] % NH
                        rows = slice(SLOT * (h % GH), SLOT * (h % GH + 1))
                        return pe_scores(pe, g, bank, qT[rows, y, h // GH, :], kT[rows, h // GH, :],
                                         (g.mask_causal, g.mask_anti)[y], (FORWARD, BACKWARD)[y])
                    l, h = of
                    if h == 0:
                        G.wait_taken(pe, it, USES[("qk_t", l, 2)])
                        G.wait_taken(pe, it, USES[("qk_t", l, 3)])
                    rows = slice(LD * (h % 2), LD * (h % 2 + 1))
                    return pe_scores(pe, g, bank, qkT[rows, 0, h // 2, :], qkT[rows, 1, h // 2, :], g.mask_band, FORWARD)

                def values(u):
                    kind, *of = UNIT_ORDER[u]
                    pt = probsT[:, u % 2, :]
                    if kind == "wide":
                        y, h = of[0] // NH, of[0] % NH
                        at = (y * NH + h) * NC * DH
                        n = min(D, WAYS * NC * D - at - DH)
                        outs = [wide_sum[:, at + c * DH:at + c * DH + n] for c in range(NC)]
                        last = pe_values(pe, outs, pt, v[:, :, h * DH:h * DH + n], (FORWARD, BACKWARD)[y])
                        if of[0] == WAYS * NH - 1:
                            last.then_inc(heads_summed, 1)
                        return
                    l, h = of
                    hh = h % (LH // 2)
                    if h == LH // 2:
                        pe.wait_ge(on2_ready, (it * DEPTH + l) * 2 + 1)
                    n = min(2, LH // 2 - hh)
                    outs = [local_sum[:, (c * LH // 2 + hh) * LD:(c * LH // 2 + hh + n) * LD] for c in range(NC)]
                    last = pe_values(pe, outs, pt, v2[:, :, h * LD:(h + n) * LD], FORWARD)
                    if hh == LH // 2 - 1:
                        last.then_inc(heads2_summed, 1)

                pe.wait_ge(xn_ready, it + 1)
                for name, *args in PROLOGUE:
                    do[name](*args)
                for name in PROLOGUE[-2:]:
                    G.wait_taken(pe, it, USES[name])
                for s in range(STEPS):
                    if s < UNITS:
                        scores(s).then_inc(scores_ready, 1)
                    for name, *args in BESIDE.get(s, ()):
                        if name in do:
                            do[name](*args)
                    if 0 <= s - LAG:
                        pe.wait_ge(probsT_ready, it * UNITS + s - LAG + 1)
                        values(s - LAG)
                    if 0 <= s - 2 < UNITS:
                        u = s - 2
                        pe.wait_ge(probs_ready, it * UNITS + u + 1)
                        pe_transpose3(pe, g, Tb, probs[:, u % 3, :]).then_inc(transposed, 1)
                for name, *args in EPILOGUE:
                    if name in do:
                        do[name](*args)

        @block.gpsimd
        def _(pool):
            g.wait_layer(pool, 0)
            with pool.Fori(0, B) as it:
                pool.wait_ge(var_ready, it + 1)
                norm_rstd(pool, g, st, NC).then_inc(rstd_ready, 1)
                for l in range(DEPTH):
                    for i in range(4):
                        n = (it * DEPTH + l) * 4 + i + 1
                        pool.wait_ge(ss_ready, n)
                        pool.tensor_tensor(rinv[:, i, :], ssm[:, i, :], g.neg_half[:, 0:LH], ALU.pow).then_inc(rinv_ready, 1)
                        G.wait_taken(pool, it, USES[("qk", l, i)])
                        pool.wait_ge(rinv_ready, n)
                        heads = qk_raw[:, i, :].rearrange("p (h d) -> p h d", h=LH)
                        pool.tensor_tensor(heads, heads, rinv[:, i, :].unsqueeze(2).to_broadcast([P, LH, LD]),
                                           ALU.mult).then_inc(qkn_ready, 1)
                    pool.wait_ge(var2_ready, it * DEPTH + l + 1)
                    norm_rstd(pool, g, st2, NC).then_inc(rstd2_ready, 1)

        @block.scalar
        def _(act):
            g.wait_layer(act, 2)
            g.wait_consts(act)
            with act.Fori(0, B) as it:
                def gates():
                    ch = Chain(act, act_chain, it, 2)
                    G.wait_taken(act, it, USES[("gates", )])
                    ch(act.activation(za[:, :, :], z[:, :, :], ACT.Abs))
                    ch(act.activation(ze[:, :, :], za[:, :, :], ACT.Exp, scale=-1.0))
                    act.activation(zl[:, :, :], ze[:, :, :], ACT.Ln, bias=1.0).then_inc(zl_ready, 1)

                def wide_q(u):
                    b = G.read(act, it, USES[("wide_q", u)])
                    for y in range(WAYS):
                        last = act.activation(qT[:, y, 2 * u:2 * u + 2, :], chunks(b[:, :]), ACT.Identity,
                                              bias=w["one_rows2"][:, y:y + 1], scale=DH ** -0.5)
                    G.took(last, USES[("wide_q", u)])

                def qk(l, i):
                    b = G.read(act, it, USES[("qk", l, i)])
                    act.activation(sq[:, i % 2, :], b[:, :], ACT.Square).then_inc(sq_ready, 1)

                def local_v(l, c):
                    b = G.read(act, it, USES[("local_v", l, c)])
                    G.took(act.activation(v2[:, c, :], b[:, :], ACT.Copy), USES[("local_v", l, c)])

                def qk_t(l, i):
                    b = G.read(act, it, USES[("qk_t", l, i)])
                    c = i % 2
                    G.took(act.activation(qkT[:, i // 2, :, c * P:(c + 1) * P], chunks(b[:, :], IB), ACT.Copy),
                           USES[("qk_t", l, i)])

                def up(l, m):
                    b = G.read(act, it, USES[("up", l, m)])
                    act.activation(gg[:, m, :], b[:, S:2 * S], ACT.Gelu,
                                   bias=w["bup2"][:, l, 1, m:m + 1]).then_inc(gelu_ready, 1)

                do = dict(gates=gates, wide_q=wide_q, qk=qk, local_v=local_v, qk_t=qk_t, up=up)

                for name, *args in PROLOGUE:
                    if name in do:
                        do[name](*args)
                for u in range(UNITS + LAG):
                    if u < UNITS:
                        kind, *of = UNIT_ORDER[u]
                        way = FORWARD
                        if kind == "wide":
                            y, h = of[0] // NH, of[0] % NH
                            way = (FORWARD, BACKWARD)[y]
                            sums = [rowsum[:, y, c, h:h + 1] for c in range(NC)]
                        else:
                            half, hh = of[1] // (LH // 2), of[1] % (LH // 2)
                            sums = [rowsum2[:, half, c * LH // 2 + hh:c * LH // 2 + hh + 1] for c in range(NC)]
                        act.wait_ge(negmax_ready, it * UNITS + u + 1)
                        act_probs(act, Sb[u % 3], negmax[:, u % 3, :], probs[:, u % 3, :], sums,
                                  way).then_inc(probs_ready, 1)
                    for name, *args in BESIDE.get(u, ()):
                        if name in do:
                            do[name](*args)
                for name, *args in EPILOGUE:
                    if name in do:
                        do[name](*args)

        @block.vector
        def _(dve):
            g.wait_consts(dve)
            g.wait_layer(dve, 2)
            for l in range(DEPTH):
                dve.tensor_tensor(tables[:, l, :, :].rearrange("p i (c d) -> p i c d", c=NC),
                                  w["rot2"][:, :, :].rearrange("p i (c d) -> p i c d", c=NC),
                                  w["scale_rows2"][:, l, :, :].unsqueeze(2).to_broadcast([P, 4, NC, LD]), ALU.mult)
            dve.memset(v[:, :, D:2 * D], 0.0)
            dve.memset(hT[:, 0:1], 0.0)
            dve.memset(cums[:, :, :, :], 0.0).then_inc(setup_done, 1)
            dve.wait_ge(setup_done, 1)
            with dve.Fori(0, B) as it:
                ch = Chain(dve, dve_chain, it, n_chain)

                def shifted(b):
                    dve.tensor_copy(hT[0:P // 2, :], b[0:P // 2, 0:S])
                    return dve.tensor_copy(hT[P // 2:P, 1:S], b[P // 2:P, 0:S - 1])

                def xnT_():
                    b = G.read(dve, it, USES[("xnT", )])
                    dve.tensor_copy(xnT[:, :], b[:, 0:S])
                    G.took(shifted(b), USES[("xnT", )])

                def shift(l, i):
                    G.took(shifted(G.read(dve, it, USES[("shift", l, i)])), USES[("shift", l, i)])

                def gates():
                    b = G.read(dve, it, USES[("gates", )])
                    G.took(dve.tensor_tensor(z[:, :, :], chunks(b[:, 0:NC * NH]), over_chunks(w["bf2"][:, :]), ALU.add),
                           USES[("gates", )])
                    dve.wait_ge(zl_ready, it + 1)
                    dve.scalar_tensor_tensor(out=f[:, :, :], in0=z[:, :, :], scalar=0.0, in1=zl[:, :, :],
                                             op0=ALU.min, op1=ALU.subtract).then_inc(f_ready, 1)

                def cumulate():
                    b = G.read(dve, it, USES[("cumulate", )])
                    for y in range(WAYS):
                        last = dve.tensor_scalar(cums[:, :, :, DH + y], chunks(b[:, y * NC * NH:(y + 1) * NC * NH]), -1.0,
                                                 None, ALU.mult)
                    G.took(last, USES[("cumulate", )])

                def wide_k(u):
                    b = G.read(dve, it, USES[("wide_k", u)])
                    G.took(dve.tensor_copy(kT[:, 2 * u:2 * u + 2, :], chunks(b[:, :])), USES[("wide_k", u)])

                def wide_v():
                    b = G.read(dve, it, USES[("wide_v", )])
                    G.took(dve.tensor_copy(v[:, :, 0:D], chunks(b[:, 0:S])), USES[("wide_v", )])

                def qk(l, i):
                    c, cos, sin = i % 2, 2 * (i // 2), 2 * (i // 2) + 1
                    b = G.read(dve, it, USES[("qk", l, i)])
                    dve.wait_ge(sq_ready, (it * DEPTH + l) * 4 + i + 1)
                    bh = b[:, :].rearrange("p (h d) -> p h d", h=LH)
                    rh = rot[:, i % 2, :].rearrange("p (h d) -> p h d", h=LH)

                    def table(n, lo, hi):
                        return tables[:, l, n, c * LD + lo:c * LD + hi].unsqueeze(1).to_broadcast([P, LH, hi - lo])

                    dve.tensor_tensor(rh[:, :, 0:LHALF], bh[:, :, LHALF:LD], table(sin, 0, LHALF), ALU.mult)
                    m = ch.mark(dve.tensor_tensor(rh[:, :, LHALF:LD], bh[:, :, 0:LHALF], table(sin, LHALF, LD), ALU.mult))
                    m2 = ch.mark(dve.reduce_sum(ss[:, i, :], sq[:, i % 2, :].rearrange("p (h d) -> p h d", h=LH), AX.X))
                    ch.wait(m)
                    m = ch.mark(dve.tensor_tensor(bh, bh, table(cos, 0, LD), ALU.mult))
                    ch.wait(m2)
                    dve.tensor_scalar(ssm[:, i, :], ss[:, i, :], 1e-24, None, ALU.max).then_inc(ss_ready, 1)
                    ch.wait(m)
                    G.took(dve.tensor_tensor(qk_raw[:, i, :], b[:, :], rot[:, i % 2, :], ALU.add), USES[("qk", l, i)])

                def local_norm(l, half):
                    dve.wait_ge(heads2_summed, (it * DEPTH + l) * 2 + half + 1)
                    ch(dve.reciprocal(rrow2[:, half, :], rowsum2[:, half, :]))
                    dve.tensor_tensor(on2[:, half, :, :].rearrange("p c (h d) -> p (c h) d", d=LD),
                                      local_sum[:, :].rearrange("p (x d) -> p x d", d=LD),
                                      rrow2[:, half, :].unsqueeze(2).to_broadcast([P, LH, LD]),
                                      ALU.mult).then_inc(on2_ready, 1)

                def local_o(l, half):
                    b = G.read(dve, it, USES[("local_o", l, half)])
                    G.took(dve.tensor_copy(oT2[:, 2 * half:2 * half + 2, :], chunks(b[:, :])), USES[("local_o", l, half)])

                def local_out(l):
                    b = G.read(dve, it, USES[("local_out", l)])
                    G.took(dve.tensor_tensor(xl[:, :, :], xl[:, :, :], chunks(b[:, 0:S]), ALU.add), USES[("local_out", l)])

                def back(l):
                    b = G.read(dve, it, USES[("back", l)])
                    G.took(dve.tensor_copy(hs[:, :, :], chunks(b[:, 0:S])), USES[("back", l)])
                    G.wait_taken(dve, it, USES[("back", l)])
                    norm_stats(dve, ch, hs, st2, NC).then_inc(var2_ready, 1)

                def norm(l):
                    dve.wait_ge(rstd2_ready, it * DEPTH + l + 1)
                    norm_apply(dve, hs, hn, st2, NC).then_inc(hn_ready, 1)

                def normed(l):
                    b = G.read(dve, it, USES[("normed", l)])
                    G.took(dve.tensor_scalar(hnT[:, :], b[:, 0:S], w["ln2"][:, l, 0:1], w["ln2"][:, l, 1:2],
                                             ALU.mult, ALU.add), USES[("normed", l)])

                def up(l, m):
                    b = G.read(dve, it, USES[("up", l, m)])
                    dve.wait_ge(gelu_ready, (it * DEPTH + l) * FC + m + 1)
                    G.took(dve.scalar_tensor_tensor(out=hidT[:, m, :], in0=b[:, 0:S],
                                                    scalar=w["bup2"][:, l, 0, m:m + 1], in1=gg[:, m, :],
                                                    op0=ALU.add, op1=ALU.mult), USES[("up", l, m)])

                def down(l):
                    b = G.read(dve, it, USES[("down", l)])
                    G.took(dve.tensor_tensor(xl[:, :, :], xl[:, :, :], chunks(b[:, 0:S]), ALU.add), USES[("down", l)])
                    G.wait_taken(dve, it, USES[("down", l)])
                    dve.tensor_tensor(xl[:, :, :], xl[:, :, :], over_chunks(w["bdown2"][:, l, :]),
                                      ALU.add).then_inc(xl_ready, 1)

                def wide_o(y):
                    b = G.read(dve, it, USES[("wide_o", y)])
                    G.took(dve.tensor_copy(oT[:, y, :], b[:, 0:S]), USES[("wide_o", y)])

                def wide_out():
                    b = G.read(dve, it, USES[("wide_out", )])
                    G.took(dve.tensor_tensor(xt[:, :, :], xt[:, :, :], chunks(b[:, 0:S]), ALU.add), USES[("wide_out", )])

                do = dict(xnT=xnT_, gates=gates, cumulate=cumulate, wide_k=wide_k, wide_v=wide_v, shift=shift, qk=qk,
                          local_norm=local_norm, local_o=local_o, local_out=local_out, back=back, norm=norm,
                          normed=normed, up=up, down=down, wide_o=wide_o, wide_out=wide_out)

                ch(dve.tensor_copy(xt[:, :, :], g.x_all[:, bass.ds(it * NC, NC), :]))
                norm_stats(dve, ch, xt, st, NC).then_inc(var_ready, 1)
                dve.wait_ge(rstd_ready, it + 1)
                norm_apply(dve, xt, xl, st, NC).then_inc(xn_ready, 1)
                for name, *args in PROLOGUE:
                    if name in do:
                        do[name](*args)
                for s in range(STEPS):
                    if s < UNITS:
                        y = UNIT_ORDER[s][1] // NH if UNIT_ORDER[s][0] == "wide" else 0
                        dve.wait_ge(scores_ready, it * UNITS + s + 1)
                        dve_negmax(dve, Sb[s % 3], negmax[:, s % 3, :], (FORWARD, BACKWARD)[y]).then_inc(negmax_ready, 1)
                    for name, *args in BESIDE.get(s, ()):
                        if name in do:
                            do[name](*args)
                    if 0 <= s - 2 < UNITS:
                        u = s - 2
                        dve.wait_ge(transposed, it * UNITS + u + 1)
                        dve.tensor_copy(probsT[:, u % 2, :], Tb[:, 0:AW]).then_inc(probsT_ready, 1)
                dve.wait_ge(heads_summed, it + 1)
                ch(dve.reciprocal(rrow[:, :, :, :], rowsum[:, :, :, :]))
                for y in range(WAYS):
                    for c in range(NC):
                        last = dve.tensor_tensor(
                            on[:, y, c, :].rearrange("p (h d) -> p h d", h=NH),
                            wide_sum[:, :].rearrange("p (y h c d) -> p y c h d", y=WAYS, h=NH, c=NC)[:, y, c, :, :],
                            rrow[:, y, c, :].unsqueeze(2).to_broadcast([P, NH, DH]), ALU.mult)
                last.then_inc(on_ready, 1)
                for name, *args in EPILOGUE:
                    if name in do:
                        do[name](*args)
                dve.wait_ge(xl_ready, it * DEPTH + DEPTH)
                G.wait_taken(dve, it, USES[("wide_out", )])
                dve.tensor_tensor(g.x_all[:, bass.ds(it * NC, NC), :], xt[:, :, :], xl[:, :, :],
                                  ALU.add).then_inc(x_done, 1)
                dve.wait_ge(x_done, it + 1)
                dve.memset(st.pad[:, :], 0.0)
                ch.done()


FB = 8
GELU_IN = math.sqrt(2.0 / math.pi)


def layer3(nc, g, B, out):
    w = g.w
    with ExitStack() as ctx:
        def sb(name, shape, dt=FP32):
            return ctx.enter_context(nc.sbuf_tensor("l3_" + name, shape, dt))

        def sem(name):
            return ctx.enter_context(nc.semaphore("l3_" + name))

        xt = sb("xt", [P, NC, D])
        xn = sb("xn", [P, NC, D])
        xnT = sb("xnT", [P, S])
        st = stat_buffers(sb, NC)
        r = router_buffers(sb, NC)
        bq_one = sb("bq_one", [P, FB])
        bk_one = sb("bk_one", [P, FB])
        neg_bq = sb("neg_bq", [P, FB])
        neg_bk = sb("neg_bk", [P, FB])
        neg_part = sb("neg_part", [P, 2, 2, S])
        exp_raw = sb("exp_raw", [P, 2, 2, S])
        exp_part = sb("exp_part", [P, 2, 2, S])
        k_feat = sb("k_feat", [P, 2, S])
        q_feat = sb("q_feat", [P, 2, S])
        kv_junk = sb("kv_junk", [P, 2, S])
        k_sum = sb("k_sum", [P, FB])
        kv_sum = sb("kv_sum", [P, FB])
        den = sb("den", [P, 2, S])
        rden = sb("rden", [P, 2, S])
        pool_pad = sb("pool_pad", [1, FB])
        qkv = sb("qkv", [P, 2, S])
        attnT = sb("attnT", [P, FB, S])
        th = sb("th", [P, 2, 2 * S])
        gated = sb("gated", [P, 2, 2 * S])
        hT = sb("hT", [P, 2, HC, S])
        y = sb("y", [P, NC, D])
        y2 = sb("y2", [P, NC, D])
        ty = sb("ty", [P, NC, D])

        F = Banks(g.bank[4:6], [sem(f"f_full{i}") for i in range(2)], [sem(f"f_taken{i}") for i in range(2)], 2 * FB)
        G = Banks(g.bank[0:4], [sem(f"g_full{i}") for i in range(4)], [sem(f"g_taken{i}") for i in range(4)], 4 * E)
        Db = g.bank[6]
        Ob = g.bank[7]
        var_ready = sem("var_ready")
        rstd_ready = sem("rstd_ready")
        xn_ready = sem("xn_ready")
        setup_done = sem("setup_done")
        gate_exp = sem("gate_exp")
        neg_ready = sem("neg_ready")
        raw_ready = sem("raw_ready")
        pool_chain = sem("pool_chain")
        rden_ready = sem("rden_ready")
        xnT_full = sem("xnT_full")
        xnT_ready = sem("xnT_ready")
        logits_ready = sem("logits_ready")
        ranked = sem("ranked")
        k_ready = sem("k_ready")
        attn_ready = sem("attn_ready")
        tanh_ready = sem("tanh_ready")
        down_ready = sem("down_ready")
        down_used = sem("down_used")
        out_ready = sem("out_ready")
        gelu_in = sem("gelu_in")
        gelu_tanh = sem("gelu_tanh")
        x_done = sem("x_done")
        stored = sem("stored")
        dve_chain = sem("dve_chain")
        n_chain = 1 + NORM_STEPS(NC) + ROUTER_STEPS(NC) + 1 + 2 * FB + 4

        block = ctx.enter_context(nc.Block())

        @block.tensor
        def _(pe):
            g.wait_consts(pe)
            g.wait_layer(pe, 3)
            F.open(pe)
            G.open(pe)
            pe.sem_inc(down_used, 1)
            with pe.Fori(0, B) as it:
                pe.wait_ge(xn_ready, it + 1)
                for c in range(NC):
                    last = pe.transpose(Db[:, c * P:(c + 1) * P], xn[:, c, :], g.ident[:, :])
                last.then_inc(xnT_full, 1)
                pe.wait_ge(xnT_ready, it + 1)
                for c in range(NC):
                    last = pe.matmul(Ob[:, c * E:(c + 1) * E], xnT[:, c * P:(c + 1) * P], w["gate3"][:, :],
                                     start=True, stop=True)
                last.then_inc(logits_ready, 1)
                for m in range(E + 2):
                    if m < E:
                        cols = slice(m * P, (m + 1) * P)
                        b = F.fill(pe, it, 2 * m)
                        pe.matmul(b[:, 0:S], w["k3"][:, cols], xnT[:, :], start=True, stop=True)
                        F.filled(pe.matmul(b[:, S:2 * S], w["v3"][:, cols], xnT[:, :], start=True, stop=True), 2 * m)
                        b = F.fill(pe, it, 2 * m + 1)
                        F.filled(pe.matmul(b[:, 0:S], w["q3"][:, cols], xnT[:, :], start=True, stop=True), 2 * m + 1)
                        for u in range(2):
                            for i, wt in enumerate((w["egate3"], w["eup3"])):
                                k = 4 * m + 2 * u + i
                                b = G.fill(pe, it, k)
                                for j in range(2):
                                    h = (m * HC + 2 * u + j) * P
                                    last = pe.matmul(b[:, j * S:(j + 1) * S], wt[:, h:h + P], xnT[:, :],
                                                     start=True, stop=True)
                                G.filled(last, k)
                    if 1 <= m <= E:
                        e = m - 1
                        G.wait_taken(pe, it, 4 * e + 1)
                        G.wait_taken(pe, it, 4 * e + 3)
                        pe.wait_ge(down_used, it * E + e + 1)
                        for c in range(NC):
                            for j in range(HC):
                                last = pe.matmul(Db[:, c * P:(c + 1) * P], hT[:, e % 2, j, c * P:(c + 1) * P],
                                                 w["edown3"][:, e * HC + j, :], start=(j == 0), stop=(j == HC - 1))
                        last.then_inc(down_ready, 1)
                    if m >= 2:
                        f = m - 2
                        if f == 0:
                            pe.wait_ge(ranked, it + 1)
                        pe.wait_ge(attn_ready, it * FB + f + 1)
                        for c in range(NC):
                            last = pe.matmul(Ob[:, c * P:(c + 1) * P], attnT[:, f, c * P:(c + 1) * P],
                                             w["out3"][:, f, :], start=(f == 0 and c == 0), stop=(f == FB - 1),
                                             skip_group_check=True)
                last.then_inc(out_ready, 1)

        @block.gpsimd
        def _(pool):
            g.wait_layer(pool, 0)
            with pool.Fori(0, B) as it:
                pool.wait_ge(var_ready, it + 1)
                norm_rstd(pool, g, st, NC).then_inc(rstd_ready, 1)
                ch = Chain(pool, pool_chain, it, FB)

                for m in range(FB):
                    s = m % 2
                    F.wait_taken(pool, it, 2 * m)
                    pool_hold(pool, g, pool_pad[:, m:m + 1])
                    ch(pool.tensor_scalar(qkv[:, s, :], q_feat[:, s, :], kv_sum[:, m:m + 1], None, ALU.mult))
                    pool.wait_ge(rden_ready, it * FB + m + 1)
                    pool.tensor_tensor(attnT[:, m, :], qkv[:, s, :], rden[:, s, :], ALU.mult).then_inc(attn_ready, 1)
                ch.done()

        @block.scalar
        def _(act):
            g.wait_layer(act, 3)
            act.wait_ge(setup_done, 1)
            with act.Fori(0, B) as it:
                for m in range(E):
                    b = F.read(act, it, 2 * m)
                    act.activation(neg_part[:, m % 2, 0, :], b[:, 0:S], ACT.Relu, bias=neg_bk[:, m:m + 1], scale=-1.0)
                    b = F.read(act, it, 2 * m + 1)
                    act.activation(neg_part[:, m % 2, 1, :], b[:, 0:S], ACT.Relu, bias=neg_bq[:, m:m + 1],
                                   scale=-1.0).then_inc(neg_ready, 1)
                    act.wait_ge(neg_ready, it * FB + m + 1)
                    act.activation(exp_raw[:, m % 2, :, :], neg_part[:, m % 2, :, :], ACT.Exp,
                                   scale=-1.0).then_inc(raw_ready, 1)
                    if m == 0:
                        act.wait_ge(ranked, it + 1)
                        act.activation(r.ex[:, :, :], r.ls[:, :, :], ACT.Exp).then_inc(gate_exp, 1)
                    for u in range(2):
                        b = G.read(act, it, 4 * m + 2 * u)
                        act.activation(th[:, u, :], b[:, :], ACT.Tanh, scale=0.5).then_inc(tanh_ready, 1)
                act.wait_ge(gelu_in, it + 1)
                act.activation(ty[:, :, :], y2[:, :, :], ACT.Tanh, scale=GELU_IN).then_inc(gelu_tanh, 1)

        @block.sync
        def _(sp):
            with sp.Fori(0, B) as it:
                sp.wait_ge(x_done, it + 1)
                sp.dma_start(out[bass.ds(it, 1), :, :].rearrange("b (c p) d -> p (b c) d", p=P),
                             g.x_all[:, bass.ds(it * NC, NC), :]).then_inc(stored, 16)
            sp.wait_ge(stored, 16 * B)

        @block.vector
        def _(dve):
            g.wait_consts(dve)
            g.wait_layer(dve, 3)
            dve.tensor_scalar(bq_one[:, :], w["bq3"][:, :], 1.0, None, ALU.add)
            dve.tensor_scalar(neg_bk[:, :], w["bk3"][:, :], -1.0, None, ALU.mult)
            dve.tensor_scalar(neg_bq[:, :], w["bq3"][:, :], -1.0, None, ALU.mult)
            dve.tensor_scalar(bk_one[:, :], w["bk3"][:, :], 1.0, None, ALU.add).then_inc(setup_done, 1)
            dve.wait_ge(setup_done, 1)
            with dve.Fori(0, B) as it:
                ch = Chain(dve, dve_chain, it, n_chain)
                ch(dve.tensor_copy(xt[:, :, :], g.x_all[:, bass.ds(it * NC, NC), :]))
                norm_stats(dve, ch, xt, st, NC).then_inc(var_ready, 1)
                dve.wait_ge(rstd_ready, it + 1)
                norm_apply(dve, xt, xn, st, NC).then_inc(xn_ready, 1)
                dve.wait_ge(xnT_full, it + 1)
                dve.tensor_copy(xnT[:, :], Db[:, 0:S]).then_inc(xnT_ready, 1)
                dve.wait_ge(logits_ready, it + 1)
                router_rank(dve, ch, r, Ob[:, 0:NC * E].rearrange("p (c e) -> p c e", e=E), NC).then_inc(ranked, 1)

                def gate(m, u):
                    k = 4 * m + 2 * u
                    bg = G.read(dve, it, k)
                    if m >= 1:
                        G.wait_taken(dve, it, k - 3)
                    dve.wait_ge(tanh_ready, it * 2 * E + 2 * m + u + 1)
                    G.took(dve.scalar_tensor_tensor(out=gated[:, u, :], in0=th[:, u, :], scalar=1.0,
                                                    in1=bg[:, :], op0=ALU.add, op1=ALU.mult), k)
                    bu = G.read(dve, it, k + 1)
                    G.wait_taken(dve, it, k)
                    G.took(dve.tensor_tensor(hT[:, m % 2, 2 * u:2 * u + 2, :], chunks(gated[:, u, :]),
                                             chunks(bu[:, :]), ALU.mult), k + 1)

                def features(m):
                    s = m % 2
                    dve.wait_ge(raw_ready, it * FB + m + 1)
                    ch(dve.tensor_scalar(exp_part[:, s, :, :], exp_raw[:, s, :, :], -1.0, 1.0, ALU.add, ALU.add))
                    bkv = F.read(dve, it, 2 * m)
                    bq = F.read(dve, it, 2 * m + 1)
                    if m >= 2:
                        dve.wait_ge(attn_ready, it * FB + m - 1)
                    dve.scalar_tensor_tensor(out=k_feat[:, s, :], in0=bkv[:, 0:S], scalar=bk_one[:, m:m + 1],
                                             in1=exp_part[:, s, 0, :], op0=ALU.add, op1=ALU.max,
                                             accum_out=k_sum[:, m:m + 1]).then_inc(k_ready, 1)
                    F.took(dve.scalar_tensor_tensor(out=q_feat[:, s, :], in0=bq[:, 0:S], scalar=bq_one[:, m:m + 1],
                                                    in1=exp_part[:, s, 1, :], op0=ALU.add, op1=ALU.max), 2 * m + 1)
                    dve.wait_ge(k_ready, it * E + m + 1)
                    F.took(dve.scalar_tensor_tensor(out=kv_junk[:, s, :], in0=bkv[:, S:2 * S],
                                                    scalar=w["bv3"][:, m:m + 1], in1=k_feat[:, s, :],
                                                    op0=ALU.add, op1=ALU.mult,
                                                    accum_out=kv_sum[:, m:m + 1]), 2 * m)

                def denominators(m):
                    s = m % 2
                    F.wait_taken(dve, it, 2 * m + 1)
                    ch(dve.tensor_scalar(den[:, s, :], q_feat[:, s, :], k_sum[:, m:m + 1], 1e-6, ALU.mult, ALU.add))
                    dve.reciprocal(rden[:, s, :], den[:, s, :]).then_inc(rden_ready, 1)

                for m in range(E + 1):
                    if m < E:
                        gate(m, 0)
                        features(m)
                        gate(m, 1)
                        denominators(m)
                    if m == 0:
                        dve.wait_ge(gate_exp, it + 1)
                        ch(router_mix(dve, ch, r, g.iota, NC, False, scale=0.5))
                    if m >= 1:
                        e = m - 1
                        dve.wait_ge(down_ready, it * E + e + 1)
                        dve.wait_ge(down_used, it * E + e + 1)
                        for c in range(NC):
                            last = dve.scalar_tensor_tensor(out=xt[:, c, :], in0=Db[:, c * P:(c + 1) * P],
                                                            scalar=r.comb[:, c, e:e + 1], in1=xt[:, c, :],
                                                            op0=ALU.mult, op1=ALU.add)
                        last.then_inc(down_used, 1)
                dve.wait_ge(out_ready, it + 1)
                ch(dve.tensor_tensor(y[:, :, :], chunks(Ob[:, 0:S]), over_chunks(w["bout3"][:, :]), ALU.add))
                ch(dve.tensor_tensor(ty[:, :, :], y[:, :, :], y[:, :, :], ALU.mult))
                ch(dve.tensor_scalar(ty[:, :, :], ty[:, :, :], 0.044715, 1.0, ALU.mult, ALU.add))
                dve.tensor_tensor(y2[:, :, :], ty[:, :, :], y[:, :, :], ALU.mult).then_inc(gelu_in, 1)
                dve.wait_ge(gelu_tanh, it + 1)
                ch(dve.scalar_tensor_tensor(out=y2[:, :, :], in0=ty[:, :, :], scalar=1.0, in1=y[:, :, :],
                                            op0=ALU.add, op1=ALU.mult))
                dve.wait_ge(down_used, it * E + E + 1)
                dve.scalar_tensor_tensor(out=g.x_all[:, bass.ds(it * NC, NC), :], in0=y2[:, :, :], scalar=0.5,
                                         in1=xt[:, :, :], op0=ALU.mult, op1=ALU.add).then_inc(x_done, 1)
                dve.wait_ge(x_done, it + 1)
                dve.memset(st.pad[:, :], 0.0)
                ch.done()


SHARED = ("ident", "one_row", "iota", "neg_half")


def load_lists(B):
    t = {
        "ident": (0, [P, P]), "one_row": (0, [P, 1]), "iota": (0, [P, E]), "neg_half": (0, [P, 32]),
        "alibi": (1, [P, NG, S]), "masks": (0, [P, 3, AW]),
        "before0": (0, [P, P]), "after0": (0, [P, P]), "eta0": (0, [P, 1]), "wv0": (0, [P, D]), "start0": (0, [P, D]),
        "lin0": (0, [P, D]), "bv0": (0, [P, D]), "blin0": (0, [P, D]), "gate0": (0, [P, E]),
        "left0": (0, [P, E * LR]), "right0": (0, [E * LR, D]),
        "q1": (1, [P, NG * P]), "k1": (1, [P, NG * P]), "v1": (1, [P, D]), "out1": (1, [P, D]),
        "bq1": (1, [P, NG]), "bk1": (1, [P, NG]), "bv1": (1, [P, D]), "bout1": (1, [P, D]),
        "gate1": (1, [P, E]), "up1": (1, [P, E * HID]), "down1": (1, [P, E * HC, D]),
        "bup1": (1, [P, E * HC]), "bdown1": (1, [E, D]),
        "q2": (2, [P, NG * P]), "k2": (2, [P, NG * P]), "v2w": (2, [P, D]), "f2": (2, [P, NH]), "bf2": (2, [P, NH]),
        "out2": (2, [P, WAYS, D]), "one_rows2": (2, [P, WAYS]),
        "tri2": (2, [P, P]), "tri_back2": (2, [P, P]), "ones2": (2, [P, P]),
        "rot2": (2, [P, 4, NC * LD]), "scale_rows2": (2, [P, DEPTH, 4, LD]),
        "qkv2": (2, [P, DEPTH, 3 * INNER]), "wo2": (2, [P, DEPTH, IB, D]), "ln2": (2, [P, DEPTH, 2]),
        "up2": (2, [P, DEPTH, 2, FC * P]), "bup2": (2, [P, DEPTH, 2, FC]), "down2": (2, [P, DEPTH, FC, D]),
        "bdown2": (2, [P, DEPTH, D]),
        "gate3": (3, [P, E]), "q3": (3, [P, FB * P]), "k3": (3, [P, FB * P]), "v3": (3, [P, FB * P]),
        "bq3": (3, [P, FB]), "bk3": (3, [P, FB]), "bv3": (3, [P, FB]), "out3": (3, [P, FB, D]), "bout3": (3, [P, D]),
        "egate3": (3, [P, E * HID]), "eup3": (3, [P, E * HID]), "edown3": (3, [P, E * HC, D]),
    }
    return t


def program(nc, dram, x_in, out, scratch, B):
    g = Names()
    lists = load_lists(B)
    held = {}

    def hold(ctx, layer, names=None):
        for n, (of, shape) in lists.items():
            if of == layer and n != "masks" and (names is None or n in names):
                held[n] = ctx.enter_context(nc.sbuf_tensor("w_" + n, shape, FP32))

    with ExitStack() as ctx:
        hold(ctx, 0, SHARED)
        hold(ctx, 3)
        only2 = ctx.enter_context(ExitStack())
        g.x_all = ctx.enter_context(nc.sbuf_tensor("x_all", [P, NC * B, D], FP32))
        g.ident16 = ctx.enter_context(nc.sbuf_tensor("ident16", [P, P], BF16))
        masks16 = ctx.enter_context(nc.sbuf_tensor("masks16", [P, 3, AW], BF16))
        hold(only2, 2)
        only1 = only2.enter_context(ExitStack())
        hold(only1, 1)
        only0 = only1.enter_context(ExitStack())
        hold(only0, 0, [n for n in lists if n not in SHARED])
        g.w = held
        g.ident, g.one_row, g.iota, g.alibi = held["ident"], held["one_row"], held["iota"], held["alibi"]
        g.neg_half = held["neg_half"]
        g.mask_causal, g.mask_anti, g.mask_band = masks16[:, 0, :], masks16[:, 1, :], masks16[:, 2, :]
        g.bank = [ctx.enter_context(nc.psum_tensor(f"bank{i}", [P, 512], FP32)) for i in range(8)]
        loaded = [ctx.enter_context(nc.semaphore(f"loaded{i}")) for i in range(4)]
        x_loaded = ctx.enter_context(nc.semaphore("x_loaded"))
        consts_ready = ctx.enter_context(nc.semaphore("consts_ready"))
        n_loads = [0] * 4
        for n, (layer, _) in lists.items():
            n_loads[layer] += 16

        def wait_layer(eng, layer):
            eng.wait_ge(loaded[layer], n_loads[layer])

        def wait_consts(eng):
            eng.wait_ge(loaded[0], n_loads[0])
            eng.wait_ge(consts_ready, 1)

        g.wait_layer, g.wait_consts = wait_layer, wait_consts
        with ExitStack() as c0:
            masks32 = c0.enter_context(nc.sbuf_tensor("masks32", [P, 3, AW], FP32))
            block = c0.enter_context(nc.Block())

            def load(sp, layer):
                for n, (of, shape) in lists.items():
                    if of == layer:
                        dst = masks32 if n == "masks" else held[n]
                        sp.dma_start(dst.ap(), dram[n]).then_inc(loaded[layer], 16)

            def issue_loads(sp):
                for layer in (1, 2, 3):
                    if layer in PHASES:
                        load(sp, layer)

            g.issue_loads = issue_loads

            @block.sync
            def _(sp):
                load(sp, 0)
                if 0 in PHASES:
                    return
                issue_loads(sp)
                sp.dma_start(g.x_all[:, :, :], x_in.rearrange("b (c p) d -> p (b c) d", p=P)).then_inc(x_loaded, 16)

            @block.vector
            def _(dve):
                dve.wait_ge(loaded[0], n_loads[0])
                dve.tensor_copy(g.ident16[:, :], g.ident[:, :])
                dve.tensor_copy(masks16[:, :, :], masks32[:, :, :]).then_inc(consts_ready, 1)
                if 0 not in PHASES:
                    dve.wait_ge(x_loaded, 16)

        if 0 in PHASES:
            layer0(nc, g, B, x_in, scratch)
            with ExitStack() as c0:
                block = c0.enter_context(nc.Block())

                @block.sync
                def _(sp):
                    sp.dma_start(g.x_all[:, :, :], scratch.rearrange("b (c p) d -> p (b c) d", p=P)).then_inc(x_loaded, 16)
                    sp.wait_ge(x_loaded, 16)
        only0.close()
        if 1 in PHASES:
            layer1(nc, g, B)
        only1.close()
        if 2 in PHASES:
            layer2(nc, g, B)
        only2.close()
        if 3 in PHASES:
            layer3(nc, g, B, out)
            return
        with ExitStack() as c0:
            stored = c0.enter_context(nc.semaphore("stored"))
            block = c0.enter_context(nc.Block())

            @block.sync
            def _(sp):
                sp.dma_start(out.rearrange("b (c p) d -> p (b c) d", p=P), g.x_all[:, :, :]).then_inc(stored, 16)
                sp.wait_ge(stored, 16)


def slot_columns(wt):
    out = np.zeros((wt.shape[0], NH, SLOT), wt.dtype)
    out[:, :, :DH] = wt.reshape(wt.shape[0], NH, DH)
    return out.reshape(wt.shape[0], NG * P)


def columns(v, n=P):
    return np.ascontiguousarray(v.reshape(-1, n).T)


def rows(v):
    return np.ascontiguousarray(np.broadcast_to(v, (P, v.shape[-1])))


def shape_constants():
    c = {}
    c["ident"] = np.eye(P, dtype=np.float32)
    p = np.arange(P)
    c["one_row"] = (p % SLOT == DH).astype(np.float32)[:, None]
    c["iota"] = np.broadcast_to(np.arange(E, dtype=np.float32), (P, E)).copy()
    c["neg_half"] = np.full((P, 32), -0.5, np.float32)
    early, late = (p % TS)[None, :] < (p % TS)[:, None], (p % TS)[None, :] > (p % TS)[:, None]
    c["before0"], c["after0"] = early.astype(np.float32), late.astype(np.float32)
    start = 2.0 ** (-2.0 ** (-(math.log2(NH) - 3)))
    slopes = np.array([start * start ** i for i in range(NH)], np.float32)
    al = np.zeros((NG, GH, SLOT, S), np.float32)
    al[:, :, DH, :] = slopes.reshape(NG, GH)[:, :, None] * np.arange(S, dtype=np.float32)
    c["alibi"] = al.reshape(NG, P, S).transpose(1, 0, 2).copy()
    q, k = np.arange(P)[:, None], np.arange(P)[None, :]
    c["one_rows2"] = np.stack([(p % SLOT == DH + y) for y in range(WAYS)], 1).astype(np.float32)
    c["tri2"] = (q <= k).astype(np.float32)
    c["tri_back2"] = (q >= k).astype(np.float32)
    c["ones2"] = np.ones((P, P), np.float32)
    half = np.arange(0, LD, 2, dtype=np.float64)
    t = np.arange(S, dtype=np.float64)
    inv = (1.0 / 10000.0 ** (half / LD)).astype(np.float32).astype(np.float64)
    angle = (t[:, None] * inv[None, :]).astype(np.float32).astype(np.float64)
    grow = ((half + 0.4 * LD) / (1.4 * LD))[None, :] ** ((t - S // 2) / float(WINDOW // 2))[:, None]
    cos, sin = (np.concatenate([y, y], 1) for y in (np.cos(angle), np.sin(angle)))
    grow = np.concatenate([grow, grow], 1)
    sign = np.where(np.arange(LD) < LHALF, -1.0, 1.0)[None, :]
    rot = np.stack([8 * cos * grow, 8 * sign * sin * grow, cos / grow, sign * sin / grow]).astype(np.float32)
    c["rot2"] = rot.reshape(4, NC, P, LD).transpose(2, 0, 1, 3).reshape(P, 4, NC * LD)
    no = np.float32(NEG)
    causal = np.where(k <= q, 0, no)
    anti = np.where(k >= q, 0, no)
    zero = np.zeros((P, P))
    full = np.full((P, P), no)
    far = np.where(q + P - k <= 64, 0, no)
    near = np.where((k <= q) & (q - k <= 64), 0, no)
    c["masks"] = np.stack([np.concatenate(x, 1) for x in
                           ((causal, zero, causal), (anti, zero, anti), (near, far, near))], 1).astype(np.float32)
    return c


def kernel(**a):
    import concourse.bacc as _bacc
    from concourse.bass_utils import run_bass_kernel_spmd as _run

    a = {n: np.asarray(v) for n, v in a.items()}
    x = np.ascontiguousarray(a["L0_attn_x"])
    B = x.shape[0]
    arrays = shape_constants()
    w_kv, b_kv = a["L0_attn_Wkv"], a["L0_attn_bkv"]
    arrays.update(
        eta0=rows(a["L0_attn_eta"].reshape(1)), wv0=w_kv[D:].T, start0=a["L0_attn_W0"].T, lin0=a["L0_ffn_W_lin"].T,
        bv0=rows(b_kv[D:]), blin0=rows(a["L0_ffn_b_lin"]), gate0=a["L0_ffn_gate_w"].T,
        left0=a["L0_ffn_left"].transpose(1, 0, 2).reshape(D, E * LR), right0=a["L0_ffn_right"].reshape(E * LR, D),
    )
    w_in, b_in = a["L1_attn_w_in"], a["L1_attn_b_in"]
    arrays.update(
        q1=slot_columns(w_in[:, :D]), k1=slot_columns(w_in[:, D:2 * D]), v1=w_in[:, 2 * D:], out1=a["L1_attn_w_out"],
        bq1=columns(slot_columns(b_in[None, :D])[0]), bk1=columns(slot_columns(b_in[None, D:2 * D])[0]),
        bv1=rows(b_in[2 * D:]), bout1=rows(a["L1_attn_b_out"]), gate1=a["L1_ffn_gate_w"].T,
        up1=a["L1_ffn_w1"].transpose(2, 0, 1).reshape(D, E * HID),
        down1=a["L1_ffn_w2"].transpose(0, 2, 1).reshape(E * HC, P, D).transpose(1, 0, 2),
        bup1=columns(a["L1_ffn_b1"].reshape(-1)), bdown1=a["L1_ffn_b2"],
    )
    qs, ks = a["L2_ffn_q_scale"], a["L2_ffn_k_scale"]

    def swapped(t):
        return np.concatenate([t[:, LHALF:], t[:, :LHALF]], 1)

    def ffn_blocks(t, axis):
        pad = [(0, 0)] * t.ndim
        pad[axis] = (0, FC * P - FFN)
        return np.pad(t, pad)

    w1, b1 = a["L2_ffn_w1"], a["L2_ffn_b1"]
    arrays.update(
        q2=slot_columns(a["L2_attn_Wq"].T), k2=slot_columns(a["L2_attn_Wk"].T), v2w=a["L2_attn_Wv"].T,
        f2=a["L2_attn_Wf"].T, bf2=rows(a["L2_attn_bf"]),
        out2=a["L2_attn_Wo"].T.reshape(WAYS, P, D).transpose(1, 0, 2),
        scale_rows2=rows(np.stack([qs, swapped(qs), ks, swapped(ks)], 1).reshape(-1)),
        qkv2=a["L2_ffn_wqkv"].transpose(1, 0, 2), wo2=a["L2_ffn_wo"].reshape(DEPTH, IB, P, D).transpose(2, 0, 1, 3),
        ln2=np.stack([a["L2_ffn_ln_g"], a["L2_ffn_ln_b"]], 1).transpose(2, 0, 1),
        up2=np.stack([ffn_blocks(w1[:, :, :FFN], 2), ffn_blocks(w1[:, :, FFN:], 2)], 1).transpose(2, 0, 1, 3),
        bup2=np.stack([ffn_blocks(b1[:, :FFN], 1), ffn_blocks(b1[:, FFN:], 1)], 1)
        .reshape(DEPTH, 2, FC, P).transpose(3, 0, 1, 2),
        down2=ffn_blocks(a["L2_ffn_w2"], 1).reshape(DEPTH, FC, P, D).transpose(2, 0, 1, 3),
        bdown2=rows(a["L2_ffn_b2"].reshape(-1)),
    )
    arrays.update(
        gate3=a["L3_ffn_router_w"].T,
        q3=a["L3_attn_wq"].reshape(D, FB * P), k3=a["L3_attn_wk"].reshape(D, FB * P),
        v3=a["L3_attn_wv"].reshape(D, FB * P),
        bq3=columns(a["L3_attn_bq"].reshape(-1)), bk3=columns(a["L3_attn_bk"].reshape(-1)),
        bv3=columns(a["L3_attn_bv"].reshape(-1)),
        out3=a["L3_attn_wo"].reshape(FB, P, D).transpose(1, 0, 2), bout3=rows(a["L3_attn_bo"]),
        egate3=a["L3_ffn_gate_w"].transpose(2, 0, 1).reshape(D, E * HID),
        eup3=a["L3_ffn_up_w"].transpose(2, 0, 1).reshape(D, E * HID),
        edown3=a["L3_ffn_down_w"].transpose(0, 2, 1).reshape(E * HC, P, D).transpose(1, 0, 2),
    )
    nc = _bacc.Bacc("TRN2", target_bir_lowering=False, num_devices=1)
    feed, dram = {}, {}

    def given(name, arr):
        arr = np.ascontiguousarray(arr)
        feed[f"in_{name}"] = arr
        return nc.dram_tensor(f"in_{name}", arr.shape, mybir.dt.from_np(arr.dtype), kind="ExternalInput").ap()

    for name, (_, shape) in load_lists(B).items():
        dram[name] = given(name, arrays[name].reshape(shape))
    x_in = given("x", x)
    scratch = nc.dram_tensor("scratch", x.shape, FP32, kind="Internal").ap()
    out = nc.dram_tensor("out_x", x.shape, FP32, kind="ExternalOutput").ap()
    program(nc, dram, x_in, out, scratch, B)
    res = _run(nc, [feed], core_ids=[0])
    return res.results[0]["out_x"]
```

```python
import math
from contextlib import ExitStack

import numpy as np
import concourse.bass as bass
from concourse import mybir

FP32 = mybir.dt.float32
BF16 = mybir.dt.bfloat16
U32 = mybir.dt.uint32
ALU = mybir.AluOpType
ACT = mybir.ActivationFunctionType
AX = mybir.AxisListType

PHASES = (0, 1, 2, 3)

P = 128
D = 128
S = 256
NC = S // P
NH = 16
DH = D // NH
SLOT = 32
GH = P // SLOT
NG = NH // GH
E = 8
HID = 512
HC = HID // P
LN_EPS = 1e-5
AW = 3 * P
NEG = -1e30


class Chain:

    def __init__(self, eng, sem, rnd, n_per):
        self.eng, self.sem, self.rnd, self.n_per, self.n = eng, sem, rnd, n_per, 0

    def mark(self, ins):
        ins.then_inc(self.sem, 1)
        self.n += 1
        return self.n

    def wait(self, n):
        self.eng.wait_ge(self.sem, self.rnd * self.n_per + n)

    def hold(self, n, pad):
        self.wait(n)
        self.eng.memset(pad, 0.0)

    def __call__(self, ins):
        self.wait(self.mark(ins))

    def done(self):
        assert self.n == self.n_per, f"chain: {self.n} steps, declared {self.n_per}"


def pool_hold(pool, g, pad):
    pool.tensor_tensor(pad, g.neg_half[0:1, 0:1], g.neg_half[0:1, 0:1], ALU.mult)


class Banks:

    def __init__(self, banks, full, taken, uses):
        self.b, self.full, self.taken = banks, full, taken
        self.n, self.per = len(banks), uses // len(banks)
        assert uses % len(banks) == 0

    def open(self, pe):
        for t in self.taken:
            pe.sem_inc(t, 1)

    def fill(self, pe, rnd, k, after=()):
        for bank in range(self.n):
            js = [j for j in after if j % self.n == bank]
            if js and not (bank == k % self.n and max(js) <= k - self.n):
                self.wait_taken(pe, rnd, max(js))
        pe.wait_ge(self.taken[k % self.n], rnd * self.per + k // self.n + 1)
        return self.b[k % self.n]

    def filled(self, ins, k):
        ins.then_inc(self.full[k % self.n], 1)

    def read(self, eng, rnd, k):
        eng.wait_ge(self.full[k % self.n], rnd * self.per + k // self.n + 1)
        return self.b[k % self.n]

    def took(self, ins, k):
        ins.then_inc(self.taken[k % self.n], 1)

    def wait_taken(self, eng, rnd, k):
        eng.wait_ge(self.taken[k % self.n], rnd * self.per + k // self.n + 2)


class Names:
    pass


def chunks(ap, n=NC):
    return ap.rearrange("p (c d) -> p c d", c=n)


def over_chunks(row, n=NC):
    return row.unsqueeze(1).to_broadcast([P, n, row.shape[-1]])


def stat_buffers(sb, n):
    t = Names()
    t.stats = sb("stats", [P, n, 6])
    t.mv = sb("mean_var", [P, n, 2])
    t.pad = sb("norm_pad", [1, 1])
    t.var = sb("var", [P, n])
    t.rstd = sb("rstd", [P, n])
    return t


def norm_stats(dve, chain, x, t, n):
    for c in range(n):
        m = chain.mark(dve.bn_stats(t.stats[:, c, :], x[:, c, :]))
    chain.hold(m, t.pad[:, :])
    for c in range(n):
        m = chain.mark(dve.bn_aggr(t.mv[:, c, :], t.stats[:, c, :]))
    chain.wait(m)
    return dve.tensor_scalar(t.var[:, :], t.mv[:, :, 1], LN_EPS, None, ALU.add)


def norm_rstd(pool, g, t, n):
    return pool.tensor_tensor(t.rstd[:, :], t.var[:, :], g.neg_half[:, 0:n], ALU.pow)


def norm_apply(dve, x, xn, t, n):
    for c in range(n):
        last = dve.tensor_scalar(xn[:, c, :], x[:, c, :], t.mv[:, c, 0:1], t.rstd[:, c:c + 1],
                                 ALU.subtract, ALU.mult)
    return last


def router_buffers(sb, n):
    r = Names()
    r.pad = sb("r_pad", [1, 1])
    r.lg = sb("r_logits", [P, n, E])
    r.mx = sb("r_best", [P, n, 8])
    r.ix = sb("r_index", [P, n, 8], U32)
    r.ixf = sb("r_indexf", [P, n, 2])
    r.ls = sb("r_shifted", [P, n, E])
    r.ex = sb("r_exp", [P, n, E])
    r.mk = sb("r_first", [P, n, E])
    r.mk2 = sb("r_chosen", [P, n, E])
    r.cu = sb("r_kept", [P, n, E])
    r.den = sb("r_sum", [P, n])
    r.rden = sb("r_rsum", [P, n])
    r.comb = sb("r_comb", [P, n, E])
    return r


def router_rank(dve, chain, r, logits, n):
    chain.hold(chain.mark(dve.tensor_copy(r.lg[:, :, :], logits)), r.pad[:, :])
    for c in range(n):
        m = chain.mark(dve.max(r.mx[:, c, :], r.lg[:, c, :]))
    chain.hold(m, r.pad[:, :])
    for c in range(n):
        m = chain.mark(dve.max_index(r.ix[:, c, :], r.mx[:, c, :], r.lg[:, c, :]))
    chain.wait(m)
    chain(dve.tensor_copy(r.ixf[:, :, :], r.ix[:, :, 0:2]))
    return dve.tensor_tensor(r.ls[:, :, :], r.lg[:, :, :], r.mx[:, :, 0:1].to_broadcast([P, n, E]), ALU.subtract)


def router_mix(dve, chain, r, iota, n, over_all, scale=1.0):
    for c in range(n):
        m = chain.mark(dve.tensor_scalar(r.mk[:, c, :], iota[:, 0:E], r.ixf[:, c, 0:1], None, ALU.is_equal))
    chain.wait(m)
    for c in range(n):
        m = chain.mark(dve.scalar_tensor_tensor(out=r.mk2[:, c, :], in0=iota[:, 0:E], scalar=r.ixf[:, c, 1:2],
                                                in1=r.mk[:, c, :], op0=ALU.is_equal, op1=ALU.add))
    chain.wait(m)
    chain(dve.tensor_tensor(r.cu[:, :, :], r.mk2[:, :, :], r.ex[:, :, :], ALU.mult))
    chain(dve.reduce_sum(r.den[:, :], (r.ex if over_all else r.cu)[:, :, :], AX.X))
    chain(dve.reciprocal(r.rden[:, :], r.den[:, :]))
    return dve.scalar_tensor_tensor(out=r.comb[:, :, :], in0=r.cu[:, :, :], scalar=scale,
                                    in1=r.rden[:, :].unsqueeze(2).to_broadcast([P, n, E]),
                                    op0=ALU.mult, op1=ALU.mult)


ROUTER_STEPS = lambda n: (1 + 2 * n + 1) + (2 * n + 3)
NORM_STEPS = lambda n: 2 * n

FORWARD = dict(split=P, parts=((0, 0, 1), (1, 0, 2)))
BACKWARD = dict(split=2 * P, parts=((0, 0, 2), (1, 1, 1)))


def pe_scores(pe, g, bank, q, k, mask, way):
    pe.matmul(bank[:, 0:AW], g.ident16[:, :], mask[:, :], start=True, stop=False, skip_group_check=True)
    at = 0
    for c, k0, n in way["parts"]:
        last = pe.matmul(bank[:, at:at + n * P], q[:, c * P:(c + 1) * P], k[:, k0 * P:(k0 + n) * P],
                         start=False, stop=(c == 1), skip_group_check=True)
        at += n * P
    return last


def pe_transpose3(pe, g, bank, probs):
    for j in range(3):
        last = pe.transpose(bank[:, j * P:(j + 1) * P], probs[:, j * P:(j + 1) * P], g.ident[:, :])
    return last


def pe_values(pe, outs, probsT, v, way):
    j = 0
    for c, k0, n in way["parts"]:
        for i in range(n):
            last = pe.matmul(outs[c], probsT[:, j * P:(j + 1) * P], v[:, k0 + i, :],
                             start=(i == 0), stop=(i == n - 1))
            j += 1
    return last


def dve_negmax(dve, bank, negmax, way):
    s = way["split"]
    dve.tensor_reduce(negmax[:, 0:1], bank[:, 0:s], AX.X, ALU.max, negate=True)
    return dve.tensor_reduce(negmax[:, 1:2], bank[:, s:AW], AX.X, ALU.max, negate=True)


def act_probs(act, bank, negmax, probs, sums, way):
    s = way["split"]
    act.activation(probs[:, 0:s], bank[:, 0:s], ACT.Exp, bias=negmax[:, 0:1], accum_out=sums[0])
    return act.activation(probs[:, s:AW], bank[:, s:AW], ACT.Exp, bias=negmax[:, 1:2], accum_out=sums[1])


TS = 8
RC = 4
LR = 4


ORDER = ["load", ("r", 0), "norm", ("e", 0), "xnt", ("u", 0), "gram", ("r", 1), "logit", ("e", 1), "n2", ("u", 1), "n4",
         ("r", 2), "s2", ("e", 2), "mix", ("u", 2), "lowT", ("r", 3), "at", ("e", 3), ("u", 3), "rest"]
PREPARE = [x for x in ORDER if isinstance(x, str)]


def layer0(nc, g, B, x_in, scratch):
    assert B * TS == P
    w = g.w
    rounds = S // TS // RC
    with ExitStack() as ctx:
        def sb(name, shape, dt=FP32):
            return ctx.enter_context(nc.sbuf_tensor("l0_" + name, shape, dt))

        def sem(name):
            return ctx.enter_context(nc.semaphore("l0_" + name))

        x0 = g.x_all
        xs = sb("xs", [P, RC, D])
        xn = sb("xn", [P, 2, RC, D])
        xnT = sb("xnT", [P, 2, RC, P])
        st = stat_buffers(sb, RC)
        r = router_buffers(sb, RC)
        neg_c = sb("neg_c", [P, 1])
        before, after = w["before0"], w["after0"]
        N1, N1T, N2, N2T = (sb(n, [P, RC, P]) for n in ("n1", "n1t", "n2", "n2t"))
        N4 = N1T
        S1, S2 = (sb(n, [P, RC, P]) for n in ("s1", "s2"))
        AT = sb("at", [P, 2, RC, P])
        w_sum, b_sum = w["lin0"], w["blin0"]
        U = sb("U", [P, D])
        low = sb("low", [P, RC, E * LR])
        lowT = sb("lowT", [E * LR, RC, P])
        rest = sb("rest", [P, RC, D])
        rs = sb("rs", [P, 2, D])
        err = sb("err", [P, 2, D])
        y = sb("y", [P, RC, D])
        y_pad = sb("y_pad", [1, 1])

        A_XNT, A_GRAM, A_LOGIT, A_N2, A_N2T, A_N4, A_S2, A_LOWT, A_AT, A_REST = range(10)
        G = Banks(g.bank[0:5], [sem(f"g_full{i}") for i in range(5)], [sem(f"g_taken{i}") for i in range(5)], 10)
        bank_r, bank_e, bank_u = g.bank[5:8]

        x_loaded = sem("x_loaded")
        setup_done = sem("setup_done")
        var_ready = sem("var_ready")
        rstd_ready = sem("rstd_ready")
        xn_ready = sem("xn_ready")
        gate_exp = sem("gate_exp")
        low_ready = sem("low_ready")
        s1_ready = sem("s1_ready")
        r_full = sem("r_full")
        rs_ready = sem("rs_ready")
        e_full = sem("e_full")
        err_ready = sem("err_ready")
        u_full = sem("u_full")
        u_ready = sem("u_ready")
        y_ready = sem("y_ready")
        stored = sem("stored")
        dve_chain = sem("dve_chain")
        y_chain = sem("y_chain")
        n_chain = 1 + NORM_STEPS(RC) + ROUTER_STEPS(RC) + 3

        block = ctx.enter_context(nc.Block())

        @block.sync
        def _(sp):
            for b in range(B):
                sp.dma_start(x0[b * TS:(b + 1) * TS, 0:S // TS, :],
                             x_in[b].rearrange("(c t) d -> t c d", t=TS)).then_inc(x_loaded, 16)
            g.issue_loads(sp)
            sp.sem_inc(stored, 16 * B)
            with sp.Fori(0, rounds) as rd:
                sp.wait_ge(y_ready, rd + 1)
                for b in range(B):
                    sp.dma_start(scratch[b, bass.ds(rd * (RC * TS), RC * TS), :].rearrange("(c t) d -> t c d", t=TS),
                                 y[b * TS:(b + 1) * TS, :, :]).then_inc(stored, 16)
            sp.wait_ge(stored, 16 * B * (rounds + 1))

        @block.tensor
        def _(pe):
            g.wait_consts(pe)
            pe.wait_ge(setup_done, 1)
            G.open(pe)

            def prepare(rd, buf):
                xt = xnT[:, buf, :, :]

                def each(k, lhs, rhs, width=P):
                    b = G.fill(pe, rd, k)
                    for j in range(RC):
                        last = pe.matmul(b[:, j * width:(j + 1) * width], lhs(j), rhs(j), start=True, stop=True)
                    G.filled(last, k)

                def xnt():
                    pe.wait_ge(xn_ready, rd + 1)
                    b = G.fill(pe, rd, A_XNT)
                    for j in range(RC):
                        last = pe.transpose(b[:, j * P:(j + 1) * P], xn[:, buf, j, :], g.ident[:, :])
                    G.filled(last, A_XNT)

                def gram():
                    G.wait_taken(pe, rd, A_XNT)
                    each(A_GRAM, lambda j: xt[:, j, :], lambda j: xt[:, j, :])

                def logit():
                    b = G.fill(pe, rd, A_LOGIT)
                    for j in range(RC):
                        pe.matmul(b[:, j * E:(j + 1) * E], xt[:, j, :], w["gate0"][:, :], start=True, stop=True)
                        last = pe.matmul(b[:, RC * E + j * E * LR:RC * E + (j + 1) * E * LR], xt[:, j, :],
                                         w["left0"][:, :], start=True, stop=True)
                    G.filled(last, A_LOGIT)

                def n2():
                    G.wait_taken(pe, rd, A_GRAM)
                    each(A_N2, lambda j: N1T[:, j, :], lambda j: N1[:, j, :])
                    each(A_N2T, lambda j: N1[:, j, :], lambda j: N1T[:, j, :])

                def n4():
                    G.wait_taken(pe, rd, A_N2)
                    G.wait_taken(pe, rd, A_N2T)
                    pe.wait_ge(s1_ready, rd + 1)
                    each(A_N4, lambda j: N2T[:, j, :], lambda j: N2[:, j, :])

                def s2():
                    each(A_S2, lambda j: N2[:, j, :], lambda j: S1[:, j, :])

                def lowT_():
                    pe.wait_ge(low_ready, rd + 1)
                    b = G.fill(pe, rd, A_LOWT)
                    for j in range(RC):
                        last = pe.transpose(b[0:E * LR, j * P:(j + 1) * P], low[:, j, :], g.ident[:, :])
                    G.filled(last, A_LOWT)

                def at():
                    G.wait_taken(pe, rd, A_N4)
                    G.wait_taken(pe, rd, A_S2)
                    each(A_AT, lambda j: N4[:, j, :], lambda j: S2[:, j, :])

                def rest_():
                    G.wait_taken(pe, rd, A_LOWT)
                    b = G.fill(pe, rd, A_REST)
                    for j in range(RC):
                        pe.matmul(b[:, j * P:(j + 1) * P], xt[:, j, :], w_sum[:, :], start=True, stop=False)
                        last = pe.matmul(b[:, j * P:(j + 1) * P], lowT[:, j, :], w["right0"][:, :], start=False, stop=True)
                    G.filled(last, A_REST)

                return dict(xnt=xnt, gram=gram, logit=logit, n2=n2, n4=n4, s2=s2, lowT=lowT_, at=at, rest=rest_)

            def chain(rd, buf):
                def r_(j):
                    pe.wait_ge(u_ready, rd * RC + j + 1)
                    pe.matmul(bank_r[:, 0:D], xnT[:, buf, j, :], U[:, :], start=True, stop=True).then_inc(r_full, 1)

                def e_(j):
                    pe.wait_ge(rs_ready, rd * RC + j + 1)
                    pe.matmul(bank_e[:, 0:D], AT[:, buf, j, :], rs[:, j % 2, :], start=True, stop=True).then_inc(e_full, 1)

                def u_(j):
                    pe.wait_ge(err_ready, rd * RC + j + 1)
                    pe.matmul(bank_u[:, 0:D], xn[:, buf, j, :], err[:, j % 2, :], start=True, stop=True).then_inc(u_full, 1)

                return dict(r=r_, e=e_, u=u_)

            first = prepare(0, 0)
            for x in PREPARE:
                if x in first:
                    first[x]()
            G.wait_taken(pe, 0, A_AT)
            with pe.Fori(0, rounds // 2) as pair:
                for h in range(2):
                    rd = pair * 2 + h
                    own, ahead = chain(rd, h), prepare(rd + 1, 1 - h)
                    for x in ORDER:
                        if isinstance(x, tuple):
                            own[x[0]](x[1])
                        elif x in ahead:
                            ahead[x]()
                    G.wait_taken(pe, rd + 1, A_AT)

        @block.gpsimd
        def _(pool):
            g.wait_layer(pool, 0)
            with pool.Fori(0, rounds + 1) as rd:
                pool.wait_ge(var_ready, rd + 1)
                norm_rstd(pool, g, st, RC).then_inc(rstd_ready, 1)

        @block.scalar
        def _(act):
            with act.Fori(0, rounds + 1) as rd:
                G.wait_taken(act, rd, A_LOGIT)
                act.activation(r.ex[:, :, :], r.ls[:, :, :], ACT.Exp).then_inc(gate_exp, 1)
                b = G.read(act, rd, A_N2T)
                G.took(act.activation(N2T[:, :, :], chunks(b[:, :], RC), ACT.Copy), A_N2T)
                b = G.read(act, rd, A_N4)
                G.took(act.activation(N4[:, :, :], chunks(b[:, :], RC), ACT.Copy), A_N4)

        @block.vector
        def _(dve):
            g.wait_consts(dve)
            dve.tensor_scalar(neg_c[:, :], w["eta0"][:, :], -2.0 / (B * D), None, ALU.mult).then_inc(setup_done, 1)
            dve.wait_ge(setup_done, 1)
            dve.tensor_scalar(before[:, :], w["before0"][:, :], neg_c[:, 0:1], None, ALU.mult)
            dve.tensor_scalar(after[:, :], w["after0"][:, :], neg_c[:, 0:1], None, ALU.mult)
            dve.tensor_tensor(w_sum[:, :], w["wv0"][:, :], w["lin0"][:, :], ALU.add)
            dve.tensor_tensor(b_sum[:, :], w["bv0"][:, :], w["blin0"][:, :], ALU.add)
            dve.tensor_tensor(U[:, :], w["start0"][:, :], w["wv0"][:, :], ALU.subtract).then_inc(u_ready, 1)
            dve.wait_ge(u_ready, 1)
            dve.wait_ge(x_loaded, 16 * B)

            def prepare(rd, buf):
                ch = Chain(dve, dve_chain, rd, n_chain)

                def load():
                    ch(dve.tensor_copy(xs[:, :, :], x0[:, bass.ds(rd * RC, RC), :]))
                    norm_stats(dve, ch, xs, st, RC).then_inc(var_ready, 1)

                def norm():
                    dve.wait_ge(rstd_ready, rd + 1)
                    norm_apply(dve, xs, xn[:, buf, :, :], st, RC).then_inc(xn_ready, 1)

                def xnt():
                    b = G.read(dve, rd, A_XNT)
                    G.took(dve.tensor_copy(xnT[:, buf, :, :], chunks(b[:, :], RC)), A_XNT)

                def gram():
                    b = G.read(dve, rd, A_GRAM)
                    dve.tensor_tensor(N1T[:, :, :], chunks(b[:, :], RC), over_chunks(after[:, :], RC), ALU.mult)
                    G.took(dve.tensor_tensor(N1[:, :, :], chunks(b[:, :], RC), over_chunks(before[:, :], RC), ALU.mult),
                           A_GRAM)

                def logit():
                    b = G.read(dve, rd, A_LOGIT)
                    ch(router_rank(dve, ch, r, b[:, 0:RC * E].rearrange("p (c e) -> p c e", e=E), RC))
                    G.took(dve.tensor_copy(low[:, :, :], b[:, RC * E:RC * E * (1 + LR)].rearrange(
                        "p (c k) -> p c k", c=RC)), A_LOGIT)
                    G.wait_taken(dve, rd, A_GRAM)
                    dve.tensor_tensor(S1[:, :, :], N1T[:, :, :], over_chunks(g.ident[:, :], RC), ALU.add).then_inc(s1_ready, 1)

                def n2():
                    b = G.read(dve, rd, A_N2)
                    G.took(dve.tensor_copy(N2[:, :, :], chunks(b[:, :], RC)), A_N2)

                def s2():
                    b = G.read(dve, rd, A_S2)
                    dve.wait_ge(s1_ready, rd + 1)
                    G.took(dve.tensor_tensor(S2[:, :, :], chunks(b[:, :], RC), S1[:, :, :], ALU.add), A_S2)

                def mix():
                    dve.wait_ge(gate_exp, rd + 1)
                    ch(router_mix(dve, ch, r, g.iota, RC, True))
                    G.wait_taken(dve, rd, A_LOGIT)
                    dve.tensor_tensor(low[:, :, :].rearrange("p c (e k) -> p (c e) k", k=LR),
                                      low[:, :, :].rearrange("p c (e k) -> p (c e) k", k=LR),
                                      r.comb[:, :, :].rearrange("p c e -> p (c e)").unsqueeze(2).to_broadcast(
                                          [P, RC * E, LR]), ALU.mult).then_inc(low_ready, 1)

                def lowT_():
                    b = G.read(dve, rd, A_LOWT)
                    G.took(dve.tensor_copy(lowT[:, :, :], chunks(b[0:E * LR, :], RC)), A_LOWT)

                def at():
                    b = G.read(dve, rd, A_AT)
                    G.wait_taken(dve, rd, A_S2)
                    G.took(dve.tensor_tensor(AT[:, buf, :, :], chunks(b[:, :], RC), S2[:, :, :], ALU.add), A_AT)

                def rest_():
                    b = G.read(dve, rd, A_REST)
                    G.took(dve.tensor_tensor(rest[:, :, :], chunks(b[:, :], RC), over_chunks(b_sum[:, :], RC), ALU.add), A_REST)
                    G.wait_taken(dve, rd, A_REST)
                    ch(dve.tensor_tensor(rest[:, :, :], rest[:, :, :], xs[:, :, :], ALU.add))
                    ch.done()

                return dict(load=load, norm=norm, xnt=xnt, gram=gram, logit=logit, n2=n2, s2=s2, mix=mix, lowT=lowT_,
                            at=at, rest=rest_)

            def chain(rd, buf):
                ch = Chain(dve, y_chain, rd, RC)

                def r_(j):
                    dve.wait_ge(r_full, rd * RC + j + 1)
                    dve.tensor_tensor(rs[:, j % 2, :], bank_r[:, 0:D], w["bv0"][:, :], ALU.subtract).then_inc(rs_ready, 1)

                def e_(j):
                    dve.wait_ge(e_full, rd * RC + j + 1)
                    dve.tensor_copy(err[:, j % 2, :], bank_e[:, 0:D]).then_inc(err_ready, 1)

                def u_(j):
                    if j == 0:
                        dve.wait_ge(stored, (rd + 1) * (16 * B))
                    dve.wait_ge(err_ready, rd * RC + j + 1)
                    ch.mark(dve.tensor_tensor(y[:, j, :], rest[:, j, :], err[:, j % 2, :], ALU.add))
                    dve.wait_ge(u_full, rd * RC + j + 1)
                    dve.wait_ge(u_ready, rd * RC + j + 1)
                    dve.scalar_tensor_tensor(out=U[:, :], in0=bank_u[:, 0:D], scalar=neg_c[:, 0:1], in1=U[:, :],
                                             op0=ALU.mult, op1=ALU.add).then_inc(u_ready, 1)
                    if j == RC - 1:
                        ch.wait(ch.n)
                        dve.memset(y_pad[:, :], 0.0).then_inc(y_ready, 1)
                        ch.done()

                return dict(r=r_, e=e_, u=u_)

            first = prepare(0, 0)
            for x in PREPARE:
                if x in first:
                    first[x]()
            with dve.Fori(0, rounds // 2) as pair:
                for h in range(2):
                    rd = pair * 2 + h
                    own, ahead = chain(rd, h), prepare(rd + 1, 1 - h)
                    for x in ORDER:
                        if isinstance(x, tuple):
                            own[x[0]](x[1])
                        elif x in ahead:
                            ahead[x]()




def layer1(nc, g, B):
    w = g.w
    with ExitStack() as ctx:
        def sb(name, shape, dt=FP32):
            return ctx.enter_context(nc.sbuf_tensor("l1_" + name, shape, dt))

        def sem(name):
            return ctx.enter_context(nc.semaphore("l1_" + name))

        xt = sb("xt", [P, NC, D])
        x_next = sb("x_next", [P, NC, D])
        xn = sb("xn", [P, NC, D])
        xnT = sb("xnT", [P, S])
        st = stat_buffers(sb, NC)
        qT = sb("qT", [P, NG, S])
        kT = sb("kT", [P, NG, S])
        v = sb("v", [P, NC, D])
        negmax = sb("negmax", [P, 2, NC])
        probs = sb("probs", [P, 2, AW])
        probsT = sb("probsT", [P, 2, AW])
        rowsum = sb("rowsum", [P, NC, NH])
        rrow = sb("rrow", [P, NC, NH])
        on = sb("on", [P, NC, D])
        oT = sb("oT", [P, S])
        hT = sb("hT", [P, 2, HC, S])
        combT = sb("combT", [E, S])
        qbias = sb("qbias", [P, NG])
        kconst = sb("kconst", [P, NG, S])
        r = router_buffers(sb, NC)

        Sb, Tb, Ob = g.bank[0:2], g.bank[2:4], g.bank[6]
        Db = g.bank[7]
        G_Q, G_K, G_V, G_UP = 0, 2, 4, 6
        G = Banks(g.bank[4:6], [sem("g_full0"), sem("g_full1")], [sem("g_taken0"), sem("g_taken1")], G_UP + 2 * E)

        setup_done = sem("setup_done")
        var_ready = sem("var_ready")
        rstd_ready = sem("rstd_ready")
        xn_ready = sem("xn_ready")
        xnT_full = sem("xnT_full")
        xnT_ready = sem("xnT_ready")
        logits_ready = sem("logits_ready")
        ranked = sem("ranked")
        gate_exp = sem("gate_exp")
        comb_ready = sem("comb_ready")
        scores_ready = sem("scores_ready")
        negmax_ready = sem("negmax_ready")
        probs_ready = sem("probs_ready")
        transposed = sem("transposed")
        probsT_ready = sem("probsT_ready")
        heads_summed = sem("heads_summed")
        on_ready = sem("on_ready")
        oT_full = sem("oT_full")
        oT_ready = sem("oT_ready")
        out_full = sem("out_full")
        out_used = sem("out_used")
        down_ready = sem("down_ready")
        down_used = sem("down_used")
        dve_chain = sem("dve_chain")
        norm_chain = sem("norm_chain")
        n_chain = 1 + ROUTER_STEPS(NC) + 2

        block = ctx.enter_context(nc.Block())

        @block.tensor
        def _(pe):
            g.wait_consts(pe)
            g.wait_layer(pe, 1)
            G.open(pe)
            pe.sem_inc(down_used, 1)
            pe.sem_inc(out_used, 1)
            def projections(n):
                pe.wait_ge(xn_ready, n + 1)
                pe.wait_ge(down_used, n * E + 1)
                for c in range(NC):
                    last = pe.transpose(Db[:, c * P:(c + 1) * P], xn[:, c, :], g.ident[:, :])
                last.then_inc(xnT_full, 1)
                if not isinstance(n, int):
                    transposed_output(n - 1)
                pe.wait_ge(xnT_ready, n + 1)
                for k0, wt in ((G_Q, w["q1"]), (G_K, w["k1"])):
                    for u in range(2):
                        b = G.fill(pe, n, k0 + u)
                        for j in range(2):
                            gg = 2 * u + j
                            last = pe.matmul(b[:, j * S:(j + 1) * S], wt[:, gg * P:(gg + 1) * P], xnT[:, :],
                                             start=True, stop=True)
                        G.filled(last, k0 + u)
                for c in range(NC):
                    b = G.fill(pe, n, G_V + c)
                    G.filled(pe.matmul(b[:, 0:P], xnT[:, c * P:(c + 1) * P], w["v1"][:, :], start=True, stop=True),
                             G_V + c)
                for c in range(NC):
                    last = pe.matmul(Db[:, c * E:(c + 1) * E], xnT[:, c * P:(c + 1) * P], w["gate1"][:, :],
                                     start=True, stop=True)
                last.then_inc(logits_ready, 1)

            def transposed_output(it):
                pe.wait_ge(comb_ready, it + 1)
                pe.wait_ge(on_ready, it + 1)
                for c in range(NC):
                    pe.transpose(Tb[0][0:E, S + c * P:S + (c + 1) * P], r.comb[:, c, :], g.ident[:, :])
                    last = pe.transpose(Tb[0][:, c * P:(c + 1) * P], on[:, c, :], g.ident[:, :])
                last.then_inc(oT_full, 1)

            projections(0)
            with pe.Fori(0, B) as it:
                G.wait_taken(pe, it, G_V)
                G.wait_taken(pe, it, G_V + 1)
                for s in range(NH + 2):
                    e = s // 2
                    if s < NH:
                        rows, gg = slice(SLOT * (s % GH), SLOT * (s % GH + 1)), s // GH
                        pe_scores(pe, g, Sb[s % 2], qT[rows, gg, :], kT[rows, gg, :], g.mask_causal,
                                  FORWARD).then_inc(scores_ready, 1)
                        if s % 2 == 0:
                            for u in range(2):
                                k = G_UP + 2 * e + u
                                b = G.fill(pe, it, k)
                                for j in range(2):
                                    h = (e * HC + 2 * u + j) * P
                                    last = pe.matmul(b[:, j * S:(j + 1) * S], w["up1"][:, h:h + P], xnT[:, :],
                                                     start=True, stop=True)
                                G.filled(last, k)
                        else:
                            G.wait_taken(pe, it, G_UP + 2 * e)
                            G.wait_taken(pe, it, G_UP + 2 * e + 1)
                            pe.wait_ge(down_used, it * E + e + 1)
                            if e == 0:
                                pe.wait_ge(ranked, it + 1)
                            for c in range(NC):
                                for j in range(HC):
                                    last = pe.matmul(Db[:, c * P:(c + 1) * P], hT[:, e % 2, j, c * P:(c + 1) * P],
                                                     w["down1"][:, e * HC + j, :], start=(j == 0), stop=(j == HC - 1))
                            last.then_inc(down_ready, 1)
                    if s >= 2:
                        h = s - 2
                        pe.wait_ge(probsT_ready, it * NH + h + 1)
                        last = pe_values(pe, [Ob[:, c * D + h * DH:c * D + (h + 1) * DH] for c in range(NC)],
                                         probsT[:, h % 2, :], v[:, :, h * DH:(h + 1) * DH], FORWARD)
                        if h == NH - 1:
                            last.then_inc(heads_summed, 1)
                    if 1 <= s <= NH:
                        h = s - 1
                        pe.wait_ge(probs_ready, it * NH + h + 1)
                        if h == 1:
                            pe.wait_ge(out_used, it + 1)
                        pe_transpose3(pe, g, Tb[h % 2], probs[:, h % 2, :]).then_inc(transposed, 1)
                projections(it + 1)
                pe.wait_ge(oT_ready, it + 1)
                for c in range(NC):
                    pe.matmul(Tb[1][:, c * P:(c + 1) * P], oT[:, c * P:(c + 1) * P], w["out1"][:, :], start=True, stop=False)
                    last = pe.matmul(Tb[1][:, c * P:(c + 1) * P], combT[:, c * P:(c + 1) * P], w["bdown1"][:, :],
                                     start=False, stop=True)
                last.then_inc(out_full, 1)

        @block.gpsimd
        def _(pool):
            g.wait_layer(pool, 0)
            with pool.Fori(0, B + 1) as n:
                pool.wait_ge(var_ready, n + 1)
                norm_rstd(pool, g, st, NC).then_inc(rstd_ready, 1)

        @block.scalar
        def _(act):
            g.wait_layer(act, 1)
            act.wait_ge(setup_done, 1)
            def queries(n):
                for u in range(2):
                    b = G.read(act, n, G_Q + u)
                    for j in range(2):
                        gg = 2 * u + j
                        last = act.activation(qT[:, gg, :], b[:, j * S:(j + 1) * S], ACT.Identity,
                                              bias=qbias[:, gg:gg + 1], scale=DH ** -0.5)
                    G.took(last, G_Q + u)

            queries(0)
            with act.Fori(0, B) as it:
                for s in range(NH):
                    act.wait_ge(negmax_ready, it * NH + s + 1)
                    act_probs(act, Sb[s % 2], negmax[:, s % 2, :], probs[:, s % 2, :],
                              [rowsum[:, c, s:s + 1] for c in range(NC)], FORWARD).then_inc(probs_ready, 1)
                    if s % 2 == 0:
                        e = s // 2
                        b = G.read(act, it, G_UP + 2 * e)
                        for j in range(2):
                            h = e * HC + j
                            last = act.activation(hT[:, e % 2, j, :], b[:, j * S:(j + 1) * S], ACT.Relu,
                                                  bias=w["bup1"][:, h:h + 1])
                        G.took(last, G_UP + 2 * e)
                    if s == 0:
                        act.wait_ge(ranked, it + 1)
                        act.activation(r.ex[:, :, :], r.ls[:, :, :], ACT.Exp).then_inc(gate_exp, 1)
                queries(it + 1)

        @block.vector
        def _(dve):
            g.wait_consts(dve)
            g.wait_layer(dve, 1)
            for gg in range(NG):
                dve.tensor_scalar(qbias[:, gg:gg + 1], w["bq1"][:, gg:gg + 1], DH ** -0.5, g.one_row[:, 0:1],
                                  ALU.mult, ALU.add)
                last = dve.tensor_scalar(kconst[:, gg, :], g.alibi[:, gg, :], w["bk1"][:, gg:gg + 1], None, ALU.add)
            last.then_inc(setup_done, 1)
            dve.wait_ge(setup_done, 1)
            def next_stats(n):
                ch = Chain(dve, norm_chain, n, 1 + NORM_STEPS(NC))
                ch(dve.tensor_copy(x_next[:, :, :], g.x_all[:, bass.ds(n * NC, NC), :]))
                norm_stats(dve, ch, x_next, st, NC).then_inc(var_ready, 1)
                ch.done()

            def next_norm(n):
                dve.wait_ge(rstd_ready, n + 1)
                norm_apply(dve, x_next, xn, st, NC).then_inc(xn_ready, 1)

            def next_xnT(n):
                dve.wait_ge(xnT_full, n + 1)
                dve.tensor_copy(xnT[:, :], Db[:, 0:S]).then_inc(xnT_ready, 1)

            def keys_values(n):
                for u in range(2):
                    b = G.read(dve, n, G_K + u)
                    G.took(dve.tensor_tensor(kT[:, 2 * u:2 * u + 2, :], chunks(b[:, :]),
                                             kconst[:, 2 * u:2 * u + 2, :], ALU.add), G_K + u)
                for c in range(NC):
                    b = G.read(dve, n, G_V + c)
                    G.took(dve.tensor_tensor(v[:, c, :], b[:, 0:P], w["bv1"][:, :], ALU.add), G_V + c)

            for part in (next_stats, next_norm, next_xnT, keys_values):
                part(0)
            with dve.Fori(0, B) as it:
                ch = Chain(dve, dve_chain, it, n_chain)
                ch(dve.tensor_copy(xt[:, :, :], x_next[:, :, :]))
                for s in range(NH + 1):
                    e = s // 2
                    if s < NH:
                        dve.wait_ge(scores_ready, it * NH + s + 1)
                        dve_negmax(dve, Sb[s % 2], negmax[:, s % 2, :], FORWARD).then_inc(negmax_ready, 1)
                        if s % 2 == 0:
                            b = G.read(dve, it, G_UP + 2 * e + 1)
                            for j in range(2):
                                h = e * HC + 2 + j
                                last = dve.tensor_scalar(hT[:, e % 2, 2 + j, :], b[:, j * S:(j + 1) * S],
                                                         w["bup1"][:, h:h + 1], 0.0, ALU.add, ALU.max)
                            G.took(last, G_UP + 2 * e + 1)
                    if s == 0:
                        dve.wait_ge(logits_ready, it + 1)
                        router_rank(dve, ch, r, Db[:, 0:NC * E].rearrange("p (c e) -> p c e", e=E),
                                    NC).then_inc(ranked, 1)
                    if s == 1:
                        dve.wait_ge(gate_exp, it + 1)
                        router_mix(dve, ch, r, g.iota, NC, False).then_inc(comb_ready, 1)
                        dve.wait_ge(comb_ready, it + 1)
                    if s >= 1:
                        dve.wait_ge(transposed, it * NH + s)
                        dve.tensor_copy(probsT[:, (s - 1) % 2, :], Tb[(s - 1) % 2][:, 0:AW]).then_inc(probsT_ready, 1)
                    if s < NH and s % 2 == 1:
                        dve.wait_ge(down_ready, it * E + e + 1)
                        if e:
                            dve.wait_ge(down_used, it * E + e + 1)
                        dve.scalar_tensor_tensor(out=xt[:, 0, :], in0=Db[:, 0:D], scalar=r.comb[:, 0, e:e + 1],
                                                 in1=xt[:, 0, :], op0=ALU.mult, op1=ALU.add)
                        dve.scalar_tensor_tensor(out=xt[:, 1, :], in0=Db[:, D:2 * D], scalar=r.comb[:, 1, e:e + 1],
                                                 in1=xt[:, 1, :], op0=ALU.mult, op1=ALU.add).then_inc(down_used, 1)
                    if s == NH - 4:
                        next_stats(it + 1)
                    if s == NH - 3:
                        next_norm(it + 1)
                next_xnT(it + 1)
                dve.wait_ge(heads_summed, it + 1)
                ch(dve.reciprocal(rrow[:, :, :], rowsum[:, :, :]))
                for c in range(NC):
                    last = dve.tensor_tensor(on[:, c, :].rearrange("p (h d) -> p h d", h=NH),
                                             Ob[:, c * D:(c + 1) * D].rearrange("p (h d) -> p h d", h=NH),
                                             rrow[:, c, :].unsqueeze(2).to_broadcast([P, NH, DH]), ALU.mult)
                last.then_inc(on_ready, 1)
                dve.wait_ge(oT_full, it + 1)
                dve.tensor_copy(oT[:, :], Tb[0][:, 0:S])
                dve.tensor_copy(combT[:, :], Tb[0][0:E, S:2 * S]).then_inc(oT_ready, 1)
                keys_values(it + 1)
                dve.wait_ge(out_full, it + 1)
                dve.wait_ge(down_used, it * E + E + 1)
                dve.tensor_tensor(xt[:, :, :], xt[:, :, :], chunks(Tb[1][:, 0:S]), ALU.add).then_inc(out_used, 1)
                dve.wait_ge(out_used, it + 2)
                ch(dve.tensor_tensor(g.x_all[:, bass.ds(it * NC, NC), :], xt[:, :, :], over_chunks(w["bout1"][:, :]), ALU.add))
                ch.done()


LH = 8
LD = 64
LHALF = LD // 2
INNER = LH * LD
IB = INNER // P
FFN = int(D * 4 * 2 / 3)
FC = -(-FFN // P)
WINDOW = 64
DEPTH = 2
WAYS = 2
UNITS = WAYS * NH + DEPTH * LH


def attention_order():
    wide = [("wide", i) for i in range(WAYS * NH)]
    order = []
    for l, (before, between) in enumerate(((4, 1), (18, 1))):
        order += [wide.pop(0) for _ in range(before)] + [("local", l, h) for h in range(LH // 2)]
        order += [wide.pop(0) for _ in range(between)] + [("local", l, h) for h in range(LH // 2, LH)]
    return order + wide


UNIT_ORDER = attention_order()
LAG = 3
STEPS = UNITS + LAG

PROLOGUE = [("xnT", ), ("gates", ), ("qk", 0, 0), ("qk", 0, 1), ("wide_q", 0), ("wide_q", 1), ("wide_v", ),
            ("cumulate", ), ("qk", 0, 2), ("wide_k", 0), ("wide_k", 1)]
WIDE_USES = {name: k for k, name in enumerate(x for x in PROLOGUE if x[0] in ("wide_q", "wide_k", "wide_v", "cumulate"))}


def local_tail(l, t):
    return {t: [("local_norm", l, 1)], t + 1: [("local_o", l, 1)], t + 2: [("local_out", l)],
            t + 3: [("shift", l, 1)], t + 4: [("back", l)], t + 5: [("norm", l)],
            t + 6: [("normed", l), ("up", l, 0)], t + 7: [("up", l, 1), ("up", l, 2)]}


BESIDE = {0: [("qk", 0, 3)], 1: [("local_v", 0, 0), ("qk_t", 0, 0)], 2: [("local_v", 0, 1), ("qk_t", 0, 1)], 3: [("qk_t", 0, 2), ("qk_t", 0, 3)],
          11: [("local_norm", 0, 0)], 12: [("local_o", 0, 0)],
          **local_tail(0, 16), 24: [("down", 0)], 25: [("shift", 1, 0), ("qk", 1, 0)], 26: [("qk", 1, 1), ("qk", 1, 2)],
          27: [("qk", 1, 3), ("local_v", 1, 0)], 28: [("local_v", 1, 1)],
          29: [("qk_t", 1, 0), ("qk_t", 1, 1)], 30: [("qk_t", 1, 2), ("qk_t", 1, 3)],
          38: [("local_norm", 1, 0)], 39: [("local_o", 1, 0)], **local_tail(1, 43)}
EPILOGUE = [("down", 1), ("wide_o", )]
NO_BANK = ("local_norm", "norm")
USES = {name: k for k, name in enumerate(x for x in PROLOGUE + [y for s in range(STEPS) for y in BESIDE.get(s, ())]
                                         + EPILOGUE if x[0] not in NO_BANK and x not in WIDE_USES)}


def layer2(nc, g, B):
    w = g.w
    with ExitStack() as ctx:
        def sb(name, shape, dt=FP32):
            return ctx.enter_context(nc.sbuf_tensor("l2_" + name, shape, dt))

        def sem(name):
            return ctx.enter_context(nc.semaphore("l2_" + name))

        xt = sb("xt", [P, NC, D])
        xn = sb("xn", [P, NC, D])
        xl = sb("xl", [P, NC, D])
        xnT = sb("xnT", [P, S])
        st = stat_buffers(sb, NC)
        z = sb("z", [P, NC, NH])
        za = sb("za", [P, NC, NH])
        ze = sb("ze", [P, NC, NH])
        zl = sb("zl", [P, NC, NH])
        f = sb("f", [P, NC, NH])
        cums = sb("cums", [P, NC, NH, SLOT])
        qT = sb("qT", [P, WAYS, NG, S])
        kT = sb("kT", [P, NG, S])
        v = sb("v", [P, NC, 2 * D])
        negmax = sb("negmax", [P, 3, NC])
        probs = sb("probs", [P, 3, AW])
        probsT = sb("probsT", [P, 2, AW])
        rowsum = sb("rowsum", [P, WAYS, NC, NH])
        rrow = sb("rrow", [P, WAYS, NC, NH])
        on = sb("on", [P, WAYS, NC, D])
        oT = sb("oT", [P, WAYS, S])
        tables = sb("tables", [P, DEPTH, 4, NC * LD])
        hT = sb("hT", [P, S])
        sq = sb("sq", [P, 2, INNER])
        ss = sb("ss", [P, 4, LH])
        ssm = sb("ssm", [P, 4, LH])
        rinv = sb("rinv", [P, 4, LH])
        rot = sb("rot", [P, 2, INNER])
        qk_raw = sb("qk_raw", [P, 4, INNER])
        qkT = sb("qkT", [P, 2, IB, S])
        v2 = sb("v2", [P, NC, INNER])
        rowsum2 = sb("rowsum2", [P, 2, LH])
        rrow2 = sb("rrow2", [P, 2, LH])
        on2 = sb("on2", [P, 2, NC, INNER // 2])
        oT2 = sb("oT2", [P, IB, S])
        st2 = Names()
        st2.stats, st2.mv, st2.pad = sb("stats2", [P, NC, 6]), sb("mean_var2", [P, NC, 2]), sb("norm_pad2", [1, 1])
        st2.var, st2.rstd = sb("var2", [P, NC]), sb("rstd2", [P, NC])
        hs = sb("hs", [P, NC, D])
        hnT = sb("hnT", [P, S])
        gg = sb("gg", [P, FC, S])
        hidT = sb("hidT", [P, FC, S])

        Sb, Tb, wide_sum, local_sum = g.bank[0:3], g.bank[3], g.bank[6], g.bank[7]
        G = Banks(g.bank[4:6], [sem("g_full0"), sem("g_full1")], [sem("g_taken0"), sem("g_taken1")], len(USES))
        W = Banks(Sb, [sem(f"w_full{i}") for i in range(3)], [sem(f"w_taken{i}") for i in range(3)], len(WIDE_USES))

        setup_done = sem("setup_done")
        var_ready = sem("var_ready")
        rstd_ready = sem("rstd_ready")
        xn_ready = sem("xn_ready")
        act_chain = sem("act_chain")
        zl_ready = sem("zl_ready")
        f_ready = sem("f_ready")
        scores_ready = sem("scores_ready")
        negmax_ready = sem("negmax_ready")
        probs_ready = sem("probs_ready")
        transposed = sem("transposed")
        probsT_ready = sem("probsT_ready")
        heads_summed = sem("heads_summed")
        on_ready = sem("on_ready")
        sq_ready = sem("sq_ready")
        ss_ready = sem("ss_ready")
        rinv_ready = sem("rinv_ready")
        qkn_ready = sem("qkn_ready")
        heads2_summed = sem("heads2_summed")
        on2_ready = sem("on2_ready")
        var2_ready = sem("var2_ready")
        rstd2_ready = sem("rstd2_ready")
        hn_ready = sem("hn_ready")
        gelu_ready = sem("gelu_ready")
        out_full = sem("out_full")
        out_used = sem("out_used")
        xl_ready = sem("xl_ready")
        x_done = sem("x_done")
        dve_chain = sem("dve_chain")
        next_chain = sem("next_chain")
        early = sum(x[0] == "qk" for x in PROLOGUE)
        n_next = 1 + NORM_STEPS(NC) + 3 * early
        n_chain = 2 + 1 + 3 * (DEPTH * 4 - early) + DEPTH * (2 + NORM_STEPS(NC))

        block = ctx.enter_context(nc.Block())

        @block.tensor
        def _(pe):
            g.wait_consts(pe)
            g.wait_layer(pe, 2)
            G.open(pe)
            W.open(pe)
            pe.sem_inc(out_used, 1)

            def steps(it):
                def open_bank(name, after=()):
                    ring, uses = (W, WIDE_USES) if name in WIDE_USES else (G, USES)
                    return ring.fill(pe, it, uses[name], [uses[n] for n in after])

                def transposes(name, blocks, after=()):
                    b = open_bank(name, after)
                    for j, t in enumerate(blocks):
                        last = pe.transpose(b[:, j * P:(j + 1) * P], t, g.ident[:, :])
                    G.filled(last, USES[name])

                def xnT_():
                    pe.wait_ge(xn_ready, it + 1)
                    transposes(("xnT", ), [xn[:, c, :] for c in range(NC)])

                def gates():
                    b = open_bank(("gates", ), [("xnT", )])
                    for c in range(NC):
                        last = pe.matmul(b[:, c * NH:(c + 1) * NH], xnT[:, c * P:(c + 1) * P], w["f2"][:, :],
                                         start=True, stop=True)
                    G.filled(last, USES[("gates", )])

                def cumulate():
                    pe.wait_ge(f_ready, it + 1)
                    b = open_bank(("cumulate", ))
                    for y, c, parts in ((0, 0, ((0, w["tri2"]), )), (0, 1, ((0, w["ones2"]), (1, w["tri2"]))),
                                        (1, 0, ((0, w["tri_back2"]), (1, w["ones2"]))), (1, 1, ((1, w["tri_back2"]), ))):
                        at = (y * NC + c) * NH
                        for i, (src, m) in enumerate(parts):
                            last = pe.matmul(b[:, at:at + NH], m[:, :], f[:, src, :],
                                             start=(i == 0), stop=(i == len(parts) - 1))
                    W.filled(last, WIDE_USES[("cumulate", )])

                def wide_q(u):
                    b = open_bank(("wide_q", u))
                    for j in range(2):
                        gi = 2 * u + j
                        last = pe.matmul(b[:, j * S:(j + 1) * S], w["q2"][:, gi * P:(gi + 1) * P], xnT[:, :],
                                         start=True, stop=True)
                    W.filled(last, WIDE_USES[("wide_q", u)])

                def wide_k(u):
                    b = open_bank(("wide_k", u), [("cumulate", )])
                    for j in range(2):
                        gi = 2 * u + j
                        pe.matmul(b[:, j * S:(j + 1) * S], w["k2"][:, gi * P:(gi + 1) * P], xnT[:, :],
                                  start=True, stop=False, skip_group_check=True)
                        for c in range(NC):
                            last = pe.matmul(b[:, j * S + c * P:j * S + (c + 1) * P],
                                             cums[:, c, gi * GH:(gi + 1) * GH, :].rearrange("p h s -> p (h s)"),
                                             g.ident[:, :], start=False, stop=(c == NC - 1), skip_group_check=True)
                    W.filled(last, WIDE_USES[("wide_k", u)])

                def wide_v():
                    b = open_bank(("wide_v", ))
                    for c in range(NC):
                        last = pe.matmul(b[:, c * P:(c + 1) * P], xnT[:, c * P:(c + 1) * P], w["v2w"][:, :],
                                         start=True, stop=True)
                    W.filled(last, WIDE_USES[("wide_v", )])

                def shift(l, i):
                    if i == 0:
                        pe.wait_ge(xl_ready, it * DEPTH + l)
                    transposes(("shift", l, i), [xl[:, c, :] for c in range(NC)], [("local_out", l)] if i else [])

                def qk(l, i):
                    b = open_bank(("qk", l, i), [("shift", l, 0) if l else ("xnT", )])
                    c = i % 2
                    G.filled(pe.matmul(b[:, :], hT[:, c * P:(c + 1) * P],
                                       w["qkv2"][:, l, (i // 2) * INNER:(i // 2 + 1) * INNER], start=True, stop=True),
                             USES[("qk", l, i)])

                def local_v(l, c):
                    b = open_bank(("local_v", l, c))
                    G.filled(pe.matmul(b[:, :], hT[:, c * P:(c + 1) * P], w["qkv2"][:, l, 2 * INNER:3 * INNER],
                                       start=True, stop=True), USES[("local_v", l, c)])

                def qk_t(l, i):
                    pe.wait_ge(qkn_ready, (it * DEPTH + l) * 4 + i + 1)
                    transposes(("qk_t", l, i), [qk_raw[:, i, j * P:(j + 1) * P] for j in range(IB)])

                def local_o(l, half):
                    pe.wait_ge(on2_ready, (it * DEPTH + l) * 2 + half + 1)
                    transposes(("local_o", l, half),
                               [on2[:, half, c, j * P:(j + 1) * P] for j in range(IB // 2) for c in range(NC)])

                def local_out(l):
                    b = open_bank(("local_out", l), [("local_o", l, 0), ("local_o", l, 1)])
                    for c in range(NC):
                        for j in range(IB):
                            last = pe.matmul(b[:, c * P:(c + 1) * P], oT2[:, j, c * P:(c + 1) * P],
                                             w["wo2"][:, l, j, :], start=(j == 0), stop=(j == IB - 1))
                    G.filled(last, USES[("local_out", l)])

                def back(l):
                    transposes(("back", l), [hT[:, c * P:(c + 1) * P] for c in range(NC)], [("shift", l, 1)])

                def normed(l):
                    pe.wait_ge(hn_ready, it * DEPTH + l + 1)
                    transposes(("normed", l), [hs[:, c, :] for c in range(NC)])

                def up(l, m):
                    b = open_bank(("up", l, m), [("normed", l)])
                    pe.matmul(b[:, 0:S], w["up2"][:, l, 0, m * P:(m + 1) * P], hnT[:, :], start=True, stop=True)
                    G.filled(pe.matmul(b[:, S:2 * S], w["up2"][:, l, 1, m * P:(m + 1) * P], hnT[:, :],
                                       start=True, stop=True), USES[("up", l, m)])

                def down(l):
                    b = open_bank(("down", l), [("up", l, m) for m in range(FC)])
                    for c in range(NC):
                        for m in range(FC):
                            last = pe.matmul(b[:, c * P:(c + 1) * P], hidT[:, m, c * P:(c + 1) * P],
                                             w["down2"][:, l, m, :], start=(m == 0), stop=(m == FC - 1))
                    G.filled(last, USES[("down", l)])

                def wide_o():
                    pe.wait_ge(on_ready, it + 1)
                    transposes(("wide_o", ), [on[:, y, c, :] for y in range(WAYS) for c in range(NC)])

                def wide_out():
                    G.wait_taken(pe, it, USES[("wide_o", )])
                    for c in range(NC):
                        for y in range(WAYS):
                            last = pe.matmul(Tb[:, c * P:(c + 1) * P], oT[:, y, c * P:(c + 1) * P], w["out2"][:, y, :],
                                             start=(y == 0), stop=(y == WAYS - 1))
                    last.then_inc(out_full, 1)

                do = dict(xnT=xnT_, gates=gates, cumulate=cumulate, wide_q=wide_q, wide_k=wide_k, wide_v=wide_v,
                          shift=shift, qk=qk, local_v=local_v, qk_t=qk_t, local_o=local_o, local_out=local_out,
                          back=back, normed=normed, up=up, down=down, wide_o=wide_o, wide_out=wide_out)
                return do

            first = steps(0)
            for name, *args in PROLOGUE:
                first[name](*args)
            with pe.Fori(0, B) as it:
                do, following = steps(it), steps(it + 1)

                def scores(u):
                    kind, *of = UNIT_ORDER[u]
                    bank = Sb[u % 3]
                    if kind == "wide":
                        y, h = of[0] // NH, of[0] % NH
                        rows = slice(SLOT * (h % GH), SLOT * (h % GH + 1))
                        return pe_scores(pe, g, bank, qT[rows, y, h // GH, :], kT[rows, h // GH, :],
                                         (g.mask_causal, g.mask_anti)[y], (FORWARD, BACKWARD)[y])
                    l, h = of
                    if h == 0:
                        G.wait_taken(pe, it, USES[("qk_t", l, 2)])
                        G.wait_taken(pe, it, USES[("qk_t", l, 3)])
                    rows = slice(LD * (h % 2), LD * (h % 2 + 1))
                    return pe_scores(pe, g, bank, qkT[rows, 0, h // 2, :], qkT[rows, 1, h // 2, :], g.mask_band, FORWARD)

                def values(u):
                    kind, *of = UNIT_ORDER[u]
                    pt = probsT[:, u % 2, :]
                    if kind == "wide":
                        y, h = of[0] // NH, of[0] % NH
                        at = (y * NH + h) * NC * DH
                        n = min(D, WAYS * NC * D - at - DH)
                        outs = [wide_sum[:, at + c * DH:at + c * DH + n] for c in range(NC)]
                        last = pe_values(pe, outs, pt, v[:, :, h * DH:h * DH + n], (FORWARD, BACKWARD)[y])
                        if of[0] == WAYS * NH - 1:
                            last.then_inc(heads_summed, 1)
                        return
                    l, h = of
                    hh = h % (LH // 2)
                    if h == LH // 2:
                        pe.wait_ge(on2_ready, (it * DEPTH + l) * 2 + 1)
                    n = min(2, LH // 2 - hh)
                    outs = [local_sum[:, (c * LH // 2 + hh) * LD:(c * LH // 2 + hh + n) * LD] for c in range(NC)]
                    last = pe_values(pe, outs, pt, v2[:, :, h * LD:(h + n) * LD], FORWARD)
                    if hh == LH // 2 - 1:
                        last.then_inc(heads2_summed, 1)

                for name in (("wide_k", 0), ("wide_k", 1)):
                    W.wait_taken(pe, it, WIDE_USES[name])
                for s in range(STEPS):
                    if s < UNITS:
                        scores(s).then_inc(scores_ready, 1)
                    for name, *args in BESIDE.get(s, ()):
                        if name in do:
                            do[name](*args)
                    if 0 <= s - LAG:
                        pe.wait_ge(probsT_ready, it * UNITS + s - LAG + 1)
                        values(s - LAG)
                    if 0 <= s - 2 < UNITS:
                        u = s - 2
                        pe.wait_ge(probs_ready, it * UNITS + u + 1)
                        if u == 0:
                            pe.wait_ge(out_used, it + 1)
                        pe_transpose3(pe, g, Tb, probs[:, u % 3, :]).then_inc(transposed, 1)
                for name, *args in EPILOGUE:
                    do[name](*args)
                following["xnT"]()
                do["wide_out"]()
                for name, *args in PROLOGUE[1:]:
                    following[name](*args)

        @block.gpsimd
        def _(pool):
            g.wait_layer(pool, 0)
            pool.wait_ge(var_ready, 1)
            norm_rstd(pool, g, st, NC).then_inc(rstd_ready, 1)
            with pool.Fori(0, B) as it:
                for l in range(DEPTH):
                    for i in range(4):
                        n = (it * DEPTH + l) * 4 + i + 1
                        pool.wait_ge(ss_ready, n)
                        pool.tensor_tensor(rinv[:, i, :], ssm[:, i, :], g.neg_half[:, 0:LH], ALU.pow).then_inc(rinv_ready, 1)
                        G.wait_taken(pool, it, USES[("qk", l, i)])
                        pool.wait_ge(rinv_ready, n)
                        heads = qk_raw[:, i, :].rearrange("p (h d) -> p h d", h=LH)
                        pool.tensor_tensor(heads, heads, rinv[:, i, :].unsqueeze(2).to_broadcast([P, LH, LD]),
                                           ALU.mult).then_inc(qkn_ready, 1)
                    pool.wait_ge(var2_ready, it * DEPTH + l + 1)
                    norm_rstd(pool, g, st2, NC).then_inc(rstd2_ready, 1)
                pool.wait_ge(var_ready, it + 2)
                norm_rstd(pool, g, st, NC).then_inc(rstd_ready, 1)

        @block.scalar
        def _(act):
            g.wait_layer(act, 2)
            g.wait_consts(act)

            def steps(it):
                def gates():
                    ch = Chain(act, act_chain, it, 2)
                    G.wait_taken(act, it, USES[("gates", )])
                    ch(act.activation(za[:, :, :], z[:, :, :], ACT.Abs))
                    ch(act.activation(ze[:, :, :], za[:, :, :], ACT.Exp, scale=-1.0))
                    act.activation(zl[:, :, :], ze[:, :, :], ACT.Ln, bias=1.0).then_inc(zl_ready, 1)

                def wide_q(u):
                    b = W.read(act, it, WIDE_USES[("wide_q", u)])
                    for y in range(WAYS):
                        last = act.activation(qT[:, y, 2 * u:2 * u + 2, :], chunks(b[:, :]), ACT.Identity,
                                              bias=w["one_rows2"][:, y:y + 1], scale=DH ** -0.5)
                    W.took(last, WIDE_USES[("wide_q", u)])

                def wide_k(u):
                    b = W.read(act, it, WIDE_USES[("wide_k", u)])
                    W.took(act.activation(kT[:, 2 * u:2 * u + 2, :], chunks(b[:, :]), ACT.Copy), WIDE_USES[("wide_k", u)])

                def qk(l, i):
                    b = G.read(act, it, USES[("qk", l, i)])
                    act.activation(sq[:, i % 2, :], b[:, :], ACT.Square).then_inc(sq_ready, 1)

                def local_v(l, c):
                    b = G.read(act, it, USES[("local_v", l, c)])
                    G.took(act.activation(v2[:, c, :], b[:, :], ACT.Copy), USES[("local_v", l, c)])

                def qk_t(l, i):
                    b = G.read(act, it, USES[("qk_t", l, i)])
                    c = i % 2
                    G.took(act.activation(qkT[:, i // 2, :, c * P:(c + 1) * P], chunks(b[:, :], IB), ACT.Copy),
                           USES[("qk_t", l, i)])

                def up(l, m):
                    b = G.read(act, it, USES[("up", l, m)])
                    act.activation(gg[:, m, :], b[:, S:2 * S], ACT.Gelu,
                                   bias=w["bup2"][:, l, 1, m:m + 1]).then_inc(gelu_ready, 1)

                return dict(gates=gates, wide_q=wide_q, wide_k=wide_k, qk=qk, local_v=local_v, qk_t=qk_t, up=up)

            def prologue(do):
                for name, *args in PROLOGUE:
                    if name in do:
                        do[name](*args)

            prologue(steps(0))
            with act.Fori(0, B) as it:
                do = steps(it)
                for u in range(UNITS + LAG):
                    if u < UNITS:
                        kind, *of = UNIT_ORDER[u]
                        way = FORWARD
                        if kind == "wide":
                            y, h = of[0] // NH, of[0] % NH
                            way = (FORWARD, BACKWARD)[y]
                            sums = [rowsum[:, y, c, h:h + 1] for c in range(NC)]
                        else:
                            half, hh = of[1] // (LH // 2), of[1] % (LH // 2)
                            sums = [rowsum2[:, half, c * LH // 2 + hh:c * LH // 2 + hh + 1] for c in range(NC)]
                        act.wait_ge(negmax_ready, it * UNITS + u + 1)
                        act_probs(act, Sb[u % 3], negmax[:, u % 3, :], probs[:, u % 3, :], sums,
                                  way).then_inc(probs_ready, 1)
                    for name, *args in BESIDE.get(u, ()):
                        if name in do:
                            do[name](*args)
                    if 0 <= u - 2 < UNITS:
                        act.wait_ge(transposed, it * UNITS + u - 2 + 1)
                        act.activation(probsT[:, u % 2, :], Tb[:, 0:AW], ACT.Copy).then_inc(probsT_ready, 1)
                prologue(steps(it + 1))

        @block.vector
        def _(dve):
            g.wait_consts(dve)
            g.wait_layer(dve, 2)
            for l in range(DEPTH):
                dve.tensor_tensor(tables[:, l, :, :].rearrange("p i (c d) -> p i c d", c=NC),
                                  w["rot2"][:, :, :].rearrange("p i (c d) -> p i c d", c=NC),
                                  w["scale_rows2"][:, l, :, :].unsqueeze(2).to_broadcast([P, 4, NC, LD]), ALU.mult)
            dve.memset(v[:, :, D:2 * D], 0.0)
            dve.memset(hT[:, 0:1], 0.0)
            dve.memset(cums[:, :, :, :], 0.0).then_inc(setup_done, 1)
            dve.wait_ge(setup_done, 1)

            def steps(it, ch):
                def shifted(b):
                    dve.tensor_copy(hT[0:P // 2, :], b[0:P // 2, 0:S])
                    return dve.tensor_copy(hT[P // 2:P, 1:S], b[P // 2:P, 0:S - 1])

                def xnT_():
                    b = G.read(dve, it, USES[("xnT", )])
                    dve.tensor_copy(xnT[:, :], b[:, 0:S])
                    G.took(shifted(b), USES[("xnT", )])

                def shift(l, i):
                    G.took(shifted(G.read(dve, it, USES[("shift", l, i)])), USES[("shift", l, i)])

                def gates():
                    b = G.read(dve, it, USES[("gates", )])
                    G.took(dve.tensor_tensor(z[:, :, :], chunks(b[:, 0:NC * NH]), over_chunks(w["bf2"][:, :]), ALU.add),
                           USES[("gates", )])
                    dve.wait_ge(zl_ready, it + 1)
                    dve.scalar_tensor_tensor(out=f[:, :, :], in0=z[:, :, :], scalar=0.0, in1=zl[:, :, :],
                                             op0=ALU.min, op1=ALU.subtract).then_inc(f_ready, 1)

                def cumulate():
                    b = W.read(dve, it, WIDE_USES[("cumulate", )])
                    for y in range(WAYS):
                        last = dve.tensor_scalar(cums[:, :, :, DH + y], chunks(b[:, y * NC * NH:(y + 1) * NC * NH]), -1.0,
                                                 None, ALU.mult)
                    W.took(last, WIDE_USES[("cumulate", )])

                def wide_v():
                    b = W.read(dve, it, WIDE_USES[("wide_v", )])
                    W.took(dve.tensor_copy(v[:, :, 0:D], chunks(b[:, 0:S])), WIDE_USES[("wide_v", )])

                def qk(l, i):
                    c, cos, sin = i % 2, 2 * (i // 2), 2 * (i // 2) + 1
                    b = G.read(dve, it, USES[("qk", l, i)])
                    dve.wait_ge(sq_ready, (it * DEPTH + l) * 4 + i + 1)
                    bh = b[:, :].rearrange("p (h d) -> p h d", h=LH)
                    rh = rot[:, i % 2, :].rearrange("p (h d) -> p h d", h=LH)

                    def table(n, lo, hi):
                        return tables[:, l, n, c * LD + lo:c * LD + hi].unsqueeze(1).to_broadcast([P, LH, hi - lo])

                    dve.tensor_tensor(rh[:, :, 0:LHALF], bh[:, :, LHALF:LD], table(sin, 0, LHALF), ALU.mult)
                    m = ch.mark(dve.tensor_tensor(rh[:, :, LHALF:LD], bh[:, :, 0:LHALF], table(sin, LHALF, LD), ALU.mult))
                    m2 = ch.mark(dve.reduce_sum(ss[:, i, :], sq[:, i % 2, :].rearrange("p (h d) -> p h d", h=LH), AX.X))
                    ch.wait(m)
                    m = ch.mark(dve.tensor_tensor(bh, bh, table(cos, 0, LD), ALU.mult))
                    ch.wait(m2)
                    dve.tensor_scalar(ssm[:, i, :], ss[:, i, :], 1e-24, None, ALU.max).then_inc(ss_ready, 1)
                    ch.wait(m)
                    G.took(dve.tensor_tensor(qk_raw[:, i, :], b[:, :], rot[:, i % 2, :], ALU.add), USES[("qk", l, i)])

                def local_norm(l, half):
                    dve.wait_ge(heads2_summed, (it * DEPTH + l) * 2 + half + 1)
                    ch(dve.reciprocal(rrow2[:, half, :], rowsum2[:, half, :]))
                    dve.tensor_tensor(on2[:, half, :, :].rearrange("p c (h d) -> p (c h) d", d=LD),
                                      local_sum[:, :].rearrange("p (x d) -> p x d", d=LD),
                                      rrow2[:, half, :].unsqueeze(2).to_broadcast([P, LH, LD]),
                                      ALU.mult).then_inc(on2_ready, 1)

                def local_o(l, half):
                    b = G.read(dve, it, USES[("local_o", l, half)])
                    G.took(dve.tensor_copy(oT2[:, 2 * half:2 * half + 2, :], chunks(b[:, :])), USES[("local_o", l, half)])

                def local_out(l):
                    b = G.read(dve, it, USES[("local_out", l)])
                    G.took(dve.tensor_tensor(xl[:, :, :], xl[:, :, :], chunks(b[:, 0:S]), ALU.add), USES[("local_out", l)])

                def back(l):
                    b = G.read(dve, it, USES[("back", l)])
                    G.took(dve.tensor_copy(hs[:, :, :], chunks(b[:, 0:S])), USES[("back", l)])
                    G.wait_taken(dve, it, USES[("back", l)])
                    norm_stats(dve, ch, hs, st2, NC).then_inc(var2_ready, 1)

                def norm(l):
                    dve.wait_ge(rstd2_ready, it * DEPTH + l + 1)
                    norm_apply(dve, hs, hs, st2, NC).then_inc(hn_ready, 1)

                def normed(l):
                    b = G.read(dve, it, USES[("normed", l)])
                    G.took(dve.tensor_scalar(hnT[:, :], b[:, 0:S], w["ln2"][:, l, 0:1], w["ln2"][:, l, 1:2],
                                             ALU.mult, ALU.add), USES[("normed", l)])

                def up(l, m):
                    b = G.read(dve, it, USES[("up", l, m)])
                    dve.wait_ge(gelu_ready, (it * DEPTH + l) * FC + m + 1)
                    G.took(dve.scalar_tensor_tensor(out=hidT[:, m, :], in0=b[:, 0:S],
                                                    scalar=w["bup2"][:, l, 0, m:m + 1], in1=gg[:, m, :],
                                                    op0=ALU.add, op1=ALU.mult), USES[("up", l, m)])

                def down(l):
                    b = G.read(dve, it, USES[("down", l)])
                    G.took(dve.tensor_tensor(xl[:, :, :], xl[:, :, :], chunks(b[:, 0:S]), ALU.add), USES[("down", l)])
                    G.wait_taken(dve, it, USES[("down", l)])
                    dve.tensor_tensor(xl[:, :, :], xl[:, :, :], over_chunks(w["bdown2"][:, l, :]),
                                      ALU.add).then_inc(xl_ready, 1)

                def wide_o():
                    b = G.read(dve, it, USES[("wide_o", )])
                    G.took(dve.tensor_copy(oT[:, :, :], chunks(b[:, :])), USES[("wide_o", )])

                def wide_out():
                    dve.wait_ge(out_full, it + 1)
                    dve.tensor_tensor(xt[:, :, :], xt[:, :, :], chunks(Tb[:, 0:S]), ALU.add).then_inc(out_used, 1)

                do = dict(xnT=xnT_, gates=gates, cumulate=cumulate, wide_v=wide_v, shift=shift, qk=qk,
                          local_norm=local_norm, local_o=local_o, local_out=local_out, back=back, norm=norm,
                          normed=normed, up=up, down=down, wide_o=wide_o, wide_out=wide_out)

                return do

            def next_stats(n):
                ch = Chain(dve, next_chain, n, n_next)
                ch(dve.tensor_copy(xn[:, :, :], g.x_all[:, bass.ds(n * NC, NC), :]))
                norm_stats(dve, ch, xn, st, NC).then_inc(var_ready, 1)

            def next_norm(n):
                dve.wait_ge(rstd_ready, n + 1)
                norm_apply(dve, xn, xn, st, NC).then_inc(xn_ready, 1)

            def next_steps(n):
                ch = Chain(dve, next_chain, n, n_next)
                ch.n = 1 + NORM_STEPS(NC)
                return steps(n, ch), ch

            next_stats(0)
            next_norm(0)
            first, ch = next_steps(0)
            for name, *args in PROLOGUE:
                if name in first:
                    first[name](*args)
            ch.done()
            with dve.Fori(0, B) as it:
                ch = Chain(dve, dve_chain, it, n_chain)
                do = steps(it, ch)
                ch.mark(dve.tensor_copy(xl[:, :, :], xn[:, :, :]))
                ch(dve.tensor_copy(xt[:, :, :], g.x_all[:, bass.ds(it * NC, NC), :]))
                for s in range(STEPS):
                    if s < UNITS:
                        y = UNIT_ORDER[s][1] // NH if UNIT_ORDER[s][0] == "wide" else 0
                        dve.wait_ge(scores_ready, it * UNITS + s + 1)
                        dve_negmax(dve, Sb[s % 3], negmax[:, s % 3, :], (FORWARD, BACKWARD)[y]).then_inc(negmax_ready, 1)
                    for name, *args in BESIDE.get(s, ()):
                        if name in do:
                            do[name](*args)
                    if s == STEPS - 4:
                        next_stats(it + 1)
                    if s == STEPS - 2:
                        next_norm(it + 1)
                dve.wait_ge(heads_summed, it + 1)
                ch(dve.reciprocal(rrow[:, :, :, :], rowsum[:, :, :, :]))
                for y in range(WAYS):
                    for c in range(NC):
                        last = dve.tensor_tensor(
                            on[:, y, c, :].rearrange("p (h d) -> p h d", h=NH),
                            wide_sum[:, :].rearrange("p (y h c d) -> p y c h d", y=WAYS, h=NH, c=NC)[:, y, c, :, :],
                            rrow[:, y, c, :].unsqueeze(2).to_broadcast([P, NH, DH]), ALU.mult)
                last.then_inc(on_ready, 1)
                for name, *args in EPILOGUE:
                    do[name](*args)
                following, next_ch = next_steps(it + 1)
                following["xnT"]()
                do["wide_out"]()
                dve.wait_ge(xl_ready, it * DEPTH + DEPTH)
                dve.wait_ge(out_used, it + 2)
                dve.tensor_tensor(g.x_all[:, bass.ds(it * NC, NC), :], xt[:, :, :], xl[:, :, :],
                                  ALU.add).then_inc(x_done, 1)
                dve.wait_ge(x_done, it + 1)
                dve.memset(st.pad[:, :], 0.0)
                ch.done()
                for name, *args in PROLOGUE[1:]:
                    if name in following:
                        following[name](*args)
                next_ch.done()


FB = 8
NEXT_STATS = 4
GELU_IN = math.sqrt(2.0 / math.pi)


def layer3(nc, g, B, out):
    w = g.w
    with ExitStack() as ctx:
        def sb(name, shape, dt=FP32):
            return ctx.enter_context(nc.sbuf_tensor("l3_" + name, shape, dt))

        def sem(name):
            return ctx.enter_context(nc.semaphore("l3_" + name))

        xt = sb("xt", [P, NC, D])
        x_next = sb("x_next", [P, NC, D])
        xn = sb("xn", [P, NC, D])
        xnT = sb("xnT", [P, S])
        st = stat_buffers(sb, NC)
        r = router_buffers(sb, NC)
        bq_one = sb("bq_one", [P, FB])
        bk_one = sb("bk_one", [P, FB])
        neg_bq = sb("neg_bq", [P, FB])
        neg_one = sb("neg_one", [P, 1])
        eps = sb("eps", [P, 1])
        neg_bk = sb("neg_bk", [P, FB])
        neg_part = sb("neg_part", [P, 2, 2, S])
        exp_raw = sb("exp_raw", [P, 2, 2, S])
        exp_less = sb("exp_less", [P, 2, 2, S])
        exp_part = sb("exp_part", [P, 2, 2, S])
        k_feat = sb("k_feat", [P, 2, S])
        q_feat = sb("q_feat", [P, 2, S])
        kv_junk = sb("kv_junk", [P, 2, S])
        k_sum = sb("k_sum", [P, FB])
        kv_sum = sb("kv_sum", [P, FB])
        den = sb("den", [P, 2, S])
        rden = sb("rden", [P, 2, S])
        pool_pad = sb("pool_pad", [1, FB])
        qkv = sb("qkv", [P, 2, S])
        attnT = sb("attnT", [P, FB, S])
        th = sb("th", [P, 2, 2 * S])
        gated = sb("gated", [P, 2, 2 * S])
        hT = sb("hT", [P, 2, HC, S])
        y = sb("y", [P, NC, D])
        y2 = sb("y2", [P, NC, D])
        ty = sb("ty", [P, NC, D])

        F_XNT, F_LOGIT, F_KV = 0, 1, 2
        F = Banks(g.bank[4:6], [sem(f"f_full{i}") for i in range(2)], [sem(f"f_taken{i}") for i in range(2)], 2 + 2 * FB)
        G = Banks(g.bank[0:4], [sem(f"g_full{i}") for i in range(4)], [sem(f"g_taken{i}") for i in range(4)], 4 * E)
        Db, Ob = g.bank[6], g.bank[7]
        var_ready = sem("var_ready")
        rstd_ready = sem("rstd_ready")
        xn_ready = sem("xn_ready")
        setup_done = sem("setup_done")
        gate_exp = sem("gate_exp")
        neg_ready = sem("neg_ready")
        raw_ready = sem("raw_ready")
        less_ready = sem("less_ready")
        exp_ready = sem("exp_ready")
        den_ready = sem("den_ready")
        pool_chain = sem("pool_chain")
        rden_ready = sem("rden_ready")
        k_ready = sem("k_ready")
        attn_ready = sem("attn_ready")
        tanh_ready = sem("tanh_ready")
        down_ready = sem("down_ready")
        down_used = sem("down_used")
        out_ready = sem("out_ready")
        out_used = sem("out_used")
        gelu_in = sem("gelu_in")
        gelu_tanh = sem("gelu_tanh")
        x_done = sem("x_done")
        stored = sem("stored")
        dve_chain = sem("dve_chain")
        next_chain = sem("next_chain")
        n_chain = 1 + 2 * NC + 3 + 1 + 3

        block = ctx.enter_context(nc.Block())

        @block.tensor
        def _(pe):
            g.wait_consts(pe)
            g.wait_layer(pe, 3)
            F.open(pe)
            G.open(pe)
            pe.sem_inc(down_used, 1)
            pe.sem_inc(out_used, 1)

            def next_tokens(n):
                pe.wait_ge(xn_ready, n + 1)
                b = F.fill(pe, n, F_XNT)
                for c in range(NC):
                    last = pe.transpose(b[:, c * P:(c + 1) * P], xn[:, c, :], g.ident[:, :])
                F.filled(last, F_XNT)
                b = F.fill(pe, n, F_LOGIT, [F_XNT])
                for c in range(NC):
                    last = pe.matmul(b[:, c * E:(c + 1) * E], xnT[:, c * P:(c + 1) * P], w["gate3"][:, :],
                                     start=True, stop=True)
                F.filled(last, F_LOGIT)

            next_tokens(0)
            with pe.Fori(0, B) as it:
                for m in range(E + 2):
                    if m < E:
                        cols = slice(m * P, (m + 1) * P)
                        b = F.fill(pe, it, F_KV + 2 * m)
                        pe.matmul(b[:, 0:S], w["k3"][:, cols], xnT[:, :], start=True, stop=True)
                        F.filled(pe.matmul(b[:, S:2 * S], w["v3"][:, cols], xnT[:, :], start=True, stop=True), F_KV + 2 * m)
                        b = F.fill(pe, it, F_KV + 2 * m + 1)
                        F.filled(pe.matmul(b[:, 0:S], w["q3"][:, cols], xnT[:, :], start=True, stop=True),
                                 F_KV + 2 * m + 1)
                        for u in range(2):
                            for i, wt in enumerate((w["egate3"], w["eup3"])):
                                k = 4 * m + 2 * u + i
                                b = G.fill(pe, it, k)
                                for j in range(2):
                                    h = (m * HC + 2 * u + j) * P
                                    last = pe.matmul(b[:, j * S:(j + 1) * S], wt[:, h:h + P], xnT[:, :],
                                                     start=True, stop=True)
                                G.filled(last, k)
                    if 1 <= m <= E:
                        e = m - 1
                        G.wait_taken(pe, it, 4 * e + 1)
                        G.wait_taken(pe, it, 4 * e + 3)
                        pe.wait_ge(down_used, it * E + e + 1)
                        for c in range(NC):
                            for j in range(HC):
                                last = pe.matmul(Db[:, c * P:(c + 1) * P], hT[:, e % 2, j, c * P:(c + 1) * P],
                                                 w["edown3"][:, e * HC + j, :], start=(j == 0), stop=(j == HC - 1))
                        last.then_inc(down_ready, 1)
                    if m >= 2:
                        f = m - 2
                        if f == 0:
                            pe.wait_ge(out_used, it + 1)
                        pe.wait_ge(attn_ready, it * FB + f + 1)
                        for c in range(NC):
                            last = pe.matmul(Ob[:, c * P:(c + 1) * P], attnT[:, f, c * P:(c + 1) * P],
                                             w["out3"][:, f, :], start=(f == 0 and c == 0), stop=(f == FB - 1),
                                             skip_group_check=True)
                        if f == FB - 1:
                            last.then_inc(out_ready, 1)
                    if m == E:
                        next_tokens(it + 1)

        @block.gpsimd
        def _(pool):
            g.wait_layer(pool, 0)
            pool.wait_ge(var_ready, 1)
            norm_rstd(pool, g, st, NC).then_inc(rstd_ready, 1)
            with pool.Fori(0, B) as it:
                ch = Chain(pool, pool_chain, it, FB)

                for m in range(FB):
                    s = m % 2
                    F.wait_taken(pool, it, F_KV + 2 * m)
                    pool_hold(pool, g, pool_pad[:, m:m + 1])
                    ch(pool.tensor_scalar(qkv[:, s, :], q_feat[:, s, :], kv_sum[:, m:m + 1], None, ALU.mult))
                    pool.wait_ge(rden_ready, it * FB + m + 1)
                    pool.tensor_tensor(attnT[:, m, :], qkv[:, s, :], rden[:, s, :], ALU.mult).then_inc(attn_ready, 1)
                    if m == NEXT_STATS:
                        pool.wait_ge(var_ready, it + 2)
                        norm_rstd(pool, g, st, NC).then_inc(rstd_ready, 1)
                ch.done()

        @block.scalar
        def _(act):
            g.wait_layer(act, 3)
            act.wait_ge(setup_done, 1)
            def gate_tanh(it, m, u):
                b = G.read(act, it, 4 * m + 2 * u)
                act.activation(th[:, u, :], b[:, :], ACT.Tanh, scale=0.5).then_inc(tanh_ready, 1)

            with act.Fori(0, B) as it:
                for m in range(E):
                    b = F.read(act, it, F_KV + 2 * m)
                    act.activation(neg_part[:, m % 2, 0, :], b[:, 0:S], ACT.Relu, bias=neg_bk[:, m:m + 1], scale=-1.0)
                    b = F.read(act, it, F_KV + 2 * m + 1)
                    act.activation(neg_part[:, m % 2, 1, :], b[:, 0:S], ACT.Relu, bias=neg_bq[:, m:m + 1],
                                   scale=-1.0).then_inc(neg_ready, 1)
                    act.wait_ge(neg_ready, it * FB + m + 1)
                    act.activation(exp_raw[:, m % 2, :, :], neg_part[:, m % 2, :, :], ACT.Exp,
                                   scale=-1.0).then_inc(raw_ready, 1)
                    if m == 0:
                        F.wait_taken(act, it, F_LOGIT)
                        act.activation(r.ex[:, :, :], r.ls[:, :, :], ACT.Exp).then_inc(gate_exp, 1)
                    gate_tanh(it, m, 0)
                    act.wait_ge(raw_ready, it * FB + m + 1)
                    act.activation(exp_less[:, m % 2, :, :], exp_raw[:, m % 2, :, :], ACT.Identity,
                                   bias=neg_one[:, 0:1]).then_inc(less_ready, 1)
                    act.wait_ge(less_ready, it * FB + m + 1)
                    act.activation(exp_part[:, m % 2, :, :], exp_less[:, m % 2, :, :], ACT.Identity,
                                   bias=1.0).then_inc(exp_ready, 1)
                    gate_tanh(it, m, 1)
                    act.wait_ge(k_ready, it * FB + m + 1)
                    F.wait_taken(act, it, F_KV + 2 * m + 1)
                    act.activation(den[:, m % 2, :], q_feat[:, m % 2, :], ACT.Identity, bias=eps[:, 0:1],
                                   scale=k_sum[:, m:m + 1]).then_inc(den_ready, 1)
                act.wait_ge(gelu_in, it + 1)
                act.activation(ty[:, :, :], y2[:, :, :], ACT.Tanh, scale=GELU_IN).then_inc(gelu_tanh, 1)

        @block.sync
        def _(sp):
            with sp.Fori(0, B) as it:
                sp.wait_ge(x_done, it + 1)
                sp.dma_start(out[bass.ds(it, 1), :, :].rearrange("b (c p) d -> p (b c) d", p=P),
                             g.x_all[:, bass.ds(it * NC, NC), :]).then_inc(stored, 16)
            sp.wait_ge(stored, 16 * B)

        @block.vector
        def _(dve):
            g.wait_consts(dve)
            g.wait_layer(dve, 3)
            dve.memset(neg_one[:, :], -1.0)
            dve.memset(eps[:, :], 1e-6)
            dve.tensor_scalar(bq_one[:, :], w["bq3"][:, :], 1.0, None, ALU.add)
            dve.tensor_scalar(neg_bk[:, :], w["bk3"][:, :], -1.0, None, ALU.mult)
            dve.tensor_scalar(neg_bq[:, :], w["bq3"][:, :], -1.0, None, ALU.mult)
            dve.tensor_scalar(bk_one[:, :], w["bk3"][:, :], 1.0, None, ALU.add).then_inc(setup_done, 1)
            dve.wait_ge(setup_done, 1)
            def next_stats(n):
                ch = Chain(dve, next_chain, n, 1 + NORM_STEPS(NC) + 2 + 2 * NC)
                ch(dve.tensor_copy(x_next[:, :, :], g.x_all[:, bass.ds(n * NC, NC), :]))
                norm_stats(dve, ch, x_next, st, NC).then_inc(var_ready, 1)

            def next_norm(n):
                dve.wait_ge(rstd_ready, n + 1)
                norm_apply(dve, x_next, xn, st, NC).then_inc(xn_ready, 1)

            def next_rank(n):
                ch = Chain(dve, next_chain, n, 1 + NORM_STEPS(NC) + 2 + 2 * NC)
                ch.n = 1 + NORM_STEPS(NC)
                b = F.read(dve, n, F_XNT)
                F.took(dve.tensor_copy(xnT[:, :], b[:, 0:S]), F_XNT)
                b = F.read(dve, n, F_LOGIT)
                F.took(router_rank(dve, ch, r, b[:, 0:NC * E].rearrange("p (c e) -> p c e", e=E), NC), F_LOGIT)
                ch.done()

            for part in (next_stats, next_norm, next_rank):
                part(0)
            with dve.Fori(0, B) as it:
                ch = Chain(dve, dve_chain, it, n_chain)
                ch(dve.tensor_copy(xt[:, :, :], x_next[:, :, :]))

                def gate(m, u):
                    k = 4 * m + 2 * u
                    bg = G.read(dve, it, k)
                    if m >= 1:
                        G.wait_taken(dve, it, k - 3)
                    dve.wait_ge(tanh_ready, it * 2 * E + 2 * m + u + 1)
                    G.took(dve.scalar_tensor_tensor(out=gated[:, u, :], in0=th[:, u, :], scalar=1.0,
                                                    in1=bg[:, :], op0=ALU.add, op1=ALU.mult), k)
                    bu = G.read(dve, it, k + 1)
                    G.wait_taken(dve, it, k)
                    G.took(dve.tensor_tensor(hT[:, m % 2, 2 * u:2 * u + 2, :], chunks(gated[:, u, :]),
                                             chunks(bu[:, :]), ALU.mult), k + 1)

                def features(m):
                    s = m % 2
                    dve.wait_ge(exp_ready, it * FB + m + 1)
                    bkv = F.read(dve, it, F_KV + 2 * m)
                    bq = F.read(dve, it, F_KV + 2 * m + 1)
                    if m >= 2:
                        dve.wait_ge(attn_ready, it * FB + m - 1)
                    dve.scalar_tensor_tensor(out=k_feat[:, s, :], in0=bkv[:, 0:S], scalar=bk_one[:, m:m + 1],
                                             in1=exp_part[:, s, 0, :], op0=ALU.add, op1=ALU.max,
                                             accum_out=k_sum[:, m:m + 1]).then_inc(k_ready, 1)
                    F.took(dve.scalar_tensor_tensor(out=q_feat[:, s, :], in0=bq[:, 0:S], scalar=bq_one[:, m:m + 1],
                                                    in1=exp_part[:, s, 1, :], op0=ALU.add, op1=ALU.max),
                           F_KV + 2 * m + 1)
                    dve.wait_ge(k_ready, it * E + m + 1)
                    F.took(dve.scalar_tensor_tensor(out=kv_junk[:, s, :], in0=bkv[:, S:2 * S],
                                                    scalar=w["bv3"][:, m:m + 1], in1=k_feat[:, s, :],
                                                    op0=ALU.add, op1=ALU.mult,
                                                    accum_out=kv_sum[:, m:m + 1]), F_KV + 2 * m)

                for m in range(E + 1):
                    if m < E:
                        gate(m, 0)
                        features(m)
                        gate(m, 1)
                    if m == 0:
                        dve.wait_ge(gate_exp, it + 1)
                        ch(router_mix(dve, ch, r, g.iota, NC, False, scale=0.5))
                    if m >= 1:
                        e = m - 1
                        dve.wait_ge(down_ready, it * E + e + 1)
                        dve.wait_ge(down_used, it * E + e + 1)
                        for c in range(NC):
                            last = dve.scalar_tensor_tensor(out=xt[:, c, :], in0=Db[:, c * P:(c + 1) * P],
                                                            scalar=r.comb[:, c, e:e + 1], in1=xt[:, c, :],
                                                            op0=ALU.mult, op1=ALU.add)
                        last.then_inc(down_used, 1)
                    if m < FB:
                        dve.wait_ge(den_ready, it * FB + m + 1)
                        dve.reciprocal(rden[:, m % 2, :], den[:, m % 2, :]).then_inc(rden_ready, 1)
                    if m == NEXT_STATS:
                        next_stats(it + 1)
                    if m == NEXT_STATS + 1:
                        next_norm(it + 1)
                next_rank(it + 1)
                dve.wait_ge(out_ready, it + 1)
                dve.tensor_tensor(y[:, :, :], chunks(Ob[:, 0:S]), over_chunks(w["bout3"][:, :]), ALU.add).then_inc(out_used, 1)
                dve.wait_ge(out_used, it + 2)
                ch(dve.tensor_tensor(ty[:, :, :], y[:, :, :], y[:, :, :], ALU.mult))
                ch(dve.tensor_scalar(ty[:, :, :], ty[:, :, :], 0.044715, 1.0, ALU.mult, ALU.add))
                dve.tensor_tensor(y2[:, :, :], ty[:, :, :], y[:, :, :], ALU.mult).then_inc(gelu_in, 1)
                dve.wait_ge(gelu_tanh, it + 1)
                ch(dve.scalar_tensor_tensor(out=y2[:, :, :], in0=ty[:, :, :], scalar=1.0, in1=y[:, :, :],
                                            op0=ALU.add, op1=ALU.mult))
                dve.wait_ge(down_used, it * E + E + 1)
                dve.scalar_tensor_tensor(out=g.x_all[:, bass.ds(it * NC, NC), :], in0=y2[:, :, :], scalar=0.5,
                                         in1=xt[:, :, :], op0=ALU.mult, op1=ALU.add).then_inc(x_done, 1)
                dve.wait_ge(x_done, it + 1)
                dve.memset(st.pad[:, :], 0.0)
                ch.done()


SHARED = ("ident", "one_row", "iota", "neg_half")


def load_lists(B):
    t = {
        "ident": (0, [P, P]), "one_row": (0, [P, 1]), "iota": (0, [P, E]), "neg_half": (0, [P, 32]),
        "alibi": (1, [P, NG, S]), "masks": (0, [P, 3, AW]),
        "before0": (0, [P, P]), "after0": (0, [P, P]), "eta0": (0, [P, 1]), "wv0": (0, [P, D]), "start0": (0, [P, D]),
        "lin0": (0, [P, D]), "bv0": (0, [P, D]), "blin0": (0, [P, D]), "gate0": (0, [P, E]),
        "left0": (0, [P, E * LR]), "right0": (0, [E * LR, D]),
        "q1": (1, [P, NG * P]), "k1": (1, [P, NG * P]), "v1": (1, [P, D]), "out1": (1, [P, D]),
        "bq1": (1, [P, NG]), "bk1": (1, [P, NG]), "bv1": (1, [P, D]), "bout1": (1, [P, D]),
        "gate1": (1, [P, E]), "up1": (1, [P, E * HID]), "down1": (1, [P, E * HC, D]),
        "bup1": (1, [P, E * HC]), "bdown1": (1, [E, D]),
        "q2": (2, [P, NG * P]), "k2": (2, [P, NG * P]), "v2w": (2, [P, D]), "f2": (2, [P, NH]), "bf2": (2, [P, NH]),
        "out2": (2, [P, WAYS, D]), "one_rows2": (2, [P, WAYS]),
        "tri2": (2, [P, P]), "tri_back2": (2, [P, P]), "ones2": (2, [P, P]),
        "rot2": (2, [P, 4, NC * LD]), "scale_rows2": (2, [P, DEPTH, 4, LD]),
        "qkv2": (2, [P, DEPTH, 3 * INNER]), "wo2": (2, [P, DEPTH, IB, D]), "ln2": (2, [P, DEPTH, 2]),
        "up2": (2, [P, DEPTH, 2, FC * P]), "bup2": (2, [P, DEPTH, 2, FC]), "down2": (2, [P, DEPTH, FC, D]),
        "bdown2": (2, [P, DEPTH, D]),
        "gate3": (3, [P, E]), "q3": (3, [P, FB * P]), "k3": (3, [P, FB * P]), "v3": (3, [P, FB * P]),
        "bq3": (3, [P, FB]), "bk3": (3, [P, FB]), "bv3": (3, [P, FB]), "out3": (3, [P, FB, D]), "bout3": (3, [P, D]),
        "egate3": (3, [P, E * HID]), "eup3": (3, [P, E * HID]), "edown3": (3, [P, E * HC, D]),
    }
    return t


def program(nc, dram, x_in, out, scratch, B):
    g = Names()
    lists = load_lists(B)
    held = {}

    def hold(ctx, layer, names=None):
        for n, (of, shape) in lists.items():
            if of == layer and n != "masks" and (names is None or n in names):
                held[n] = ctx.enter_context(nc.sbuf_tensor("w_" + n, shape, FP32))

    with ExitStack() as ctx:
        hold(ctx, 0, SHARED)
        hold(ctx, 3)
        only2 = ctx.enter_context(ExitStack())
        g.x_all = ctx.enter_context(nc.sbuf_tensor("x_all", [P, NC * B + RC, D], FP32))
        g.ident16 = ctx.enter_context(nc.sbuf_tensor("ident16", [P, P], BF16))
        masks16 = ctx.enter_context(nc.sbuf_tensor("masks16", [P, 3, AW], BF16))
        hold(only2, 2)
        only1 = only2.enter_context(ExitStack())
        hold(only1, 1)
        only0 = only1.enter_context(ExitStack())
        hold(only0, 0, [n for n in lists if n not in SHARED])
        g.w = held
        g.ident, g.one_row, g.iota, g.alibi = held["ident"], held["one_row"], held["iota"], held["alibi"]
        g.neg_half = held["neg_half"]
        g.mask_causal, g.mask_anti, g.mask_band = masks16[:, 0, :], masks16[:, 1, :], masks16[:, 2, :]
        g.bank = [ctx.enter_context(nc.psum_tensor(f"bank{i}", [P, 512], FP32)) for i in range(8)]
        loaded = [ctx.enter_context(nc.semaphore(f"loaded{i}")) for i in range(4)]
        x_loaded = ctx.enter_context(nc.semaphore("x_loaded"))
        consts_ready = ctx.enter_context(nc.semaphore("consts_ready"))
        n_loads = [0] * 4
        for n, (layer, _) in lists.items():
            n_loads[layer] += 16

        def wait_layer(eng, layer):
            eng.wait_ge(loaded[layer], n_loads[layer])

        def wait_consts(eng):
            eng.wait_ge(loaded[0], n_loads[0])
            eng.wait_ge(consts_ready, 1)

        g.wait_layer, g.wait_consts = wait_layer, wait_consts
        with ExitStack() as c0:
            masks32 = c0.enter_context(nc.sbuf_tensor("masks32", [P, 3, AW], FP32))
            block = c0.enter_context(nc.Block())

            def load(sp, layer):
                for n, (of, shape) in lists.items():
                    if of == layer:
                        dst = masks32 if n == "masks" else held[n]
                        sp.dma_start(dst.ap(), dram[n]).then_inc(loaded[layer], 16)

            def issue_loads(sp):
                for layer in (1, 2, 3):
                    if layer in PHASES:
                        load(sp, layer)

            g.issue_loads = issue_loads

            @block.sync
            def _(sp):
                load(sp, 0)
                if 0 in PHASES:
                    return
                issue_loads(sp)
                sp.dma_start(g.x_all[:, 0:NC * B, :], x_in.rearrange("b (c p) d -> p (b c) d", p=P)).then_inc(x_loaded, 16)

            @block.vector
            def _(dve):
                dve.wait_ge(loaded[0], n_loads[0])
                dve.tensor_copy(g.ident16[:, :], g.ident[:, :])
                dve.memset(g.x_all[:, NC * B:, :], 0.0)
                dve.tensor_copy(masks16[:, :, :], masks32[:, :, :]).then_inc(consts_ready, 1)
                if 0 not in PHASES:
                    dve.wait_ge(x_loaded, 16)

        if 0 in PHASES:
            layer0(nc, g, B, x_in, scratch)
            with ExitStack() as c0:
                block = c0.enter_context(nc.Block())

                @block.sync
                def _(sp):
                    sp.dma_start(g.x_all[:, 0:NC * B, :], scratch.rearrange("b (c p) d -> p (b c) d", p=P)).then_inc(x_loaded, 16)
                    sp.wait_ge(x_loaded, 16)
        only0.close()
        if 1 in PHASES:
            layer1(nc, g, B)
        only1.close()
        if 2 in PHASES:
            layer2(nc, g, B)
        only2.close()
        if 3 in PHASES:
            layer3(nc, g, B, out)
            return
        with ExitStack() as c0:
            stored = c0.enter_context(nc.semaphore("stored"))
            block = c0.enter_context(nc.Block())

            @block.sync
            def _(sp):
                sp.dma_start(out.rearrange("b (c p) d -> p (b c) d", p=P), g.x_all[:, 0:NC * B, :]).then_inc(stored, 16)
                sp.wait_ge(stored, 16)


def slot_columns(wt):
    out = np.zeros((wt.shape[0], NH, SLOT), wt.dtype)
    out[:, :, :DH] = wt.reshape(wt.shape[0], NH, DH)
    return out.reshape(wt.shape[0], NG * P)


def columns(v, n=P):
    return np.ascontiguousarray(v.reshape(-1, n).T)


def rows(v):
    return np.ascontiguousarray(np.broadcast_to(v, (P, v.shape[-1])))


def shape_constants():
    c = {}
    c["ident"] = np.eye(P, dtype=np.float32)
    p = np.arange(P)
    c["one_row"] = (p % SLOT == DH).astype(np.float32)[:, None]
    c["iota"] = np.broadcast_to(np.arange(E, dtype=np.float32), (P, E)).copy()
    c["neg_half"] = np.full((P, 32), -0.5, np.float32)
    early, late = (p % TS)[None, :] < (p % TS)[:, None], (p % TS)[None, :] > (p % TS)[:, None]
    c["before0"], c["after0"] = early.astype(np.float32), late.astype(np.float32)
    start = 2.0 ** (-2.0 ** (-(math.log2(NH) - 3)))
    slopes = np.array([start * start ** i for i in range(NH)], np.float32)
    al = np.zeros((NG, GH, SLOT, S), np.float32)
    al[:, :, DH, :] = slopes.reshape(NG, GH)[:, :, None] * np.arange(S, dtype=np.float32)
    c["alibi"] = al.reshape(NG, P, S).transpose(1, 0, 2).copy()
    q, k = np.arange(P)[:, None], np.arange(P)[None, :]
    c["one_rows2"] = np.stack([(p % SLOT == DH + y) for y in range(WAYS)], 1).astype(np.float32)
    c["tri2"] = (q <= k).astype(np.float32)
    c["tri_back2"] = (q >= k).astype(np.float32)
    c["ones2"] = np.ones((P, P), np.float32)
    half = np.arange(0, LD, 2, dtype=np.float64)
    t = np.arange(S, dtype=np.float64)
    inv = (1.0 / 10000.0 ** (half / LD)).astype(np.float32).astype(np.float64)
    angle = (t[:, None] * inv[None, :]).astype(np.float32).astype(np.float64)
    grow = ((half + 0.4 * LD) / (1.4 * LD))[None, :] ** ((t - S // 2) / float(WINDOW // 2))[:, None]
    cos, sin = (np.concatenate([y, y], 1) for y in (np.cos(angle), np.sin(angle)))
    grow = np.concatenate([grow, grow], 1)
    sign = np.where(np.arange(LD) < LHALF, -1.0, 1.0)[None, :]
    rot = np.stack([8 * cos * grow, 8 * sign * sin * grow, cos / grow, sign * sin / grow]).astype(np.float32)
    c["rot2"] = rot.reshape(4, NC, P, LD).transpose(2, 0, 1, 3).reshape(P, 4, NC * LD)
    no = np.float32(NEG)
    causal = np.where(k <= q, 0, no)
    anti = np.where(k >= q, 0, no)
    zero = np.zeros((P, P))
    full = np.full((P, P), no)
    far = np.where(q + P - k <= 64, 0, no)
    near = np.where((k <= q) & (q - k <= 64), 0, no)
    c["masks"] = np.stack([np.concatenate(x, 1) for x in
                           ((causal, zero, causal), (anti, zero, anti), (near, far, near))], 1).astype(np.float32)
    return c


def kernel(**a):
    import concourse.bacc as _bacc
    from concourse.bass_utils import run_bass_kernel_spmd as _run

    a = {n: np.asarray(v) for n, v in a.items()}
    x = np.ascontiguousarray(a["L0_attn_x"])
    B = x.shape[0]
    arrays = shape_constants()
    w_kv, b_kv = a["L0_attn_Wkv"], a["L0_attn_bkv"]
    arrays.update(
        eta0=rows(a["L0_attn_eta"].reshape(1)), wv0=w_kv[D:].T, start0=a["L0_attn_W0"].T, lin0=a["L0_ffn_W_lin"].T,
        bv0=rows(b_kv[D:]), blin0=rows(a["L0_ffn_b_lin"]), gate0=a["L0_ffn_gate_w"].T,
        left0=a["L0_ffn_left"].transpose(1, 0, 2).reshape(D, E * LR), right0=a["L0_ffn_right"].reshape(E * LR, D),
    )
    w_in, b_in = a["L1_attn_w_in"], a["L1_attn_b_in"]
    arrays.update(
        q1=slot_columns(w_in[:, :D]), k1=slot_columns(w_in[:, D:2 * D]), v1=w_in[:, 2 * D:], out1=a["L1_attn_w_out"],
        bq1=columns(slot_columns(b_in[None, :D])[0]), bk1=columns(slot_columns(b_in[None, D:2 * D])[0]),
        bv1=rows(b_in[2 * D:]), bout1=rows(a["L1_attn_b_out"]), gate1=a["L1_ffn_gate_w"].T,
        up1=a["L1_ffn_w1"].transpose(2, 0, 1).reshape(D, E * HID),
        down1=a["L1_ffn_w2"].transpose(0, 2, 1).reshape(E * HC, P, D).transpose(1, 0, 2),
        bup1=columns(a["L1_ffn_b1"].reshape(-1)), bdown1=a["L1_ffn_b2"],
    )
    qs, ks = a["L2_ffn_q_scale"], a["L2_ffn_k_scale"]

    def swapped(t):
        return np.concatenate([t[:, LHALF:], t[:, :LHALF]], 1)

    def ffn_blocks(t, axis):
        pad = [(0, 0)] * t.ndim
        pad[axis] = (0, FC * P - FFN)
        return np.pad(t, pad)

    w1, b1 = a["L2_ffn_w1"], a["L2_ffn_b1"]
    arrays.update(
        q2=slot_columns(a["L2_attn_Wq"].T), k2=slot_columns(a["L2_attn_Wk"].T), v2w=a["L2_attn_Wv"].T,
        f2=a["L2_attn_Wf"].T, bf2=rows(a["L2_attn_bf"]),
        out2=a["L2_attn_Wo"].T.reshape(WAYS, P, D).transpose(1, 0, 2),
        scale_rows2=rows(np.stack([qs, swapped(qs), ks, swapped(ks)], 1).reshape(-1)),
        qkv2=a["L2_ffn_wqkv"].transpose(1, 0, 2), wo2=a["L2_ffn_wo"].reshape(DEPTH, IB, P, D).transpose(2, 0, 1, 3),
        ln2=np.stack([a["L2_ffn_ln_g"], a["L2_ffn_ln_b"]], 1).transpose(2, 0, 1),
        up2=np.stack([ffn_blocks(w1[:, :, :FFN], 2), ffn_blocks(w1[:, :, FFN:], 2)], 1).transpose(2, 0, 1, 3),
        bup2=np.stack([ffn_blocks(b1[:, :FFN], 1), ffn_blocks(b1[:, FFN:], 1)], 1)
        .reshape(DEPTH, 2, FC, P).transpose(3, 0, 1, 2),
        down2=ffn_blocks(a["L2_ffn_w2"], 1).reshape(DEPTH, FC, P, D).transpose(2, 0, 1, 3),
        bdown2=rows(a["L2_ffn_b2"].reshape(-1)),
    )
    arrays.update(
        gate3=a["L3_ffn_router_w"].T,
        q3=a["L3_attn_wq"].reshape(D, FB * P), k3=a["L3_attn_wk"].reshape(D, FB * P),
        v3=a["L3_attn_wv"].reshape(D, FB * P),
        bq3=columns(a["L3_attn_bq"].reshape(-1)), bk3=columns(a["L3_attn_bk"].reshape(-1)),
        bv3=columns(a["L3_attn_bv"].reshape(-1)),
        out3=a["L3_attn_wo"].reshape(FB, P, D).transpose(1, 0, 2), bout3=rows(a["L3_attn_bo"]),
        egate3=a["L3_ffn_gate_w"].transpose(2, 0, 1).reshape(D, E * HID),
        eup3=a["L3_ffn_up_w"].transpose(2, 0, 1).reshape(D, E * HID),
        edown3=a["L3_ffn_down_w"].transpose(0, 2, 1).reshape(E * HC, P, D).transpose(1, 0, 2),
    )
    nc = _bacc.Bacc("TRN2", target_bir_lowering=False, num_devices=1)
    feed, dram = {}, {}

    def given(name, arr):
        arr = np.ascontiguousarray(arr)
        feed[f"in_{name}"] = arr
        return nc.dram_tensor(f"in_{name}", arr.shape, mybir.dt.from_np(arr.dtype), kind="ExternalInput").ap()

    for name, (_, shape) in load_lists(B).items():
        dram[name] = given(name, arrays[name].reshape(shape))
    x_in = given("x", x)
    scratch = nc.dram_tensor("scratch", x.shape, FP32, kind="Internal").ap()
    out = nc.dram_tensor("out_x", x.shape, FP32, kind="ExternalOutput").ap()
    program(nc, dram, x_in, out, scratch, B)
    res = _run(nc, [feed], core_ids=[0])
    return res.results[0]["out_x"]
```
